# Optimizing a Trainium2 kernel written in Bass

```python
import numpy as np
import jax
import jax.numpy as jnp

def _softmax(x, axis=-1):
    return jax.nn.softmax(x, axis=axis)

def _gelu(x):
    return jax.nn.gelu(x, approximate=True)

def _silu(x):
    return jax.nn.silu(x)

def _sigmoid(x):
    return jax.nn.sigmoid(x)

def _layernorm(x, axis=-1, eps=1e-05):
    m = jnp.mean(x, axis=axis, keepdims=True)
    v = jnp.var(x, axis=axis, keepdims=True)
    return (x - m) / jnp.sqrt(v + eps)

def _scatter_add(tgt, idx, src, axis=0):
    return tgt.at[idx].add(src)

def _segment_sum(src, seg, n):
    return jax.ops.segment_sum(src, seg, n)
kernel_name = 'mk_vit_tower_d2_tok_img512_r4_e273f9'

def setup_inputs(seed: int=0):
    np.random.seed(seed)
    _w = jnp.asarray

    def _rec_inputs():
        import jax
        import jax.numpy as jnp
        _rk = jax.random.key(seed)
        x = -0.000190493 + 0.999948 * jax.random.normal(jax.random.fold_in(_rk, 1), (128, 2, 104, 104), jnp.float32)
        return x
    x = _rec_inputs()

    def _L0_tok_setup():
        import jax, jax.numpy as jnp
        import numpy as np
        HP = 4
        PATCH = 8
        EPS = 1e-07

        def _shifts(x):
            h, w = (x.shape[2], x.shape[3])
            pad2 = ((0, 0), (0, 0))
            left_up = jnp.pad(x[:, :, HP:, :w - HP], pad2 + ((0, HP), (HP, 0)))
            right_up = jnp.pad(x[:, :, HP:, HP:], pad2 + ((0, HP), (0, HP)))
            left_down = jnp.pad(x[:, :, :h - HP, :w - HP], pad2 + ((HP, 0), (HP, 0)))
            right_down = jnp.pad(x[:, :, :h - HP, HP:], pad2 + ((HP, 0), (0, HP)))
            return (left_up, right_up, left_down, right_down)
        key = jax.random.key(seed)
        k1, k2, k3, k4 = jax.random.split(key, 4)
        B, C, S = (128, 2, 104)
        embed_dim = 128
        x = jax.random.normal(k1, (B, C, S, S), dtype=jnp.float32)
        gamma = 1.0 + 0.05 * jax.random.normal(k2, (10, S, S), dtype=jnp.float32)
        beta = 0.05 * jax.random.normal(k3, (10, S, S), dtype=jnp.float32)
        W = 0.02 * jax.random.normal(k4, (embed_dim, 10, PATCH, PATCH), dtype=jnp.float32)
        b = jnp.zeros((embed_dim,), dtype=jnp.float32)
        return {'x': x, 'gamma': gamma, 'beta': beta, 'W': W, 'b': b}
    _L0_tok_all = _L0_tok_setup()
    _L0_tok_in = {k: v for k, v in _L0_tok_all.items() if k in ('gamma', 'beta', 'W', 'b')}
    del _L0_tok_all

    def _L0_attn_setup():
        import jax, jax.numpy as jnp
        import numpy as np
        EMBED_DIM = 128
        NUM_NEURONS = 256
        key = jax.random.key(seed)
        k_x, k_pos, k_val, k_w, k_b = jax.random.split(key, 5)
        B, T, D, N = (8, 512, EMBED_DIM, NUM_NEURONS)
        x = jax.random.normal(k_x, (B, T, D), dtype=jnp.float32)
        positions = jax.random.normal(k_pos, (N, D), dtype=jnp.float32) * 0.02
        scales = jnp.ones((N,), dtype=jnp.float32) * 5.0
        values = jax.random.normal(k_val, (N, D), dtype=jnp.float32) * 0.02
        lim = 1.0 / np.sqrt(D)
        W_out = jax.random.uniform(k_w, (D, D), minval=-lim, maxval=lim, dtype=jnp.float32)
        b_out = jax.random.uniform(k_b, (D,), minval=-lim, maxval=lim, dtype=jnp.float32)
        return {'x': x, 'positions': positions, 'scales': scales, 'values': values, 'W_out': W_out, 'b_out': b_out}
    _L0_attn_all = _L0_attn_setup()
    _L0_attn_in = {k: v for k, v in _L0_attn_all.items() if k in ('positions', 'scales', 'values', 'W_out', 'b_out')}
    del _L0_attn_all

    def _L0_ffn_setup():
        import jax, jax.numpy as jnp
        import numpy as np
        FP8_MAX = 448.0
        K, N = (128, 128)
        key = jax.random.key(seed)
        kx, kw = jax.random.split(key)
        x = jax.random.normal(kx, (8, 2048, K), dtype=jnp.float32)
        weight = jax.random.normal(kw, (K, N), dtype=jnp.float32) * 0.02
        return {'x': x, 'weight': weight}
    _L0_ffn_all = _L0_ffn_setup()
    _L0_ffn_in = {k: v for k, v in _L0_ffn_all.items() if k in ('weight',)}
    del _L0_ffn_all

    def _L1_attn_setup():
        import jax, jax.numpy as jnp
        import numpy as np
        SCALE = 1.0 / np.sqrt(512.0).astype(np.float32)
        key = jax.random.key(seed)
        inputs = jax.random.normal(key, (4, 1024, 128), dtype=jnp.float32)
        return {'inputs': inputs}
    _L1_attn_all = _L1_attn_setup()
    _L1_attn_in = {k: v for k, v in _L1_attn_all.items() if k in ()}
    del _L1_attn_all

    def _L1_ffn_setup():
        import jax, jax.numpy as jnp
        import numpy as np
        TOP_K = 6
        CAP_FACTOR = 2.0
        key = jax.random.key(seed)
        ks = jax.random.split(key, 9)
        B, S, D, F, E, SH = (4, 512, 128, 64, 64, 2)
        return {'x': jax.random.normal(ks[0], (B, S, D), jnp.float32), 'router_w': jax.random.normal(ks[1], (E, D), jnp.float32) * 0.02, 'bias': jnp.zeros((E,), jnp.float32), 'shared_w_gate': jax.random.normal(ks[2], (SH, F, D), jnp.float32) * 0.02, 'shared_w_up': jax.random.normal(ks[3], (SH, F, D), jnp.float32) * 0.02, 'shared_w_down': jax.random.normal(ks[4], (SH, D, F), jnp.float32) * 0.02, 'w_gate': jax.random.normal(ks[5], (E, F, D), jnp.float32) * 0.02, 'w_up': jax.random.normal(ks[6], (E, F, D), jnp.float32) * 0.02, 'w_down': jax.random.normal(ks[7], (E, D, F), jnp.float32) * 0.02}
    _L1_ffn_all = _L1_ffn_setup()
    _L1_ffn_in = {k: v for k, v in _L1_ffn_all.items() if k in ('router_w', 'bias', 'shared_w_gate', 'shared_w_up', 'shared_w_down', 'w_gate', 'w_up', 'w_down')}
    del _L1_ffn_all
    return {'x': x, 'L0_tok_gamma': _L0_tok_in['gamma'], 'L0_tok_beta': _L0_tok_in['beta'], 'L0_tok_W': _L0_tok_in['W'], 'L0_tok_b': _L0_tok_in['b'], 'L0_attn_positions': _L0_attn_in['positions'], 'L0_attn_scales': _L0_attn_in['scales'], 'L0_attn_values': _L0_attn_in['values'], 'L0_attn_W_out': _L0_attn_in['W_out'], 'L0_attn_b_out': _L0_attn_in['b_out'], 'L0_ffn_weight': _L0_ffn_in['weight'], 'L1_ffn_router_w': _L1_ffn_in['router_w'], 'L1_ffn_bias': _L1_ffn_in['bias'], 'L1_ffn_shared_w_gate': _L1_ffn_in['shared_w_gate'], 'L1_ffn_shared_w_up': _L1_ffn_in['shared_w_up'], 'L1_ffn_shared_w_down': _L1_ffn_in['shared_w_down'], 'L1_ffn_w_gate': _L1_ffn_in['w_gate'], 'L1_ffn_w_up': _L1_ffn_in['w_up'], 'L1_ffn_w_down': _L1_ffn_in['w_down']}

def reference(x, L0_tok_gamma, L0_tok_beta, L0_tok_W, L0_tok_b, L0_attn_positions, L0_attn_scales, L0_attn_values, L0_attn_W_out, L0_attn_b_out, L0_ffn_weight, L1_ffn_router_w, L1_ffn_bias, L1_ffn_shared_w_gate, L1_ffn_shared_w_up, L1_ffn_shared_w_down, L1_ffn_w_gate, L1_ffn_w_up, L1_ffn_w_down):
    import jax
    import jax.numpy as jnp

    def _L0_tok_ref(x, gamma, beta, W, b):
        import jax, jax.numpy as jnp
        import numpy as np
        HP = 4
        PATCH = 8
        EPS = 1e-07

        def _shifts(x):
            h, w = (x.shape[2], x.shape[3])
            pad2 = ((0, 0), (0, 0))
            left_up = jnp.pad(x[:, :, HP:, :w - HP], pad2 + ((0, HP), (HP, 0)))
            right_up = jnp.pad(x[:, :, HP:, HP:], pad2 + ((0, HP), (0, HP)))
            left_down = jnp.pad(x[:, :, :h - HP, :w - HP], pad2 + ((HP, 0), (HP, 0)))
            right_down = jnp.pad(x[:, :, :h - HP, HP:], pad2 + ((HP, 0), (0, HP)))
            return (left_up, right_up, left_down, right_down)
        lu, ru, ld, rd = _shifts(x)
        concat = jnp.concatenate((x, lu, ru, ld, rd), axis=1)
        mean = jnp.mean(concat, axis=(1, 2, 3), keepdims=True)
        var = jnp.var(concat, axis=(1, 2, 3), keepdims=True)
        normed = (concat - mean) * jax.lax.rsqrt(var + EPS)
        normed = normed * gamma[None] + beta[None]
        y = jax.lax.conv_general_dilated(normed, W, window_strides=(PATCH, PATCH), padding='VALID', dimension_numbers=('NCHW', 'OIHW', 'NCHW'))
        y = y + b[None, :, None, None]
        B, E = (y.shape[0], y.shape[1])
        y = y.reshape(B, E, -1).transpose(0, 2, 1)
        return y

    def _L0_attn_ref(x, positions, scales, values, W_out, b_out):
        import jax, jax.numpy as jnp
        import numpy as np
        EMBED_DIM = 128
        NUM_NEURONS = 256
        x_sq = jnp.sum(x * x, axis=-1, keepdims=True)
        p_sq = jnp.sum(positions * positions, axis=-1)
        cross = jnp.einsum('btd,nd->btn', x, positions)
        dist_sq = jnp.maximum(x_sq + p_sq[None, None, :] - 2.0 * cross, 0.0)
        dist = jnp.sqrt(dist_sq)
        attn = jax.nn.softmax(scales[None, None, :] / (dist + 0.1), axis=-1)
        out = jnp.einsum('btn,nd->btd', attn, values)
        return out @ W_out.T + b_out

    def _L0_ffn_ref(x, weight):
        import jax, jax.numpy as jnp
        import numpy as np
        FP8_MAX = 448.0
        K, N = (128, 128)
        B, S, _ = x.shape
        x2d = x.reshape(-1, K)
        x_amax = jnp.max(jnp.abs(x2d))
        x_scale = FP8_MAX / jnp.maximum(x_amax, 1e-12)
        x_fp8 = jnp.clip(x2d * x_scale, -FP8_MAX, FP8_MAX).astype(jnp.float8_e4m3fn)
        w_amax = jnp.max(jnp.abs(weight))
        w_scale = FP8_MAX / jnp.maximum(w_amax, 1e-12)
        w_fp8 = jnp.clip(weight.T * w_scale, -FP8_MAX, FP8_MAX).astype(jnp.float8_e4m3fn)
        res = jnp.matmul(x_fp8.astype(jnp.float32), w_fp8.astype(jnp.float32).T)
        out = res * (1.0 / x_scale * (1.0 / w_scale))
        return out.reshape(B, S, N).astype(x.dtype)

    def _L1_attn_ref(inputs):
        import jax, jax.numpy as jnp
        import numpy as np
        SCALE = 1.0 / np.sqrt(512.0).astype(np.float32)
        scores = jax.nn.softmax(jnp.einsum('bnd,bmd->bnm', inputs, inputs) * SCALE, axis=-1)
        return jnp.einsum('bnm,bmd->bnd', scores, inputs)

    def _L1_ffn_ref(x, router_w, bias, shared_w_gate, shared_w_up, shared_w_down, w_gate, w_up, w_down):
        import jax, jax.numpy as jnp
        import numpy as np
        TOP_K = 6
        CAP_FACTOR = 2.0
        B, S, D = x.shape
        E = router_w.shape[0]
        K = TOP_K
        N = B * S
        C = max(1, int(N * K * CAP_FACTOR / E))
        router_logits = jnp.einsum('bsd,ed->bse', x, router_w) + bias
        hg = jnp.einsum('bsd,efd->bsef', x, shared_w_gate)
        hu = jnp.einsum('bsd,efd->bsef', x, shared_w_up)
        shared_out = jnp.einsum('bsef,edf->bsd', jax.nn.silu(hg) * hu, shared_w_down)
        shared_out = shared_out / shared_w_gate.shape[0]
        router_probs = jax.nn.softmax(router_logits, axis=-1)
        topk_p, topk_i = jax.lax.top_k(router_probs, K)
        topk_p = topk_p / (jnp.sum(topk_p, axis=-1, keepdims=True) + 1e-09)
        x_flat = x.reshape(N, D)
        flat_e = topk_i.reshape(-1)
        flat_g = topk_p.reshape(-1)
        token_ids = jnp.repeat(jnp.arange(N), K)
        order = jnp.argsort(flat_e)
        se = flat_e[order]
        st = token_ids[order]
        sg = flat_g[order]
        M = se.shape[0]
        pos = jnp.arange(M)
        is_first = jnp.concatenate([jnp.ones((1,), bool), se[1:] != se[:-1]])
        group_starts = jax.lax.cummax(pos * is_first.astype(pos.dtype))
        slot = pos - group_starts
        valid = slot < C
        safe_slot = jnp.where(valid, slot, C)
        expert_in = jnp.zeros((E, C + 1, D), x.dtype).at[se, safe_slot].set(x_flat[st])
        expert_gate = jnp.zeros((E, C + 1), x.dtype).at[se, safe_slot].set(sg)
        expert_tok = jnp.full((E, C + 1), N, jnp.int32).at[se, safe_slot].set(st.astype(jnp.int32))
        expert_mask = jnp.zeros((E, C + 1), bool).at[se, safe_slot].set(valid)
        expert_in = expert_in[:, :C]
        expert_gate = expert_gate[:, :C]
        expert_tok = expert_tok[:, :C]
        expert_mask = expert_mask[:, :C]
        hg = jnp.einsum('ecd,efd->ecf', expert_in, w_gate)
        hu = jnp.einsum('ecd,efd->ecf', expert_in, w_up)
        expert_out = jnp.einsum('ecf,edf->ecd', jax.nn.silu(hg) * hu, w_down)
        fm = expert_mask.reshape(-1)
        dst = jnp.where(fm, expert_tok.reshape(-1), N)
        fg = jnp.where(fm, expert_gate.reshape(-1), jnp.zeros((), x.dtype))
        sparse = jax.ops.segment_sum(fg[:, None] * expert_out.reshape(-1, D), dst, num_segments=N + 1)[:N]
        return shared_out + sparse.reshape(B, S, D)
    h = _L0_tok_ref(x, L0_tok_gamma, L0_tok_beta, L0_tok_W, L0_tok_b)
    h = h + _L0_attn_ref(_layernorm(h, axis=-1), L0_attn_positions, L0_attn_scales, L0_attn_values, L0_attn_W_out, L0_attn_b_out)
    h = h + _L0_ffn_ref(_layernorm(h, axis=-1), L0_ffn_weight)
    h = h + _L1_attn_ref(_layernorm(h, axis=-1))
    h = h + _L1_ffn_ref(_layernorm(h, axis=-1), L1_ffn_router_w, L1_ffn_bias, L1_ffn_shared_w_gate, L1_ffn_shared_w_up, L1_ffn_shared_w_down, L1_ffn_w_gate, L1_ffn_w_up, L1_ffn_w_down)
    return h

_drawn_inputs = setup_inputs


def setup_inputs(seed=0):
    import zlib

    import numpy as np

    out = dict(_drawn_inputs(seed))
    spreads = {'L0_tok_b': (0.0, 0.1), 'L0_attn_scales': (5.0, 0.6), 'L1_ffn_bias': (0.0, 0.8)}
    factors = {'L0_attn_positions': 28.578,
     'L0_attn_values': 8.0,
     'L0_attn_W_out': 8.0,
     'L1_ffn_router_w': 8.0,
     'L1_ffn_shared_w_gate': 8.0,
     'L1_ffn_shared_w_up': 8.0,
     'L1_ffn_shared_w_down': 8.0,
     'L1_ffn_w_gate': 8.0,
     'L1_ffn_w_up': 8.0,
     'L1_ffn_w_down': 8.0}
    for name, (base, spread) in spreads.items():
        noise = np.random.default_rng([zlib.crc32(name.encode()), seed]).standard_normal(out[name].shape)
        drawn = base * np.exp(spread * noise) if base else spread * noise
        out[name] = jnp.asarray(drawn.astype(out[name].dtype))
    for name, factor in factors.items():
        out[name] = (out[name] * factor).astype(out[name].dtype)
    return out
```

```python
from contextlib import ExitStack

import concourse.bass as bass
from concourse import mybir

ALU = mybir.AluOpType
ACT = mybir.ActivationFunctionType
AX = mybir.AxisListType
F32 = mybir.dt.float32
BF16 = mybir.dt.bfloat16
I32 = mybir.dt.int32
RMAX = bass.bass_isa.ReduceOp.max

B, CH, S, PATCH, HP = 128, 2, 104, 8, 4
NI = S // PATCH
T = NI * NI
D = 128
NCTX = 5
K = CH * PATCH * PATCH
N = B * T
TG = 4
GA = -(-T // TG)
NN = 256
LN_EPS, TOK_EPS = 1e-5, 1e-7
FP8_MAX = 448.0
NPIX = float(2 * NCTX * S * S)
NPAD = NPIX - 2.0 * (S * S + 4 * (S - HP) ** 2)
ROUND = 1.5 * 2.0 ** 20
MINEXP = 2.0 ** -6
SCALE = 1.0 / 512.0 ** 0.5
NE, F, TOPK = 64, 64, 6
CAP = int(N * TOPK * 2.0 / NE)
NGRP = 1
CR = -(-CAP // 128) * 128 + 256 * NGRP
ZR = NE * CR
XW = D + 2
BIG = 1e30
HALF = (128, T - 128)


def group_steps():
    cut = [GA * i // NGRP for i in range(NGRP + 1)]
    return list(zip(cut[:-1], cut[1:]))


def group_tiles(a, b):
    tiles = min(b * TG, T) - a * TG
    return -(-(tiles * TOPK + NE) // TG) * TG


NT = max(group_tiles(a, b) for a, b in group_steps())
YZ = 128 * NT


def after(eng, sem, value):
    if not isinstance(value, int) or value > 0:
        eng.wait_ge(sem, value)


def pipeline(eng, first, stop, parts, slots=2):
    longest = max(lag for lag, _ in parts)
    start = first + longest + slots
    start += -start % slots
    end = stop - 1 - (stop - 1) % slots

    def plain(s):
        for lag, fn in parts:
            if first <= s - lag < stop:
                fn(s - lag, (s - lag) % slots, (s - lag) // slots)

    if end - start < 2 * slots:
        start = end = stop
    for s in range(first, start):
        plain(s)
    if end > start:
        with eng.Fori(start // slots, end // slots) as i:
            for u in range(slots):
                for lag, fn in parts:
                    fn(slots * i + (u - lag), (u - lag) % slots, i + (u - lag) // slots)
    for s in range(end, stop + longest):
        plain(s)


def tiles_of(g, total=T):
    return min(TG, total - TG * g) if isinstance(g, int) else TG


def build(nc, io):
    def dram(name, shape):
        return nc.dram_tensor(name, shape, F32, kind="Internal").ap()

    h1d = dram("h1d", (B, T, D))
    h3d = dram("h3d", (N, D))
    h4d = dram("h4d", (N, D))
    gbd = dram("gbd", (2, T * D))
    xed = dram("xed", (ZR + 128, XW))
    yed = dram("yed", (YZ + 128, D))
    destd = dram("destd", (T, 128, NE))
    out = io["out"].rearrange("b t d -> (b t) d")

    with ExitStack() as ctx:
        def sb(name, shape, dt=F32, c=ctx):
            return c.enter_context(nc.sbuf_tensor(name, shape, dt))

        def sem(name):
            return ctx.enter_context(nc.semaphore(name))

        bank = [ctx.enter_context(nc.psum_tensor(f"bank{i}", [128, 512], F32)) for i in range(4)]
        wide = [ctx.enter_context(nc.psum_tensor(f"wide{i}", [128, 1024], F32)) for i in range(2)]

        ident = sb("ident", [128, 128])
        identb = sb("identb", [128, 128], BF16)
        ones = sb("ones", [128, 128])
        onesb = sb("onesb", [128, 128], BF16)
        before = sb("before", [128, 128])
        beforeb = sb("beforeb", [128, 128], BF16)
        eps_ln = sb("eps_ln", [128, 1])
        tenth = sb("tenth", [128, 1])
        wq = sb("wq", [128, 128], BF16)
        fscale = sb("fscale", [128, 4])

        front(nc, io, sb, bank, wide, dict(
            ident=ident, identb=identb, ones=ones, onesb=onesb, before=before, beforeb=beforeb,
            eps_ln=eps_ln, tenth=tenth, wq=wq, fscale=fscale), h1d, gbd)
        back(nc, io, sb, sem, bank, wide, dict(
            ident=ident, identb=identb, ones=ones, onesb=onesb, before=before, beforeb=beforeb,
            wq=wq, fscale=fscale), h1d, h3d, h4d, xed, yed, destd, out)


def front(nc, io, sb0, bank, wide, c, h1d, gbd):
    used = []

    def sem(name):
        used.append(nc.alloc_semaphore(name=name))
        return used[-1]

    with ExitStack() as ctx:
        def sb(name, shape, dt=F32):
            return sb0(name, shape, dt, ctx)

        ident, ones, onesb = c["ident"], c["ones"], c["onesb"]
        H = sb("H", [128, T * D])
        img = H[:, 0:CH * S * S].rearrange("p (c r w) -> p c r w", c=CH, r=S)
        tok = H[:, :].rearrange("p (t d) -> p t d", d=D)
        w5 = sb("w5", [128, NCTX, D])
        gam = sb("gam", [128, T, NCTX])
        bet = sb("bet", [128, T, NCTX])
        tokb = sb("tokb", [1, D])
        post = sb("post", [128, NN])
        possq = sb("possq", [128, NN])
        psqr = sb("psqr", [1, NN])
        psq_parts = sb("psq_parts", [1, 3, NN], BF16)
        psq3 = sb("psq3", [3, NN], BF16)
        valt = sb("valt", [128, NN])
        wot = sb("wot", [128, D])
        bout = sb("bout", [1, D])
        v2 = sb("v2", [128, 2, D])
        scb = sb("scb", [128, NN])
        wffn = sb("wffn", [128, D])
        part = sb("part", [128, 64])
        mstd = sb("mstd", [128, 2])
        rstd = sb("rstd", [128, 1])
        mstdT = sb("mstdT", [2, 128])
        eps_tok = sb("eps_tok", [128, 1])
        gbs = sb("gbs", [128, 4, D])

        xs = sb("xs", [128, 2, TG, NCTX, 128])
        weff = sb("weff", [128, 2, TG, NCTX, 128])
        gbx = sb("gbx", [2, 2, TG * D])
        bst = sb("bst", [128, TG, 6])
        mv = sb("mv", [128, 2, TG, 2])
        std = sb("std", [128, 2, TG])
        rs0 = sb("rs0", [128, 2, TG])
        vr = sb("vr", [128, TG])
        xsq = sb("xsq", [128, 2, TG])
        xh = sb("xh", [128, 2, TG, D])
        xT = sb("xT", [128, TG, D])
        d2 = sb("d2", [128, TG, NN])
        lnr = sb("lnr", [128, TG, NN])
        rr = sb("rr", [128, TG, NN])
        lg = sb("lg", [128, 2, TG, NN])
        mn = sb("mn", [128, 2, TG])
        zz = sb("zz", [128, 2, TG])
        rz = sb("rz", [128, TG])
        eT = sb("eT", [128, TG * 2, 128])
        bst1 = sb("bst1", [128, TG, 6])
        mvs = sb("mvs", [128, TG, 2])
        mv1 = sb("mv1", [128, T, 2])
        hmax = sb("hmax", [128, T])
        hmin = sb("hmin", [128, T])
        hstd = sb("hstd", [128, T])
        am = sb("am", [128, 8])
        am2 = sb("am2", [128, 2])
        qtmp = sb("qtmp", [128, D])
        qm = sb("qm", [128, D])

        s_img = [sem(f"s_img{i}") for i in range(4)]
        s_w = sem("s_w")
        s_const = sem("s_const")
        s_fix = sem("s_fix")
        s_vc = sem("s_vc")
        s_sq = sem("s_sq")
        s_var = sem("s_var")
        s_mstd = sem("s_mstd")
        s_mT = sem("s_mT")
        s_gb = sem("s_gb")
        s_gbs = sem("s_gbs")
        s_gbo = sem("s_gbo")
        s_psq = sem("s_psq")
        s_psp = sem("s_psp")
        s_ps3 = sem("s_ps3")
        s_v2 = sem("s_v2")

        with nc.Block() as block:
            @block.sync
            def _(sp):
                for i in range(4):
                    w = CH * S * S // 4
                    sp.dma_start(H[:, i * w:(i + 1) * w], io["ximg"][:, i * w:(i + 1) * w]).then_inc(s_img[i], 16)
                for dst, src in ((w5, "w5"), (gam, "gam"), (bet, "bet")):
                    sp.dma_start(dst[:, :, :], io[src]).then_inc(s_w, 16)
                for dst, src in ((tokb, "tokb"), (post, "post"), (valt, "valt"), (wot, "wot"),
                                 (bout, "bout"), (wffn, "wffn")):
                    sp.dma_start(dst[:, :], io[src]).then_inc(s_w, 16)
                sp.dma_start(scb[:, :], io["scales"].partition_broadcast(128)).then_inc(s_w, 16)
                sp.wait_ge(s_gbs, 1)
                for q in range(2):
                    sp.dma_start(gbd[q, 0:128 * D].rearrange("(p d) -> p d", d=D), gbs[:, q, :]).then_inc(s_gbo, 16)
                    sp.dma_start(gbd[q, 128 * D:T * D].rearrange("(p d) -> p d", d=D),
                                 gbs[0:T - 128, 2 + q, :]).then_inc(s_gbo, 16)
                sp.wait_ge(s_psp, 3)
                for k in range(3):
                    sp.dma_start(psq3[k:k + 1, :], psq_parts[:, k, :]).then_inc(s_ps3, 16)
                sp.wait_ge(s_gbo, 64)
                sp.wait_ge(s_ps3, 48)

            @block.gpsimd
            def _(g):
                g.memset(c["ident"][:, :], 0.0).then_inc(s_const, 1)
                g.memset(c["before"][:, :], 0.0).then_inc(s_const, 1)
                g.memset(c["ones"][:, :], 1.0).then_inc(s_const, 1)
                g.memset(c["onesb"][:, :], 1.0).then_inc(s_const, 1)
                g.memset(c["eps_ln"][:, :], LN_EPS).then_inc(s_const, 1)
                g.memset(c["tenth"][:, :], 0.1).then_inc(s_const, 1)
                g.memset(eps_tok[:, :], TOK_EPS).then_inc(s_const, 1)
                g.wait_ge(s_const, 7)
                g.affine_select(out=ident[:, :], in_=ident[:, :], compare_op=ALU.not_equal, fill=1.0, base=0,
                                pattern=[[-1, 128]], channel_multiplier=1).then_inc(s_fix, 1)
                g.affine_select(out=c["before"][:, :], in_=c["before"][:, :], compare_op=ALU.is_ge, fill=1.0,
                                base=0, pattern=[[-1, 128]], channel_multiplier=1).then_inc(s_fix, 1)
                g.wait_ge(s_fix, 2)
                g.tensor_copy(c["identb"][:, :], ident[:, :]).then_inc(s_fix, 1)
                g.tensor_copy(c["beforeb"][:, :], c["before"][:, :]).then_inc(s_fix, 1)
                g.wait_ge(s_fix, 4)

            def edges(v, sign, dst, link):
                at = dst
                for w0 in (0, S - HP):
                    link(v.tensor_reduce(part[:, at:at + 1], img[:, :, :, w0:w0 + HP], AX.XYZ, ALU.add))
                    at += 1
                for r0 in (0, S - HP):
                    link(v.tensor_reduce(part[:, at:at + 1], img[:, :, r0:r0 + HP, :], AX.XYZ, ALU.add))
                    at += 1
                for w0 in (0, S - HP):
                    for r0 in (0, S - HP):
                        link(v.tensor_reduce(part[:, at:at + 1], img[:, :, r0:r0 + HP, w0:w0 + HP], AX.XYZ, ALU.add))
                        at += 1

            def weigh(v, link, base, dst):
                link(v.tensor_reduce(part[:, 30:31], part[:, base:base + 4], AX.X, ALU.add))
                link(v.tensor_reduce(part[:, 31:32], part[:, base + 4:base + 8], AX.X, ALU.add))
                link(v.tensor_reduce(part[:, 32:33], part[:, base + 8:base + 12], AX.X, ALU.add))
                link(v.scalar_tensor_tensor(part[:, 33:34], part[:, 30:31], 5.0, part[:, 32:33], ALU.mult, ALU.add))
                link(v.scalar_tensor_tensor(dst, part[:, 31:32], -2.0, part[:, 33:34], ALU.mult, ALU.add))

            @block.vector
            def _(v):
                count = [0]

                def link(ins):
                    count[0] += 1
                    ins.then_inc(s_vc, 1)
                    v.wait_ge(s_vc, count[0])

                w = CH * S * S // 4
                for i in range(4):
                    v.wait_ge(s_img[i], 16)
                    link(v.tensor_reduce(part[:, i:i + 1], H[:, i * w:(i + 1) * w], AX.X, ALU.add))
                edges(v, 1, 4, link)
                weigh(v, link, 0, part[:, 40:41])
                v.tensor_scalar(mstd[:, 0:1], part[:, 40:41], -1.0 / NPIX, None, ALU.mult).then_inc(s_mstd, 1)
                v.wait_ge(s_sq, 4)
                edges(v, 1, 20, link)
                for i in range(4):
                    link(v.tensor_copy(part[:, 16 + i:17 + i], part[:, 50 + i:51 + i]))
                weigh(v, link, 16, part[:, 41:42])
                v.wait_ge(s_mstd, 1)
                link(v.tensor_tensor(part[:, 42:43], mstd[:, 0:1], mstd[:, 0:1], ALU.mult))
                link(v.scalar_tensor_tensor(part[:, 43:44], part[:, 42:43], NPAD, part[:, 41:42], ALU.mult, ALU.add))
                v.tensor_scalar(part[:, 44:45], part[:, 43:44], 1.0 / NPIX, None, ALU.mult).then_inc(s_var, 1)
                v.wait_ge(s_mstd, 2)
                v.reciprocal(rstd[:, :], mstd[:, 1:2]).then_inc(s_mstd, 1)
                v.wait_ge(s_mT, 1)
                v.tensor_copy(mstdT[:, :], bank[2][0:2, 0:128]).then_inc(s_mT, 1)
                v.wait_ge(s_w, 160)
                v.tensor_tensor(possq[:, :], post[:, :], post[:, :], ALU.mult).then_inc(s_psq, 1)
                v.wait_ge(s_psq, 1)
                v.tensor_scalar(post[:, :], post[:, :], -2.0, None, ALU.mult).then_inc(s_psq, 1)
                v.wait_ge(s_psq, 3)
                for k in range(3):
                    src = bank[3][0:1, 0:NN] if k == 0 else psqr[:, :]
                    v.tensor_copy(psq_parts[:, k, :], src).then_inc(s_psp, 1)
                    v.wait_ge(s_psp, k + 1)
                    if k < 2:
                        link(v.tensor_tensor(psqr[:, :], src, psq_parts[:, k, :], ALU.subtract))
                v.wait_ge(s_v2, 1)
                v.tensor_copy(v2[:, :, :].rearrange("p a d -> p (a d)"), bank[1][:, 0:2 * D]).then_inc(s_v2, 1)
                v.wait_ge(s_gb, 1)
                v.tensor_copy(gbs[:, 0:2, :].rearrange("p a d -> p (a d)"), bank[0][:, 0:2 * D]).then_inc(s_gb, 1)
                v.tensor_copy(gbs[0:T - 128, 2:4, :].rearrange("p a d -> p (a d)"),
                              bank[0][0:T - 128, 2 * D:4 * D]).then_inc(s_gbs, 1)
                v.wait_ge(s_gb, 2)

            @block.scalar
            def _(a):
                w = CH * S * S // 4
                a.wait_ge(s_mstd, 1)
                for i in range(4):
                    a.activation(H[:, i * w:(i + 1) * w], H[:, i * w:(i + 1) * w], ACT.Square, bias=mstd[:, 0:1],
                                 accum_out=part[:, 50 + i:51 + i]).then_inc(s_sq, 1)
                a.wait_ge(s_const, 7)
                a.wait_ge(s_var, 1)
                a.activation(mstd[:, 1:2], part[:, 44:45], ACT.Sqrt, bias=eps_tok[:, :]).then_inc(s_mstd, 1)

            @block.tensor
            def _(pe):
                pe.wait_ge(s_w, 160)
                pe.wait_ge(s_const, 7)
                pe.wait_ge(s_fix, 4)
                for half, (p0, n) in enumerate(((0, 128), (128, T - 128))):
                    for q, src in enumerate((gam, bet)):
                        dst = bank[0][0:n, (2 * half + q) * D:(2 * half + q + 1) * D]
                        for k in range(NCTX):
                            last = pe.matmul(dst, src[:, p0:p0 + n, k], w5[:, k, :], start=(k == 0),
                                             stop=(k == NCTX - 1 and q == 0))
                        if q == 1:
                            last = pe.matmul(dst, ones[0:1, 0:n], tokb[:, :], start=False, stop=True)
                last.then_inc(s_gb, 1)
                for a in range(2):
                    dst = bank[1][:, a * D:(a + 1) * D]
                    pe.matmul(dst, valt[:, a * 128:(a + 1) * 128], wot[:, :], start=True, stop=False)
                    last = pe.matmul(dst, ones[0:1, :], bout[:, :], start=False, stop=True)
                last.then_inc(s_v2, 1)
                pe.wait_ge(s_mstd, 2)
                pe.transpose(bank[2][0:2, 0:128], mstd[:, :], ident[:, :]).then_inc(s_mT, 1)
                pe.wait_ge(s_psq, 2)
                pe.matmul(bank[3][0:1, 0:NN], ones[:, 0:1], possq[:, :], start=True, stop=True).then_inc(s_psq, 1)

        xs_in = [sem(f"xs_in{i}") for i in range(2)]
        h1_out = [sem(f"h1_out{i}") for i in range(2)]
        weff_ready = sem("weff_ready")
        conv_done = sem("conv_done")
        h0_ready = sem("h0_ready")
        bn0 = sem("bn0")
        mv0 = sem("mv0")
        std0 = sem("std0")
        rs0_ready = sem("rs0_ready")
        vr_ready = sem("vr_ready")
        xsq_ready = sem("xsq_ready")
        xh_ready = sem("xh_ready")
        xt_done = sem("xt_done")
        xT_ready = sem("xT_ready")
        cross_done = sem("cross_done")
        d2_ready = sem("d2_ready")
        dist_ready = sem("dist_ready")
        ln_ready = sem("ln_ready")
        r_ready = sem("r_ready")
        t_ready = sem("t_ready")
        rs_ready = sem("rs_ready")
        lg_ready = sem("lg_ready")
        mn_ready = sem("mn_ready")
        ex_ready = sem("ex_ready")
        et_done = sem("et_done")
        eT_low = sem("eT_low")
        eT_high = sem("eT_high")
        out_done = sem("out_done")
        rz_ready = sem("rz_ready")
        h1_ready = sem("h1_ready")
        bn1 = sem("bn1")
        mvs_ready = sem("mvs_ready")
        mv1_ready = sem("mv1_ready")
        s_end = sem("s_end")
        s_std1 = sem("s_std1")
        s_am = sem("s_am")
        s_amall = sem("s_amall")

        psY = [bank[0], bank[1]]
        psT, psO = bank[2], bank[3]
        psD, psE = wide

        with nc.Block() as block:
            @block.sync
            def _(sp):
                def load(g, slot, rnd):
                    nj = tiles_of(g)
                    after(sp, conv_done, g - 1)
                    sp.dma_start(xs[:, slot, 0:nj, :, :], io["xcol"][:, bass.ds(TG * g, nj), :, :])\
                        .then_inc(xs_in[slot], 16)
                    sp.dma_start(gbx[:, slot, 0:nj * D], gbd[:, bass.ds(TG * D * g, nj * D)])\
                        .then_inc(xs_in[slot], 16)

                def store(g, slot, rnd):
                    nj = tiles_of(g)
                    sp.wait_ge(h1_ready, g + 1)
                    sp.dma_start(h1d[:, bass.ds(TG * g, nj), :], tok[:, bass.ds(TG * g, nj), :])\
                        .then_inc(h1_out[slot], 16)

                pipeline(sp, 0, GA, [(0, load), (3, store)])
                sp.wait_ge(h1_out[0], 16 * (-(-GA // 2)))
                sp.wait_ge(h1_out[1], 16 * (GA // 2))

            @block.gpsimd
            def _(p):
                def fold(g, slot, rnd):
                    nj = tiles_of(g)
                    after(p, conv_done, g - 1)
                    for j in range(nj):
                        ins = p.tensor_tensor(
                            weff[:, slot, j, :, :], w5[:, :, :],
                            gam[:, bass.ds(TG * g + j, 1), :].rearrange("p o c -> p (o c)").unsqueeze(2).to_broadcast([128, NCTX, 128]),
                            ALU.mult)
                    ins.then_inc(weff_ready, 1)

                def scale(g, slot, rnd):
                    nj = tiles_of(g)
                    p.wait_ge(r_ready, g + 1)
                    after(p, lg_ready, g)
                    p.tensor_tensor(lnr[:, 0:nj, :], rr[:, 0:nj, :],
                                    scb[:, :].unsqueeze(1).to_broadcast([128, nj, NN]), ALU.mult).then_inc(rs_ready, 1)

                pipeline(p, 0, GA, [(0, fold), (1, scale)])
                p.wait_ge(s_am, 1)
                p.partition_all_reduce(am[:, 0:2], am2[:, :], 128, RMAX).then_inc(s_amall, 1)

            @block.tensor
            def _(pe):
                def conv(g, slot, rnd):
                    pe.wait_ge(xs_in[slot], 32 * (rnd + 1))
                    pe.wait_ge(weff_ready, g + 1)
                    after(pe, h0_ready, g - 1)
                    for j in range(tiles_of(g)):
                        dst = psY[slot][:, j * D:(j + 1) * D]
                        for k in range(NCTX):
                            pe.matmul(dst, xs[:, slot, j, k, :], weff[:, slot, j, k, :], start=(k == 0), stop=False)
                        last = pe.matmul(dst, mstdT[:, :], gbx[:, slot, j * D:(j + 1) * D], start=False, stop=True)
                    last.then_inc(conv_done, 1)

                def turn(g, slot, rnd):
                    pe.wait_ge(xh_ready, g + 1)
                    after(pe, xT_ready, g)
                    for j in range(tiles_of(g)):
                        last = pe.transpose(psT[:, j * 128:(j + 1) * 128], xh[:, slot, j, :], ident[:, :])
                    last.then_inc(xt_done, 1)

                def cross(g, slot, rnd):
                    pe.wait_ge(xT_ready, g + 1)
                    after(pe, d2_ready, g)
                    for j in range(tiles_of(g)):
                        dst = psD[:, j * NN:(j + 1) * NN]
                        pe.matmul(dst, xT[:, j, :], post[:, :], start=True, stop=False)
                        last = pe.matmul(dst, onesb[0:3, :], psq3[:, :], start=False, stop=True)
                    last.then_inc(cross_done, 1)

                def turn_probs(g, slot, rnd):
                    pe.wait_ge(ex_ready, g + 1)
                    after(pe, eT_low, g)
                    after(pe, eT_high, g)
                    for j in range(tiles_of(g)):
                        for a in range(2):
                            last = pe.transpose(psE[:, (2 * j + a) * 128:(2 * j + a + 1) * 128],
                                                lg[:, slot, j, a * 128:(a + 1) * 128], ident[:, :])
                    last.then_inc(et_done, 1)

                def mix(g, slot, rnd):
                    pe.wait_ge(eT_low, g + 1)
                    pe.wait_ge(eT_high, g + 1)
                    after(pe, h1_ready, g)
                    for j in range(tiles_of(g)):
                        for a in range(2):
                            last = pe.matmul(psO[:, j * D:(j + 1) * D], eT[:, 2 * j + a, :], v2[:, a, :],
                                             start=(a == 0), stop=(a == 1))
                    last.then_inc(out_done, 1)

                pipeline(pe, 0, GA, [(1, turn), (0, conv), (2, turn_probs), (1, cross), (2, mix)])

            @block.scalar
            def _(a):
                def copy_h0(g, slot, rnd):
                    a.wait_ge(conv_done, g + 1)
                    nj = tiles_of(g)
                    a.activation(tok[:, bass.ds(TG * g, nj), :], psY[slot][:, 0:nj * D].rearrange("p (j d) -> p j d", d=D),
                                 ACT.Copy, scale=rstd[:, 0:1]).then_inc(h0_ready, 1)

                def sqrt_var(g, slot, rnd):
                    a.wait_ge(mv0, g + 1)
                    after(a, rs0_ready, g - 1)
                    nj = tiles_of(g)
                    a.activation(std[:, slot, 0:nj], mv[:, slot, 0:nj, 1], ACT.Sqrt, bias=c["eps_ln"][:, :])\
                        .then_inc(std0, 1)

                def copy_xT(g, slot, rnd):
                    a.wait_ge(xt_done, g + 1)
                    after(a, cross_done, g)
                    nj = tiles_of(g)
                    a.activation(xT[:, 0:nj, :].rearrange("p j d -> p (j d)"), psT[:, 0:nj * D], ACT.Copy).then_inc(xT_ready, 1)

                def distance(g, slot, rnd):
                    nj = tiles_of(g)
                    a.wait_ge(d2_ready, g + 1)
                    a.activation(d2[:, 0:nj, :], d2[:, 0:nj, :], ACT.Sqrt).then_inc(dist_ready, 1)

                def inverse(g, slot, rnd):
                    nj = tiles_of(g)
                    a.wait_ge(dist_ready, g + 1)
                    after(a, lg_ready, g)
                    a.activation(lnr[:, 0:nj, :], d2[:, 0:nj, :], ACT.Ln, bias=c["tenth"][:, :]).then_inc(ln_ready, 1)
                    a.wait_ge(ln_ready, g + 1)
                    a.activation(rr[:, 0:nj, :], lnr[:, 0:nj, :], ACT.Exp, scale=-1.0).then_inc(r_ready, 1)

                def probs(g, slot, rnd):
                    a.wait_ge(mn_ready, g + 1)
                    after(a, rz_ready, g - 1)
                    for j in range(tiles_of(g)):
                        last = a.activation(lg[:, slot, j, :], lg[:, slot, j, :], ACT.Exp, scale=-1.0,
                                            bias=mn[:, slot, j:j + 1], accum_out=zz[:, slot, j:j + 1])
                    last.then_inc(ex_ready, 1)

                def copy_eT(g, slot, rnd):
                    nj = tiles_of(g)
                    a.wait_ge(et_done, g + 1)
                    after(a, out_done, g)
                    n = min(nj, 2)
                    a.activation(eT[:, 0:2 * n, :].rearrange("p j d -> p (j d)"), psE[:, 0:n * 256], ACT.Copy)\
                        .then_inc(eT_low, 1)

                pipeline(a, 0, GA, [(1, copy_xT), (2, probs), (2, copy_eT), (0, copy_h0), (1, distance), (0, sqrt_var),
                                 (1, inverse)])
                a.wait_ge(mv1_ready, GA)
                a.activation(hstd[:, :], mv1[:, :, 1], ACT.Sqrt, bias=c["eps_ln"][:, :]).then_inc(s_std1, 1)

            @block.vector
            def _(v):
                def stats(src, dst6, dst2, nj, done6, done2, g):
                    for j in range(nj):
                        last = v.bn_stats(dst6[:, j, :], src(j))
                    last.then_inc(done6, 1)
                    v.wait_ge(done6, g + 1)
                    v.nop(nofuse=True)
                    for j in range(nj):
                        last = v.bn_aggr(dst2(j), dst6[:, j, :])
                    last.then_inc(done2, 1)

                def stats0(g, slot, rnd):
                    v.wait_ge(h0_ready, g + 1)
                    stats(lambda j: tok[:, bass.ds(TG * g + j, 1), :].rearrange("p o d -> p (o d)"), bst,
                          lambda j: mv[:, slot, j, :], tiles_of(g), bn0, mv0, g)

                def normalise0(g, slot, rnd):
                    nj = tiles_of(g)
                    v.wait_ge(std0, g + 1)
                    after(v, xt_done, g - 1)
                    v.reciprocal(rs0[:, slot, 0:nj], std[:, slot, 0:nj]).then_inc(rs0_ready, 1)
                    v.wait_ge(rs0_ready, g + 1)
                    for j in range(nj):
                        last = v.tensor_scalar(xh[:, slot, j, :], tok[:, bass.ds(TG * g + j, 1), :].rearrange("p o d -> p (o d)"),
                                               mv[:, slot, j, 0:1], rs0[:, slot, j:j + 1], ALU.subtract, ALU.mult)
                    last.then_inc(xh_ready, 1)
                    v.scalar_tensor_tensor(vr[:, 0:nj], mv[:, slot, 0:nj, 1], float(D), rs0[:, slot, 0:nj],
                                           ALU.mult, ALU.mult).then_inc(vr_ready, 1)
                    v.wait_ge(vr_ready, g + 1)
                    v.tensor_tensor(xsq[:, slot, 0:nj], vr[:, 0:nj], rs0[:, slot, 0:nj], ALU.mult).then_inc(xsq_ready, 1)

                def dist2(g, slot, rnd):
                    v.wait_ge(xsq_ready, g + 1)
                    v.wait_ge(cross_done, g + 1)
                    after(v, lg_ready, g)
                    for j in range(tiles_of(g)):
                        last = v.tensor_scalar(d2[:, j, :], psD[:, j * NN:(j + 1) * NN], xsq[:, slot, j:j + 1], 0.0,
                                               ALU.add, ALU.max)
                    last.then_inc(d2_ready, 1)

                def logits(g, slot, rnd):
                    nj = tiles_of(g)
                    v.wait_ge(r_ready, g + 1)
                    v.scalar_tensor_tensor(d2[:, 0:nj, :], d2[:, 0:nj, :], 0.1, rr[:, 0:nj, :], ALU.add, ALU.mult)\
                        .then_inc(t_ready, 1)
                    v.wait_ge(t_ready, g + 1)
                    v.wait_ge(rs_ready, g + 1)
                    after(v, et_done, g - 1)
                    v.scalar_tensor_tensor(lg[:, slot, 0:nj, :], d2[:, 0:nj, :], 2.0, lnr[:, 0:nj, :],
                                           ALU.subtract, ALU.mult).then_inc(lg_ready, 1)
                    v.wait_ge(lg_ready, g + 1)
                    v.tensor_reduce(mn[:, slot, 0:nj], lg[:, slot, 0:nj, :], AX.X, ALU.min).then_inc(mn_ready, 1)

                def copy_eT(g, slot, rnd):
                    v.wait_ge(et_done, g + 1)
                    after(v, out_done, g)
                    n = max(tiles_of(g) - 2, 0)
                    if n:
                        v.tensor_copy(eT[:, 4:4 + 2 * n, :].rearrange("p j d -> p (j d)"),
                                      psE[:, 512:512 + n * 256]).then_inc(eT_high, 1)
                    else:
                        v.nop(nofuse=True).then_inc(eT_high, 1)

                def residual(g, slot, rnd):
                    nj = tiles_of(g)
                    v.wait_ge(ex_ready, g + 1)
                    v.reciprocal(rz[:, 0:nj], zz[:, slot, 0:nj]).then_inc(rz_ready, 1)
                    v.wait_ge(rz_ready, g + 1)
                    v.wait_ge(out_done, g + 1)
                    for j in range(nj):
                        t = tok[:, bass.ds(TG * g + j, 1), :].rearrange("p o d -> p (o d)")
                        last = v.scalar_tensor_tensor(t, psO[:, j * D:(j + 1) * D], rz[:, j:j + 1], t, ALU.mult, ALU.add)
                    last.then_inc(h1_ready, 1)

                def stats1(g, slot, rnd):
                    nj = tiles_of(g)
                    v.wait_ge(h1_ready, g + 1)
                    here = tok[:, bass.ds(TG * g, nj), :]
                    v.tensor_reduce(hmax[:, bass.ds(TG * g, nj)], here, AX.X, ALU.max)
                    v.tensor_reduce(hmin[:, bass.ds(TG * g, nj)], here, AX.X, ALU.min)
                    stats(lambda j: tok[:, bass.ds(TG * g + j, 1), :].rearrange("p o d -> p (o d)"), bst1,
                          lambda j: mvs[:, j, :], nj, bn1, mvs_ready, g)
                    v.wait_ge(mvs_ready, g + 1)
                    v.tensor_copy(mv1[:, bass.ds(TG * g, nj), :], mvs[:, 0:nj, :]).then_inc(mv1_ready, 1)

                pipeline(v, 0, GA, [(1, dist2), (2, copy_eT), (0, stats0), (0, normalise0), (2, residual), (1, logits),
                                 (2, stats1)])
                count = [0]
                s_vf = s_end

                def link(ins):
                    count[0] += 1
                    ins.then_inc(s_vf, 1)
                    v.wait_ge(s_vf, count[0])

                v.wait_ge(mv1_ready, GA)
                link(v.tensor_tensor(hmax[:, :], hmax[:, :], mv1[:, :, 0], ALU.subtract))
                link(v.tensor_tensor(hmin[:, :], mv1[:, :, 0], hmin[:, :], ALU.subtract))
                link(v.tensor_tensor(hmax[:, :], hmax[:, :], hmin[:, :], ALU.max))
                v.wait_ge(s_std1, 1)
                link(v.reciprocal(hmin[:, :], hstd[:, :]))
                link(v.tensor_tensor(hmax[:, :], hmax[:, :], hmin[:, :], ALU.mult))
                link(v.tensor_reduce(am2[:, 0:1], hmax[:, :], AX.X, ALU.max))
                link(v.tensor_reduce(am[:, 2:3], wffn[:, :], AX.X, ALU.max))
                link(v.tensor_reduce(am[:, 3:4], wffn[:, :], AX.X, ALU.min))
                link(v.tensor_scalar(am[:, 3:4], am[:, 3:4], -1.0, None, ALU.mult))
                v.tensor_tensor(am2[:, 1:2], am[:, 2:3], am[:, 3:4], ALU.max).then_inc(s_am, 1)
                v.wait_ge(s_amall, 1)
                link(v.tensor_scalar(am[:, 0:2], am[:, 0:2], 1e-12, None, ALU.max))
                link(v.reciprocal(am[:, 4:6], am[:, 0:2]))
                link(v.tensor_scalar(am[:, 6:8], am[:, 4:6], FP8_MAX, None, ALU.mult))
                link(v.tensor_copy(c["fscale"][:, 0:1], am[:, 6:7]))
                link(v.tensor_tensor(am[:, 2:3], am[:, 0:1], am[:, 1:2], ALU.mult))
                link(v.tensor_scalar(c["fscale"][:, 1:2], am[:, 2:3], 1.0 / FP8_MAX / FP8_MAX, None, ALU.mult))
                quantise(v, link, wffn[:, :], am[:, 7:8], qtmp[:, :], qm[:, :], c["wq"][:, :])

    nc.clear_and_free_semaphores(used)
    nc.all_engine_barrier()

def quantise(v, link, src, scale, tmp, mag, dst):
    link(v.tensor_scalar(tmp, src, scale, FP8_MAX, ALU.mult, ALU.min))
    link(v.tensor_scalar(mag.bitcast(I32), tmp.bitcast(I32), 0x7F800000, None, ALU.bitwise_and))
    link(v.tensor_scalar(mag, mag, MINEXP, ROUND, ALU.max, ALU.mult))
    link(v.scalar_tensor_tensor(tmp, tmp, -FP8_MAX, mag, ALU.max, ALU.add))
    link(v.tensor_tensor(dst, tmp, mag, ALU.subtract))


def rsqrt(v, var, eps, out, xe, half, done, base):
    v.tensor_scalar(xe, var, eps, None, ALU.add).then_inc(done, 1)
    v.wait_ge(done, base + 1)
    v.tensor_scalar(half.bitcast(I32), xe.bitcast(I32), 1, None, ALU.logical_shift_right).then_inc(done, 1)
    v.wait_ge(done, base + 2)
    v.tensor_scalar(out.bitcast(I32), half.bitcast(I32), -1.0, float(0x5F3759DF), ALU.mult, ALU.add).then_inc(done, 1)
    for k in range(3):
        v.wait_ge(done, base + 3 + 3 * k)
        v.tensor_tensor(half, out, out, ALU.mult).then_inc(done, 1)
        v.wait_ge(done, base + 4 + 3 * k)
        v.scalar_tensor_tensor(half, half, -0.5, xe, ALU.mult, ALU.mult).then_inc(done, 1)
        v.wait_ge(done, base + 5 + 3 * k)
        v.scalar_tensor_tensor(out, half, 1.5, out, ALU.add, ALU.mult).then_inc(done, 1)
    v.wait_ge(done, base + RSQRT_STEPS)


RSQRT_STEPS = 12


def back(nc, io, sb, sem, bank, wide, c, h1d, h3d, h4d, xed, yed, destd, out):
    ident, identb, ones, onesb = c["ident"], c["identb"], c["ones"], c["onesb"]
    before, beforeb, wq, fscale = c["before"], c["beforeb"], c["wq"], c["fscale"]
    NB = B // 2
    GR = GA
    NQ = NT // TG
    ES = 4

    def entries(engine, table, first, count, top):
        return nc.values_load_multi_w_load_instructions(
            table[0:1, bass.ds(first, count)], engines=[engine], min_val=0, max_val=top,
            skip_runtime_bounds_check_because="the chip computes the table and keeps it within the bounds")[1]

    wgu = sb("wgu", [128, NE, 2 * F])
    wdt = sb("wdt", [F, NE, D])
    rwt = sb("rwt", [128, NE])
    rbias = sb("rbias", [1, NE])
    sgu = sb("sgu", [128, 4 * F])
    sdt = sb("sdt", [128, D])
    zrow = sb("zrow", [128, XW])

    h1s = sb("h1s", [128, 2, 4, D])
    bstb = sb("bstb", [128, 4, 6])
    mvb = sb("mvb", [128, 4, 2])
    ra = sb("ra", [128, 4])
    xea = sb("xea", [128, 4])
    hfa = sb("hfa", [128, 4])
    xq = sb("xq", [128, 4, D])
    qmag = sb("qmag", [128, 4, D])
    xqb = sb("xqb", [128, 4, D], BF16)
    xqT = sb("xqT", [128, 4, D], BF16)
    h2 = sb("h2", [128, 2, 4, D])
    bstc = sb("bstc", [128, 4, 6])
    mvc = sb("mvc", [128, 4, 2])
    rb = sb("rb", [128, 4])
    xeb = sb("xeb", [128, 4])
    hfb = sb("hfb", [128, 4])
    xn = sb("xn", [128, 2, 4, D + 4])
    xnT = sb("xnT", [128, 2, T + 1])
    e0 = sb("e0", [128, 2, T + 1])
    e1 = sb("e1", [128, 2, T + 1])
    rzb = sb("rzb", [128, 4])
    h3 = sb("h3", [128, 2, 4, D])

    h3s = sb("h3s", [128, 2, TG, D])
    bstd = sb("bstd", [128, TG, 6])
    mvd = sb("mvd", [128, TG, 2])
    rc = sb("rc", [128, TG])
    xec = sb("xec", [128, TG])
    hfc = sb("hfc", [128, TG])
    xr = sb("xr", [128, 2, TG, XW])
    x4T = sb("x4T", [128, TG, D])
    lo = sb("lo", [128, TG, NE + 2])
    lr = sb("lr", [128, TG, NE + 2])
    t8 = sb("t8", [128, TG, 8])
    mask = sb("mask", [128, TG, NE], BF16)
    taken = sb("taken", [128, NE])
    first1 = sb("first1", [128, NE])
    slotm = sb("slotm", [128, TG, NE])
    valid = sb("valid", [128, TG, NE])
    dest = sb("dest", [128, 2, TG, NE])
    dk = sb("dk", [128, TG, 8])
    zk = sb("zk", [128, TG, TOPK])
    idxs = sb("idxs", [128, 2, TG, TOPK], I32)
    ex = sb("ex", [128, TG, NE])
    zz = sb("zz4", [128, TG])
    s6 = sb("s6", [128, TG])
    den = sb("den", [128, TG])
    th = sb("th", [128, TG, 2 * F])
    sa = sb("sa", [128, TG, 2 * F])
    hs = sb("hs", [128, TG, 2 * F])
    hsT = sb("hsT", [128, TG, D])
    h4 = sb("h4", [128, 2, TG, D])

    eiota = sb("eiota", [NE + 1, 2], I32)
    iiota = sb("iiota", [NE + 1, NT], I32)
    it = sb("it", [NE + 1, NT])
    itin = sb("itin", [NE + 1, NT])
    oh = sb("oh", [NE + 1, NT])
    col = sb("col", [NE + 1, 16])
    coli = sb("coli", [NE, 2], I32)
    diag = sb("diag", [NE, NE])
    tin = sb("tin", [1, NT], I32)
    texp = sb("texp", [1, NT], I32)
    ttail = sb("ttail", [1, NE], I32)

    xin = sb("xin", [128, ES, TG, XW])
    xeT = sb("xeT", [128, 2, TG, 128])
    gate = sb("gate", [128, ES, TG])
    the = sb("the", [128, TG, F])
    ae = sb("ae", [128, TG, F])
    hh = sb("hh", [128, 2, TG, F])
    hT = sb("hT", [F, 2, TG, 128])
    yo = sb("yo", [128, 2, TG, D])

    dests = sb("dests", [128, 2, TG, NE])
    shift = sb("shift", [128, NE])
    drow = sb("drow", [128, TG, NE])
    dg = sb("dg", [128, TG, 8])
    zg = sb("zg", [128, TG, TOPK])
    idxg = sb("idxg", [128, 2, TG, TOPK], I32)
    yg = sb("yg", [128, 2, TG, TOPK, D])
    h4s, ot = h3s, h4

    n = {}
    for name in ("s_wt", "s_c", "s_c2", "s_z", "s_half",
                 "bnb", "mvb_r", "rsa", "xq_r", "q_r", "xqb_r", "qt_done", "xqT_r", "ffn_done", "h2_r", "bnc",
                 "mvc_r", "rsb", "xn_r", "xt_done2", "xnT_r", "s_done", "e_r", "pv_done", "rzb_r", "h3_r",
                 "bnd", "mvd_r", "rsc", "x4_r", "x4t_done", "x4T_r", "lo_done", "gu_done", "lo_r", "top_r",
                 "rep_r", "mask_r", "nl_r", "cum_done", "slot_r", "valid_r", "dest0_r", "dest_r", "taken_r",
                 "dk_r", "zk_r", "idx_r", "shift_p", "shift_r", "ex_r", "em_r", "s6_r", "den_r", "row_r",
                 "th_r", "sa_r", "hs_r", "hst_done", "hsT_r", "sh_done", "h4_r",
                 "tab_v", "tab_p", "tab_ready", "tail_z",
                 "xet_done", "xeT_r", "geu_done", "g1_r", "gx_r", "gate_r", "the_r", "ae_r", "hh_r", "ht_done",
                 "hT_r", "dn_done", "yo_r",
                 "idxg_r", "sh0_r", "sh1_r", "dg_r", "zg_r", "sum_done", "ot_r"):
        n[name] = sem(name)
    h1_in = [sem(f"h1_in{i}") for i in range(2)]
    h3_out = [sem(f"h3_out{i}") for i in range(2)]
    h3_in = [sem(f"h3_in{i}") for i in range(2)]
    h4_out = [sem(f"h4_out{i}") for i in range(2)]
    scat = [sem(f"scat{i}") for i in range(2)]
    xin_in = [sem(f"xin_in{i}") for i in range(ES)]
    yo_out = [sem(f"yo_out{i}") for i in range(2)]
    gath = [sem(f"gath{i}") for i in range(2)]
    h4_in = [sem(f"h4_in{i}") for i in range(2)]
    dest_out = [sem(f"dest_out{i}") for i in range(2)]
    dest_in = [sem(f"dest_in{i}") for i in range(2)]
    ot_out = [sem(f"ot_out{i}") for i in range(2)]

    pP = wide[0]
    pS0, pS1 = bank[3], wide[1][:, 0:512]
    WEIGHTS = 16 * 7
    eT_ = (bank[0], bank[2])
    eG = (bank[1], bank[3])
    eH = (wide[0][:, 0:512], wide[0][:, 512:1024])
    eO = (wide[1][:, 0:512], wide[1][:, 512:1024])
    SP, PE = mybir.EngineType.SP, mybir.EngineType.PE

    with nc.Block() as block:
        @block.gpsimd
        def _(p):
            p.memset(zrow[:, :], 0.0).then_inc(n["s_c"], 1)
            p.memset(h1s[:, :, :, :], 0.0).then_inc(n["s_c"], 1)
            for slot in range(2):
                for j in range(4):
                    p.memset(xn[:, slot, j, D:D + 1], 1.0)
            p.memset(lo[:, :, :], BIG)
            p.memset(taken[:, :], 0.0)
            p.memset(col[:, :], 0.0)
            p.iota(eiota[:, :], [[0, 2]], base=0, channel_multiplier=1)
            p.iota(iiota[:, :], [[128, NT]], base=0, channel_multiplier=0).then_inc(n["s_c"], 1)

            def scatter(g, slot, rnd):
                nj = tiles_of(g)
                p.wait_ge(n["row_r"], g + 1)
                p.wait_ge(n["idx_r"], g + 1)
                p.nop(nofuse=True)
                for j in range(nj):
                    for k in range(TOPK):
                        p.indirect_dma_start(
                            xed[:, :], bass.IndirectOffsetOnAxis(ap=idxs[:, slot, j, k:k + 1], axis=0),
                            xr[:, slot, j, :], None, bounds_check=ZR - 1, oob_is_err=False).then_inc(scat[slot], 16)

            def gather(g, slot, rnd):
                p.wait_ge(n["idxg_r"], g + 1)
                after(p, n["sum_done"], g - 1)
                p.nop(nofuse=True)
                for j in range(tiles_of(g)):
                    for k in range(TOPK):
                        p.indirect_dma_start(
                            yg[:, slot, j, k, :], None, yed[:, :],
                            bass.IndirectOffsetOnAxis(ap=idxg[:, slot, j, k:k + 1], axis=0)).then_inc(gath[slot], 16)

            for a, b in group_steps():
                pipeline(p, a, b, [(0, scatter)])
            p.wait_ge(yo_out[0], 16 * (-(-NQ // 2)))
            p.wait_ge(yo_out[1], 16 * (NQ // 2))
            p.wait_ge(n["s_z"], 16)
            pipeline(p, 0, GR, [(0, gather)])

        @block.sync
        def _(sp):
            def load_h1(g, slot, rnd):
                after(sp, n["h2_r"], g - 1)
                src = h1d[bass.ds(2 * g, 2), :, :].rearrange("b t d -> t b d")
                sp.dma_start(h1s[:, slot, 0:4:2, :], src[0:HALF[0]]).then_inc(h1_in[slot], 16)
                sp.dma_start(h1s[0:HALF[1], slot, 1:4:2, :], src[HALF[0]:T]).then_inc(h1_in[slot], 16)

            def store_h3(g, slot, rnd):
                sp.wait_ge(n["h3_r"], g + 1)
                dst = h3d[bass.ds(2 * T * g, 2 * T), :].rearrange("(b t) d -> t b d", t=T)
                sp.dma_start(dst[0:HALF[0]], h3[:, slot, 0:4:2, :]).then_inc(h3_out[slot], 16)
                sp.dma_start(dst[HALF[0]:T], h3[0:HALF[1], slot, 1:4:2, :]).then_inc(h3_out[slot], 16)

            sp.wait_ge(n["s_c"], 3)
            for dst, src in ((wgu, "wgu"), (wdt, "wdt")):
                sp.dma_start(dst[:, :, :], io[src]).then_inc(n["s_wt"], 16)
            for dst, src in ((rwt, "rwt"), (rbias, "rbias"), (sgu, "sgu"), (sdt, "sdt")):
                sp.dma_start(dst[:, :], io[src]).then_inc(n["s_wt"], 16)
            sp.dma_start(xed[ZR:ZR + 128, :], zrow[:, :]).then_inc(n["s_wt"], 16)
            sp.dma_start(yed[YZ:YZ + 128, :], zrow[:, 0:D]).then_inc(n["s_z"], 16)
            pipeline(sp, 0, NB, [(0, load_h1), (2, store_h3)])
            sp.wait_ge(h3_out[0], 32 * (NB // 2))
            sp.wait_ge(h3_out[1], 32 * (NB // 2))

            def load_h3(g, slot, rnd):
                nj = tiles_of(g)
                after(sp, n["h4_r"], g - 1)
                sp.dma_start(h3s[:, slot, 0:nj, :],
                             h3d[bass.ds(TG * 128 * g, nj * 128), :].rearrange("(j p) d -> p j d", p=128))\
                    .then_inc(h3_in[slot], 16)

            def store_h4(g, slot, rnd):
                nj = tiles_of(g)
                sp.wait_ge(n["h4_r"], g + 1)
                sp.dma_start(h4d[bass.ds(TG * 128 * g, nj * 128), :].rearrange("(j p) d -> p j d", p=128),
                             h4[:, slot, 0:nj, :]).then_inc(h4_out[slot], 16)
                sp.wait_ge(n["dest_r"], g + 1)
                sp.dma_start(destd[bass.ds(TG * g, nj), :, :].rearrange("j p e -> p j e"),
                             dest[:, slot, 0:nj, :]).then_inc(dest_out[slot], 16)

            def load_rows(q, slot, rnd):
                rows = entries(SP, tin, TG * q, TG, ZR)
                after(sp, n["gate_r"], q - ES + 1)
                for j, row in enumerate(rows):
                    sp.dma_start(xin[:, slot, j, :], xed[bass.ds(row, 128), :]).then_inc(xin_in[slot], 16)

            def store_rows(q, slot, rnd):
                sp.wait_ge(n["yo_r"], q + 1)
                sp.dma_start(yed[bass.ds(TG * 128 * q, TG * 128), :].rearrange("(j p) d -> p j d", p=128),
                             yo[:, slot % 2, :, :]).then_inc(yo_out[slot % 2], 16)

            for a, b in group_steps():
                pipeline(sp, a, b, [(0, load_h3), (0, store_h4)])
                sp.wait_ge(n["tab_ready"], 1)
                for e in range(0, NE, 4):
                    for row in entries(SP, ttail, e, 4, ZR - 128):
                        sp.dma_start(xed[bass.ds(row, 128), :], zrow[:, :]).then_inc(n["tail_z"], 16)
                sp.wait_ge(n["tail_z"], 16 * NE)
                tiles = T
                sp.wait_ge(scat[0], 16 * TOPK * sum(tiles_of(g) for g in range(0, GR, 2)))
                sp.wait_ge(scat[1], 16 * TOPK * sum(tiles_of(g) for g in range(1, GR, 2)))
                pipeline(sp, 0, NQ, [(0, load_rows), (5, store_rows)], ES)
            sp.wait_ge(h4_out[0], 16 * (-(-GR // 2)))
            sp.wait_ge(h4_out[1], 16 * (GR // 2))
            sp.wait_ge(dest_out[0], 16 * (-(-GR // 2)))
            sp.wait_ge(dest_out[1], 16 * (GR // 2))

            def load_tokens(g, slot, rnd):
                nj = tiles_of(g)
                after(sp, n["sh1_r"], g - 1)
                sp.dma_start(dests[:, slot, 0:nj, :], destd[bass.ds(TG * g, nj), :, :].rearrange("j p e -> p j e"))\
                    .then_inc(dest_in[slot], 16)
                after(sp, n["ot_r"], g - 1)
                sp.dma_start(h4s[:, slot, 0:nj, :],
                             h4d[bass.ds(TG * 128 * g, nj * 128), :].rearrange("(j p) d -> p j d", p=128))\
                    .then_inc(h4_in[slot], 16)

            def store_out(g, slot, rnd):
                nj = tiles_of(g)
                sp.wait_ge(n["ot_r"], g + 1)
                sp.dma_start(out[bass.ds(TG * 128 * g, nj * 128), :].rearrange("(j p) d -> p j d", p=128),
                             ot[:, slot, 0:nj, :]).then_inc(ot_out[slot], 16)

            pipeline(sp, 0, GR, [(0, load_tokens), (1, store_out)])
            sp.wait_ge(ot_out[0], 16 * (-(-GR // 2)))
            sp.wait_ge(ot_out[1], 16 * (GR // 2))

        @block.tensor
        def _(pe):
            pe.wait_ge(n["s_wt"], WEIGHTS)
            pe.wait_ge(n["s_c"], 3)
            pQT = bank[0][:, 0:256].bitcast(BF16)
            pF, pX = bank[1], bank[2]

            def turn_q(g, slot, rnd):
                pe.wait_ge(n["xqb_r"], g + 1)
                after(pe, n["xqT_r"], g)
                for j in range(4):
                    last = pe.transpose(pQT[:, j * D:(j + 1) * D], xqb[:, j, :], identb[:, :])
                last.then_inc(n["qt_done"], 1)

            def ffn(g, slot, rnd):
                pe.wait_ge(n["xqT_r"], g + 1)
                after(pe, n["h2_r"], g)
                for j in range(4):
                    last = pe.matmul(pF[:, j * D:(j + 1) * D], xqT[:, j, :], wq[:, :], start=True, stop=True)
                last.then_inc(n["ffn_done"], 1)

            def turn_x(g, slot, rnd):
                pe.wait_ge(n["xn_r"], g + 1)
                after(pe, n["xnT_r"], g)
                for i in range(2):
                    for h, m in enumerate(HALF):
                        last = pe.transpose(pX[:, 256 * i + 128 * h:256 * i + 128 * h + m],
                                            xn[0:m, slot, 2 * i + h, 0:D], ident[0:m, 0:m])
                last.then_inc(n["xt_done2"], 1)

            def scores(g, slot, rnd):
                pe.wait_ge(n["xnT_r"], g + 1)
                after(pe, n["e_r"], 2 * g)
                for i in range(2):
                    for h, m in enumerate(HALF):
                        dst = (pS0, pS1)[h][0:m, 256 * i:256 * i + T]
                        last = pe.matmul(dst, xnT[:, i, 128 * h:128 * h + m], xnT[:, i, 0:T], start=True, stop=True)
                last.then_inc(n["s_done"], 1)

            def mix(g, slot, rnd):
                pe.wait_ge(n["e_r"], 2 * g + 2)
                after(pe, n["h3_r"], g)
                for i in range(2):
                    for h, m in enumerate(HALF):
                        dst = pP[0:m, 512 * i + 256 * h:512 * i + 256 * h + D + 1]
                        for h2_, (e, m2) in enumerate(zip((e0, e1), HALF)):
                            last = pe.matmul(dst, e[0:m2, i, 128 * h:128 * h + m], xn[0:m2, slot, 2 * i + h2_, 0:D + 1],
                                             start=(h2_ == 0), stop=(h2_ == 1))
                last.then_inc(n["pv_done"], 1)

            pipeline(pe, 0, NB, [(0, turn_q), (0, ffn), (1, turn_x), (1, scores), (1, mix)])

            rA, rB, rC = bank[0], bank[1], wide[1]

            def turn_r(g, slot, rnd):
                pe.wait_ge(n["x4_r"], g + 1)
                after(pe, n["h4_r"], g)
                for j in range(tiles_of(g)):
                    last = pe.transpose(rA[:, j * 128:(j + 1) * 128], xr[:, slot, j, 0:D], ident[:, :])
                last.then_inc(n["x4t_done"], 1)

            def route(g, slot, rnd):
                nj = tiles_of(g)
                pe.wait_ge(n["x4T_r"], g + 1)
                after(pe, n["taken_r"], g)
                after(pe, n["slot_r"], g)
                for j in range(nj):
                    dst = rB[:, j * NE:(j + 1) * NE]
                    pe.matmul(dst, x4T[:, j, :], rwt[:, :], start=True, stop=False)
                    last = pe.matmul(dst, ones[0:1, :], rbias[:, :], start=False, stop=True)
                last.then_inc(n["lo_done"], 1)
                after(pe, n["hs_r"], g)
                for j in range(nj):
                    last = pe.matmul(rC[:, j * 256:(j + 1) * 256], x4T[:, j, :], sgu[:, :], start=True, stop=True)
                last.then_inc(n["gu_done"], 1)

            def count(g, slot, rnd):
                nj = tiles_of(g)
                pe.wait_ge(n["mask_r"], g + 1)
                pe.wait_ge(n["lo_r"], g + 1)
                for j in range(nj):
                    dst = rB[:, 256 + j * NE:256 + (j + 1) * NE]
                    for i in range(j + 1):
                        pe.matmul(dst, beforeb[:, :] if i == j else onesb[:, :], mask[:, i, :],
                                  start=(i == 0), stop=(i == j))
                for i in range(nj):
                    last = pe.matmul(rB[:, 0:NE], onesb[:, :], mask[:, i, :], start=(i == 0), stop=(i == nj - 1))
                last.then_inc(n["cum_done"], 1)

            def turn_h(g, slot, rnd):
                pe.wait_ge(n["hs_r"], g + 1)
                for j in range(tiles_of(g)):
                    last = pe.transpose(rA[:, j * 128:(j + 1) * 128], hs[:, j, :], ident[:, :])
                last.then_inc(n["hst_done"], 1)

            def shared_down(g, slot, rnd):
                pe.wait_ge(n["hsT_r"], g + 1)
                for j in range(tiles_of(g)):
                    last = pe.matmul(rA[:, j * D:(j + 1) * D], hsT[:, j, :], sdt[:, :], start=True, stop=True)
                last.then_inc(n["sh_done"], 1)

            def turn_e(q, slot, rnd):
                pe.wait_ge(xin_in[slot], 64 * (rnd + 1))
                after(pe, n["g1_r"], q - 1)
                for j in range(TG):
                    last = pe.transpose(eT_[slot % 2][:, j * 128:(j + 1) * 128], xin[:, slot, j, 0:D], ident[:, :])
                last.then_inc(n["xet_done"], 1)

            def up(q, slot, rnd):
                experts = entries(PE, texp, TG * q, TG, NE - 1)
                pe.wait_ge(n["xeT_r"], q + 1)
                after(pe, n["hh_r"], q - 1)
                pe.nop(nofuse=True)
                lg = eT_[slot % 2]
                for j, e in enumerate(experts):
                    pe.matmul(lg[:, j:j + 1], xeT[:, slot % 2, j, :], rwt[:, bass.ds(e, 1)], start=True, stop=False)
                    pe.matmul(lg[:, j:j + 1], ones[0:1, :], rbias[:, bass.ds(e, 1)], start=False, stop=True)
                    last = pe.matmul(eG[slot % 2][:, j * 128:(j + 1) * 128], xeT[:, slot % 2, j, :],
                                     wgu[:, bass.ds(e, 1), :].rearrange("p o f -> p (o f)"), start=True, stop=True)
                last.then_inc(n["geu_done"], 1)

            def turn_hh(q, slot, rnd):
                pe.wait_ge(n["hh_r"], q + 1)
                after(pe, n["hT_r"], q - 1)
                pe.nop(nofuse=True)
                for j in range(TG):
                    last = pe.transpose(eH[slot % 2][0:F, j * 128:(j + 1) * 128], hh[:, slot % 2, j, :], ident[:, :])
                last.then_inc(n["ht_done"], 1)

            def down(q, slot, rnd):
                experts = entries(PE, texp, TG * q, TG, NE - 1)
                pe.wait_ge(n["hT_r"], q + 1)
                after(pe, n["yo_r"], q - 1)
                pe.nop(nofuse=True)
                for j, e in enumerate(experts):
                    last = pe.matmul(eO[slot % 2][:, j * D:(j + 1) * D], hT[:, slot % 2, j, :],
                                     wdt[:, bass.ds(e, 1), :].rearrange("p o f -> p (o f)"), start=True, stop=True)
                last.then_inc(n["dn_done"], 1)

            def first_rows():
                pe.matmul(rB[:, 0:NE], ones[0:NE, :], diag[:, :], start=True, stop=True).then_inc(n["tab_p"], 1)

            pe.wait_ge(n["h3_r"], NB)
            pe.wait_ge(n["tab_v"], 1)
            first_rows()
            for a, b in group_steps():
                pipeline(pe, a, b, [(0, turn_r), (0, route), (0, count), (0, turn_h), (0, shared_down)])
                pe.wait_ge(n["tab_v"], 2)
                pe.wait_ge(n["taken_r"], GR)
                pe.transpose(rB[0:NE, 0:128], taken[:, :], ident[:, :]).then_inc(n["tab_p"], 1)
                pe.wait_ge(n["tab_v"], 3)
                pe.matmul(rB[0:NE + 1, 128:129], before[0:NE, 0:NE + 1], col[0:NE, 2:3], start=True, stop=True)\
                    .then_inc(n["tab_p"], 1)
                for k, src in enumerate((oh, itin)):
                    pe.wait_ge(n["tab_v"], (4, 6)[k])
                    for i, w in enumerate(range(0, NT, 512)):
                        m = min(512, NT - w)
                        dst = (wide[1][0:1, 0:512], wide[1][0:1, 512:1024], rA[0:1, 0:512])[i]
                        last = pe.matmul(dst[:, 0:m], ones[0:NE + 1, 0:1], src[:, w:w + m], start=True, stop=True)
                    last.then_inc(n["tab_p"], 1)
                pe.wait_ge(n["tab_v"], 7)
                pe.matmul(rB[0:1, 0:NE], col[0:NE, 11:12], ident[0:NE, 0:NE], start=True, stop=True)\
                    .then_inc(n["tab_p"], 1)
                pe.matmul(rB[:, 256:256 + NE], ones[0:NE, :], diag[:, :], start=True, stop=True).then_inc(n["tab_p"], 1)
                pe.wait_ge(n["tab_ready"], 1)
                pipeline(pe, 0, NQ, [(0, turn_e), (1, up), (3, down), (2, turn_hh)], ES)

            def total(g, slot, rnd):
                nj = tiles_of(g)
                pe.wait_ge(gath[slot], 16 * TOPK * (TG * rnd + nj))
                after(pe, n["ot_r"], g - 1)
                for j in range(nj):
                    for k in range(TOPK):
                        last = pe.matmul(bank[slot][:, j * D:(j + 1) * D], ident[:, :], yg[:, slot, j, k, :],
                                         start=(k == 0), stop=(k == TOPK - 1))
                last.then_inc(n["sum_done"], 1)

            pe.wait_ge(n["yo_r"], NQ)
            pipeline(pe, 0, GR, [(0, total)])

        @block.scalar
        def _(a):
            def copy_q(g, slot, rnd):
                a.wait_ge(n["qt_done"], g + 1)
                after(a, n["ffn_done"], g)
                a.activation(xqT[:, :, :].rearrange("p j d -> p (j d)"), bank[0][:, 0:256].bitcast(BF16), ACT.Copy)\
                    .then_inc(n["xqT_r"], 1)

            def copy_x(g, slot, rnd):
                a.wait_ge(n["xt_done2"], g + 1)
                after(a, n["s_done"], g)
                a.activation(xnT[:, :, 0:T], bank[2][:, :].rearrange("p (i t) -> p i t", i=2)[:, :, 0:T], ACT.Copy)\
                    .then_inc(n["xnT_r"], 1)

            def expo(g, slot, rnd):
                a.wait_ge(n["s_done"], g + 1)
                after(a, n["pv_done"], g)
                for e, ps, m in ((e0, pS0, HALF[0]), (e1, pS1, HALF[1])):
                    a.activation(e[0:m, :, 0:T], ps[0:m, :].rearrange("p (i t) -> p i t", i=2)[:, :, 0:T], ACT.Exp,
                                 scale=SCALE).then_inc(n["e_r"], 1)

            pipeline(a, 0, NB, [(0, copy_q), (1, copy_x), (1, expo)])

            def copy_x4(g, slot, rnd):
                nj = tiles_of(g)
                a.wait_ge(n["x4t_done"], g + 1)
                after(a, n["gu_done"], g)
                a.activation(x4T[:, 0:nj, :].rearrange("p j d -> p (j d)"), bank[0][:, 0:nj * 128], ACT.Copy)\
                    .then_inc(n["x4T_r"], 1)

            def tanh(g, slot, rnd):
                nj = tiles_of(g)
                a.wait_ge(n["gu_done"], g + 1)
                after(a, n["sa_r"], g)
                a.activation(th[:, 0:nj, :], wide[1][:, 0:nj * 256].rearrange("p (j f) -> p j f", j=nj)[:, :, 0:2 * F],
                             ACT.Tanh, scale=0.5).then_inc(n["th_r"], 1)

            def probs(g, slot, rnd):
                a.wait_ge(n["nl_r"], g + 1)
                after(a, n["den_r"], g)
                for j in range(tiles_of(g)):
                    last = a.activation(ex[:, j, :], lo[:, j, 0:NE], ACT.Exp, bias=xr[:, slot, j, D:D + 1],
                                        accum_out=zz[:, j:j + 1])
                last.then_inc(n["ex_r"], 1)

            def copy_h(g, slot, rnd):
                nj = tiles_of(g)
                a.wait_ge(n["hst_done"], g + 1)
                after(a, n["sh_done"], g)
                a.activation(hsT[:, 0:nj, :].rearrange("p j d -> p (j d)"), bank[0][:, 0:nj * 128], ACT.Copy)\
                    .then_inc(n["hsT_r"], 1)

            def copy_xe(q, slot, rnd):
                a.wait_ge(n["xet_done"], q + 1)
                after(a, n["geu_done"], q - 1)
                a.activation(xeT[:, slot % 2, :, :].rearrange("p j d -> p (j d)"), eT_[slot % 2][:, :], ACT.Copy)\
                    .then_inc(n["xeT_r"], 1)

            def tanh_e(q, slot, rnd):
                a.wait_ge(n["geu_done"], q + 1)
                after(a, n["ae_r"], q)
                a.activation(the[:, :, :], eG[slot % 2][:, :].rearrange("p (j f) -> p j f", j=TG)[:, :, 0:F],
                             ACT.Tanh, scale=0.5).then_inc(n["the_r"], 1)

            def gate_e(q, slot, rnd):
                a.wait_ge(n["g1_r"], q + 1)
                a.activation(gate[:, slot, :], gate[:, slot, :], ACT.Exp).then_inc(n["gx_r"], 1)

            def copy_y(q, slot, rnd):
                a.wait_ge(n["dn_done"], q + 1)
                a.wait_ge(n["gate_r"], q + 1)
                half = slot % 2
                if not isinstance(q, int) or q >= 2:
                    a.wait_ge(yo_out[half], 16 * (2 * rnd + slot // 2))
                for j in range(TG):
                    last = a.activation(yo[:, half, j, :], eO[half][:, j * D:(j + 1) * D], ACT.Copy,
                                        scale=gate[:, slot, j:j + 1])
                last.then_inc(n["yo_r"], 1)

            for s0, s1 in group_steps():
                pipeline(a, s0, s1, [(0, copy_x4), (0, tanh), (0, probs), (0, copy_h)])
                pipeline(a, 0, NQ, [(0, copy_xe), (1, tanh_e), (1, gate_e), (3, copy_y)], ES)

        @block.vector
        def _(v):
            v.wait_ge(n["s_wt"], WEIGHTS)
            v.tensor_scalar(wdt[:, :, :], wdt[:, :, :], 0.5, None, ALU.mult).then_inc(n["s_half"], 1)
            v.tensor_scalar(sdt[:, :], sdt[:, :], 0.25, None, ALU.mult).then_inc(n["s_half"], 1)
            v.wait_ge(n["s_c"], 3)

            def stats(src, dst6, dst2, nj, done6, done2, g):
                for j in range(nj):
                    last = v.bn_stats(dst6[:, j, :], src[:, j, :])
                last.then_inc(n[done6], 1)
                v.wait_ge(n[done6], g + 1)
                v.nop(nofuse=True)
                for j in range(nj):
                    last = v.bn_aggr(dst2[:, j, :], dst6[:, j, :])
                last.then_inc(n[done2], 1)
                v.wait_ge(n[done2], g + 1)

            def quant(g, slot, rnd):
                v.wait_ge(h1_in[slot], 32 * (rnd + 1))
                stats(h1s[:, slot, :, :], bstb, mvb, 4, "bnb", "mvb_r", g)
                rsqrt(v, mvb[:, :, 1], LN_EPS, ra[:, :], xea[:, :], hfa[:, :], n["rsa"], RSQRT_STEPS * g)
                for j in range(4):
                    last = v.tensor_scalar(xq[:, j, :], h1s[:, slot, j, :], mvb[:, j, 0:1], ra[:, j:j + 1],
                                           ALU.subtract, ALU.mult)
                last.then_inc(n["xq_r"], 1)
                v.wait_ge(n["xq_r"], g + 1)
                v.tensor_scalar(xq[:, :, :], xq[:, :, :], fscale[:, 0:1], FP8_MAX, ALU.mult, ALU.min).then_inc(n["q_r"], 1)
                v.wait_ge(n["q_r"], 4 * g + 1)
                v.tensor_scalar(qmag[:, :, :].bitcast(I32), xq[:, :, :].bitcast(I32), 0x7F800000, None,
                                ALU.bitwise_and).then_inc(n["q_r"], 1)
                v.wait_ge(n["q_r"], 4 * g + 2)
                v.tensor_scalar(qmag[:, :, :], qmag[:, :, :], MINEXP, ROUND, ALU.max, ALU.mult).then_inc(n["q_r"], 1)
                v.wait_ge(n["q_r"], 4 * g + 3)
                v.scalar_tensor_tensor(xq[:, :, :], xq[:, :, :], -FP8_MAX, qmag[:, :, :], ALU.max, ALU.add)\
                    .then_inc(n["q_r"], 1)
                v.wait_ge(n["q_r"], 4 * g + 4)
                after(v, n["qt_done"], g)
                v.tensor_tensor(xqb[:, :, :], xq[:, :, :], qmag[:, :, :], ALU.subtract).then_inc(n["xqb_r"], 1)

            def ffn_out(g, slot, rnd):
                v.wait_ge(n["ffn_done"], g + 1)
                v.scalar_tensor_tensor(h2[:, slot, :, :], bank[1][:, :].rearrange("p (j d) -> p j d", j=4),
                                       fscale[:, 1:2], h1s[:, slot, :, :], ALU.mult, ALU.add).then_inc(n["h2_r"], 1)
                v.wait_ge(n["h2_r"], g + 1)
                stats(h2[:, slot, :, :], bstc, mvc, 4, "bnc", "mvc_r", g)
                rsqrt(v, mvc[:, :, 1], LN_EPS, rb[:, :], xeb[:, :], hfb[:, :], n["rsb"], RSQRT_STEPS * g)
                after(v, n["pv_done"], g - 1)
                for j in range(4):
                    last = v.tensor_scalar(xn[:, slot, j, 0:D], h2[:, slot, j, :], mvc[:, j, 0:1], rb[:, j:j + 1],
                                           ALU.subtract, ALU.mult)
                last.then_inc(n["xn_r"], 1)

            def attn_out(g, slot, rnd):
                v.wait_ge(n["pv_done"], g + 1)
                if not isinstance(g, int) or g >= 2:
                    v.wait_ge(h3_out[slot], 32 * rnd)
                for h, m in enumerate(HALF):
                    den_ = pP[0:m, :].rearrange("p (i h w) -> p i h w", i=2, h=2)[:, :, h, D]
                    last = v.reciprocal(rzb[0:m, h:4:2], den_)
                last.then_inc(n["rzb_r"], 1)
                v.wait_ge(n["rzb_r"], g + 1)
                for i in range(2):
                    for h, m in enumerate(HALF):
                        j = 2 * i + h
                        last = v.scalar_tensor_tensor(h3[0:m, slot, j, :], pP[0:m, 512 * i + 256 * h:512 * i + 256 * h + D],
                                                      rzb[0:m, j:j + 1], h2[0:m, slot, j, :], ALU.mult, ALU.add)
                last.then_inc(n["h3_r"], 1)

            pipeline(v, 0, NB, [(0, quant), (0, ffn_out), (1, attn_out)])

            def norm(g, slot, rnd):
                nj = tiles_of(g)
                v.wait_ge(h3_in[slot], 16 * (rnd + 1))
                stats(h3s[:, slot, :, :], bstd, mvd, nj, "bnd", "mvd_r", g)
                rsqrt(v, mvd[:, 0:nj, 1], LN_EPS, rc[:, 0:nj], xec[:, 0:nj], hfc[:, 0:nj], n["rsc"], RSQRT_STEPS * g)
                scattered(g, slot, rnd)
                for j in range(nj):
                    last = v.tensor_scalar(xr[:, slot, j, 0:D], h3s[:, slot, j, :], mvd[:, j, 0:1], rc[:, j:j + 1],
                                           ALU.subtract, ALU.mult)
                last.then_inc(n["x4_r"], 1)

            def scattered(g, slot, rnd):
                if not isinstance(g, int) or g >= 2:
                    v.wait_ge(scat[slot], 16 * TOPK * TG * rnd)

            def choose(g, slot, rnd):
                nj = tiles_of(g)
                v.wait_ge(n["lo_done"], g + 1)
                after(v, n["ex_r"], g)
                v.tensor_copy(lo[:, 0:nj, 0:NE], bank[1][:, 0:nj * NE].rearrange("p (j e) -> p j e", j=nj))\
                    .then_inc(n["lo_r"], 1)
                v.wait_ge(n["lo_r"], g + 1)
                v.nop(nofuse=True)
                for j in range(nj):
                    last = v.max(t8[:, j, :], lo[:, j, :])
                last.then_inc(n["top_r"], 1)
                v.wait_ge(n["top_r"], g + 1)
                v.tensor_scalar(xr[:, slot, 0:nj, D], t8[:, 0:nj, 2], -1.0, None, ALU.mult).then_inc(n["nl_r"], 1)
                for j in range(nj):
                    last = v.match_replace(lr[:, j, :], t8[:, j, :], lo[:, j, :], -BIG)
                last.then_inc(n["rep_r"], 1)
                v.wait_ge(n["rep_r"], g + 1)
                v.tensor_scalar(mask[:, 0:nj, :], lr[:, 0:nj, 0:NE], -BIG / 2, None, ALU.is_le).then_inc(n["mask_r"], 1)

            def silu(g, slot, rnd):
                nj = tiles_of(g)
                gu = wide[1][:, 0:nj * 256].rearrange("p (j f) -> p j f", j=nj)
                v.wait_ge(n["th_r"], g + 1)
                v.scalar_tensor_tensor(sa[:, 0:nj, :], th[:, 0:nj, :], 1.0, gu[:, :, 0:2 * F], ALU.add, ALU.mult)\
                    .then_inc(n["sa_r"], 1)
                v.wait_ge(n["sa_r"], g + 1)
                after(v, n["hst_done"], g)
                v.tensor_tensor(hs[:, 0:nj, :], sa[:, 0:nj, :], gu[:, :, 2 * F:4 * F], ALU.mult).then_inc(n["hs_r"], 1)

            def place(g, slot, rnd):
                nj = tiles_of(g)
                v.wait_ge(n["cum_done"], g + 1)
                after(v, n["taken_r"], g)
                v.tensor_tensor(slotm[:, 0:nj, :], bank[1][:, 256:256 + nj * NE].rearrange("p (j e) -> p j e", j=nj),
                                taken[:, :].unsqueeze(1).to_broadcast([128, nj, NE]), ALU.add).then_inc(n["slot_r"], 1)
                v.wait_ge(n["slot_r"], g + 1)
                v.tensor_tensor(taken[:, :], taken[:, :], bank[1][:, 0:NE], ALU.add).then_inc(n["taken_r"], 1)
                v.scalar_tensor_tensor(valid[:, 0:nj, :], slotm[:, 0:nj, :], float(CAP), mask[:, 0:nj, :],
                                       ALU.is_lt, ALU.mult).then_inc(n["valid_r"], 1)
                if not isinstance(g, int) or g >= 2:
                    v.wait_ge(dest_out[slot], 16 * rnd)
                v.tensor_tensor(dest[:, slot, 0:nj, :], slotm[:, 0:nj, :],
                                first1[:, :].unsqueeze(1).to_broadcast([128, nj, NE]), ALU.add).then_inc(n["dest0_r"], 1)
                v.wait_ge(n["dest0_r"], g + 1)
                v.wait_ge(n["valid_r"], g + 1)
                v.tensor_tensor(dest[:, slot, 0:nj, :], dest[:, slot, 0:nj, :], valid[:, 0:nj, :], ALU.mult).then_inc(n["dest_r"], 1)
                v.wait_ge(n["dest_r"], g + 1)
                v.nop(nofuse=True)
                for j in range(nj):
                    last = v.max(dk[:, j, :], dest[:, slot, j, :])
                last.then_inc(n["dk_r"], 1)
                v.wait_ge(n["dk_r"], g + 1)
                v.tensor_scalar(zk[:, 0:nj, :], dk[:, 0:nj, 0:TOPK], 0.0, float(ZR + 1), ALU.is_equal, ALU.mult)\
                    .then_inc(n["zk_r"], 1)
                v.wait_ge(n["zk_r"], g + 1)
                v.scalar_tensor_tensor(idxs[:, slot, 0:nj, :], dk[:, 0:nj, 0:TOPK], -1.0, zk[:, 0:nj, :],
                                       ALU.add, ALU.add).then_inc(n["idx_r"], 1)

            def denominator(g, slot, rnd):
                nj = tiles_of(g)
                v.wait_ge(n["ex_r"], g + 1)
                v.tensor_tensor(lr[:, 0:nj, 0:NE], ex[:, 0:nj, :], mask[:, 0:nj, :], ALU.mult).then_inc(n["em_r"], 1)
                v.wait_ge(n["em_r"], g + 1)
                v.tensor_reduce(s6[:, 0:nj], lr[:, 0:nj, 0:NE], AX.X, ALU.add).then_inc(n["s6_r"], 1)
                v.wait_ge(n["s6_r"], g + 1)
                v.scalar_tensor_tensor(den[:, 0:nj], zz[:, 0:nj], 1e-9, s6[:, 0:nj], ALU.mult, ALU.add)\
                    .then_inc(n["den_r"], 1)
                v.wait_ge(n["den_r"], g + 1)
                v.reciprocal(xr[:, slot, 0:nj, D + 1], den[:, 0:nj]).then_inc(n["row_r"], 1)

            def shared_out(g, slot, rnd):
                nj = tiles_of(g)
                v.wait_ge(n["sh_done"], g + 1)
                if not isinstance(g, int) or g >= 2:
                    v.wait_ge(h4_out[slot], 16 * rnd)
                v.tensor_tensor(h4[:, slot, 0:nj, :], bank[0][:, 0:nj * D].rearrange("p (j d) -> p j d", j=nj),
                                h3s[:, slot, 0:nj, :], ALU.add).then_inc(n["h4_r"], 1)

            def link_to(name):
                count = [0]

                def link(ins):
                    count[0] += 1
                    ins.then_inc(n[name], 1)
                    v.wait_ge(n[name], count[0])
                return link

            link = link_to("s_c2")
            C = NE
            link(v.tensor_copy(col[:, 12:13], eiota[:, 0:1]))
            link(v.tensor_scalar(col[0:C, 5:6], col[0:C, 12:13], float(CR), None, ALU.mult))
            link(v.memset(col[C:C + 1, 12:13], 0.0))
            link(v.memset(col[C:C + 1, 2:3], 128.0 * 16384))

            def offsets(k):
                link(v.tensor_tensor(col[0:C, 10:11], col[0:C, 5:6], col[0:C, 6:7], ALU.subtract))
                link(v.tensor_scalar(col[0:C, 10:11], col[0:C, 10:11], 1.0, None, ALU.add))
                v.tensor_scalar(diag[:, :], ident[0:C, 0:C], col[0:C, 10:11], None, ALU.mult).then_inc(n["tab_v"], 1)

            offsets(0)
            v.wait_ge(n["tab_p"], 1)
            link(v.tensor_copy(first1[:, :], bank[1][:, 0:NE]))

            def tables(k):
                link(v.tensor_copy(it[:, :], iiota[:, :]))
                v.wait_ge(n["taken_r"], GR)
                v.nop(nofuse=True).then_inc(n["tab_v"], 1)
                v.wait_ge(n["tab_p"], 2)
                link(v.tensor_scalar(col[0:C, 7:8], bank[1][0:C, 0:1], float(CAP), None, ALU.min))
                link(v.tensor_tensor(col[0:C, 1:2], col[0:C, 7:8], col[0:C, 6:7], ALU.subtract))
                link(v.tensor_scalar(coli[:, 0:1], col[0:C, 1:2], 127.0, None, ALU.add))
                link(v.tensor_scalar(coli[:, 1:2], coli[:, 0:1], 7, None, ALU.logical_shift_right))
                v.tensor_scalar(col[0:C, 2:3], coli[:, 1:2], 128.0, None, ALU.mult).then_inc(n["tab_v"], 1)
                v.wait_ge(n["tab_v"], 3)
                v.wait_ge(n["tab_p"], 3)
                link(v.tensor_copy(col[:, 4:5], bank[1][0:C + 1, 128:129]))
                link(v.tensor_tensor(col[:, 3:4], col[:, 4:5], col[:, 2:3], ALU.add))
                link(v.tensor_tensor(col[0:C, 8:9], col[0:C, 5:6], col[0:C, 4:5], ALU.subtract))
                link(v.tensor_scalar(diag[:, :], ident[0:C, 0:C], col[0:C, 8:9], -1.0, ALU.mult, ALU.mult))
                link(v.memset(col[C:C + 1, 8:9], float(ZR)))
                link(v.tensor_scalar(itin[:, :], it[:, :], col[:, 4:5], None, ALU.is_ge))
                link(v.scalar_tensor_tensor(oh[:, :], it[:, :], col[:, 3:4], itin[:, :], ALU.is_lt, ALU.mult))
                link(v.memset(it[C:C + 1, :], 0.0))
                link(v.scalar_tensor_tensor(itin[:, :], it[:, :], col[:, 8:9], oh[:, :], ALU.add, ALU.mult))
                v.tensor_scalar(oh[:, :], oh[:, :], col[:, 12:13], None, ALU.mult).then_inc(n["tab_v"], 1)
                for k, dst in enumerate((texp, tin)):
                    v.wait_ge(n["tab_p"], 4 + k)
                    for i, w in enumerate(range(0, NT, 512)):
                        m = min(512, NT - w)
                        src = (wide[1][0:1, 0:512], wide[1][0:1, 512:1024], bank[0][0:1, 0:512])[i]
                        link(v.tensor_copy(dst[:, w:w + m], src[:, 0:m]))
                    if k == 0:
                        v.nop(nofuse=True).then_inc(n["tab_v"], 2)
                link(v.tensor_tensor(col[0:C, 11:12], col[0:C, 5:6], col[0:C, 1:2], ALU.add))
                v.nop(nofuse=True).then_inc(n["tab_v"], 1)
                v.wait_ge(n["tab_p"], 7)
                link(v.tensor_copy(ttail[:, :], bank[1][0:1, 0:NE]))
                link(v.tensor_copy(shift[:, :], bank[1][:, 256:256 + NE]))
                v.wait_ge(n["s_half"], 2)
                v.nop(nofuse=True).then_inc(n["tab_ready"], 1)

            def gate_sum(q, slot, rnd):
                v.wait_ge(n["geu_done"], q + 1)
                after(v, n["yo_r"], q - ES + 1)
                v.tensor_tensor(gate[:, slot, :], eT_[slot % 2][:, 0:TG], xin[:, slot, :, D], ALU.add)\
                    .then_inc(n["g1_r"], 1)

            def act_e(q, slot, rnd):
                gu = eG[slot % 2][:, :].rearrange("p (j f) -> p j f", j=TG)
                v.wait_ge(n["the_r"], q + 1)
                after(v, n["hh_r"], q)
                v.scalar_tensor_tensor(ae[:, :, :], the[:, :, :], 1.0, gu[:, :, 0:F], ALU.add, ALU.mult)\
                    .then_inc(n["ae_r"], 1)
                v.wait_ge(n["ae_r"], q + 1)
                after(v, n["ht_done"], q - 1)
                v.tensor_tensor(hh[:, slot % 2, :, :], ae[:, :, :], gu[:, :, F:2 * F], ALU.mult).then_inc(n["hh_r"], 1)
                v.wait_ge(n["gx_r"], q + 1)
                v.tensor_tensor(gate[:, slot, :], gate[:, slot, :], xin[:, slot, :, D + 1], ALU.mult)\
                    .then_inc(n["gate_r"], 1)

            def copy_hT(q, slot, rnd):
                v.wait_ge(n["ht_done"], q + 1)
                after(v, n["dn_done"], q - 1)
                v.tensor_copy(hT[:, slot % 2, :, :].rearrange("p j d -> p (j d)"), eH[slot % 2][0:F, :])\
                    .then_inc(n["hT_r"], 1)

            for k, (a, b) in enumerate(group_steps()):
                pipeline(v, a, b, [(0, norm), (0, choose), (0, silu), (0, place), (0, denominator), (0, shared_out)])
                tables(k)
                pipeline(v, 0, NQ, [(1, gate_sum), (1, act_e), (2, copy_hT)], ES)

            def indices(g, slot, rnd):
                nj = tiles_of(g)
                v.wait_ge(dest_in[slot], 16 * (rnd + 1))
                v.tensor_tensor(drow[:, 0:nj, :], dests[:, slot, 0:nj, :],
                                shift[:, :].unsqueeze(1).to_broadcast([128, nj, NE]), ALU.add).then_inc(n["sh0_r"], 1)
                v.wait_ge(n["sh0_r"], g + 1)
                v.scalar_tensor_tensor(drow[:, 0:nj, :], dests[:, slot, 0:nj, :], 0.0, drow[:, 0:nj, :],
                                       ALU.is_gt, ALU.mult).then_inc(n["sh1_r"], 1)
                v.wait_ge(n["sh1_r"], g + 1)
                v.nop(nofuse=True)
                for j in range(nj):
                    last = v.max(dg[:, j, :], drow[:, j, :])
                last.then_inc(n["dg_r"], 1)
                v.wait_ge(n["dg_r"], g + 1)
                v.tensor_scalar(zg[:, 0:nj, :], dg[:, 0:nj, 0:TOPK], 0.0, float(YZ + 1), ALU.is_equal, ALU.mult)\
                    .then_inc(n["zg_r"], 1)
                v.wait_ge(n["zg_r"], g + 1)
                if not isinstance(g, int) or g >= 2:
                    v.wait_ge(gath[slot], 16 * TOPK * TG * rnd)
                v.scalar_tensor_tensor(idxg[:, slot, 0:nj, :], dg[:, 0:nj, 0:TOPK], -1.0, zg[:, 0:nj, :],
                                       ALU.add, ALU.add).then_inc(n["idxg_r"], 1)

            def add_up(g, slot, rnd):
                nj = tiles_of(g)
                v.wait_ge(n["sum_done"], g + 1)
                v.wait_ge(h4_in[slot], 16 * (rnd + 1))
                if not isinstance(g, int) or g >= 2:
                    v.wait_ge(ot_out[slot], 16 * rnd)
                v.tensor_tensor(ot[:, slot, 0:nj, :], bank[slot][:, 0:nj * D].rearrange("p (j d) -> p j d", j=nj),
                                h4s[:, slot, 0:nj, :], ALU.add).then_inc(n["ot_r"], 1)

            pipeline(v, 0, GR, [(0, indices), (1, add_up)])


def lay_out(a):
    import numpy as np
    x = np.ascontiguousarray(a["x"])
    padded = np.zeros((B, CH, S + 2 * HP, S + 2 * HP), x.dtype)
    padded[:, :, HP:HP + S, HP:HP + S] = x
    own = x.reshape(B, CH, NI, PATCH, NI, PATCH).transpose(2, 4, 1, 3, 5, 0).reshape(NI, NI, K, B)
    off = padded.reshape(B, CH, NI + 1, PATCH, NI + 1, PATCH).transpose(2, 4, 1, 3, 5, 0).reshape(NI + 1, NI + 1, K, B)
    col = np.stack([own, off[1:, :NI], off[1:, 1:], off[:NI, :NI], off[:NI, 1:]], axis=2)
    col = col.reshape(T, NCTX, K, B).transpose(2, 0, 1, 3)

    def by_position(m):
        m = np.asarray(m).reshape(NCTX, CH, NI, PATCH, NI, PATCH)
        return m.transpose(1, 3, 5, 2, 4, 0).reshape(K, T, NCTX)

    wg, wu = np.asarray(a["L1_ffn_w_gate"]), np.asarray(a["L1_ffn_w_up"])
    sg, su = np.asarray(a["L1_ffn_shared_w_gate"]), np.asarray(a["L1_ffn_shared_w_up"])
    sd = np.asarray(a["L1_ffn_shared_w_down"])
    return {
        "ximg": x.reshape(B, CH * S * S),
        "xcol": col,
        "w5": np.asarray(a["L0_tok_W"]).reshape(D, NCTX, K).transpose(2, 1, 0),
        "gam": by_position(a["L0_tok_gamma"]),
        "bet": by_position(a["L0_tok_beta"]),
        "tokb": np.asarray(a["L0_tok_b"]).reshape(1, D),
        "post": np.asarray(a["L0_attn_positions"]).T,
        "scales": np.asarray(a["L0_attn_scales"]),
        "valt": np.asarray(a["L0_attn_values"]).T,
        "wot": np.asarray(a["L0_attn_W_out"]).T,
        "bout": np.asarray(a["L0_attn_b_out"]).reshape(1, D),
        "wffn": np.asarray(a["L0_ffn_weight"]),
        "rwt": np.asarray(a["L1_ffn_router_w"]).T,
        "rbias": np.asarray(a["L1_ffn_bias"]).reshape(1, NE),
        "sgu": np.concatenate([sg.reshape(2 * F, D), su.reshape(2 * F, D)]).T,
        "sdt": sd.transpose(0, 2, 1).reshape(2 * F, D),
        "wgu": np.concatenate([wg, wu], axis=1).transpose(2, 0, 1),
        "wdt": np.asarray(a["L1_ffn_w_down"]).transpose(2, 0, 1),
    }


def kernel(**inputs):
    import numpy as _np
    import concourse.bacc as _bacc
    from concourse.bass_utils import run_bass_kernel_spmd as _run

    nc = _bacc.Bacc("TRN2", target_bir_lowering=False, num_devices=1)
    arrays, io = {}, {}
    for name, a in lay_out(inputs).items():
        arrays[f"in_{name}"] = _np.ascontiguousarray(a)
        io[name] = nc.dram_tensor(f"in_{name}", arrays[f"in_{name}"].shape, F32, kind="ExternalInput").ap()
    io["out"] = nc.dram_tensor("out_tokens", (B, T, D), F32, kind="ExternalOutput").ap()
    build(nc, io)
    r = _run(nc, [arrays], core_ids=[0])
    return r.results[0]["out_tokens"]
```

```python
from contextlib import ExitStack

import concourse.bass as bass
from concourse import mybir

ALU = mybir.AluOpType
ACT = mybir.ActivationFunctionType
AX = mybir.AxisListType
F32 = mybir.dt.float32
BF16 = mybir.dt.bfloat16
I32 = mybir.dt.int32
RMAX = bass.bass_isa.ReduceOp.max

B, CH, S, PATCH, HP = 128, 2, 104, 8, 4
NI = S // PATCH
T = NI * NI
D = 128
NCTX = 5
K = CH * PATCH * PATCH
N = B * T
TG = 4
GA = -(-T // TG)
NN = 256
LN_EPS, TOK_EPS = 1e-5, 1e-7
FP8_MAX = 448.0
NPIX = float(2 * NCTX * S * S)
NPAD = NPIX - 2.0 * (S * S + 4 * (S - HP) ** 2)
ROUND = 1.5 * 2.0 ** 20
MINEXP = 2.0 ** -6
SCALE = 1.0 / 512.0 ** 0.5
NE, F, TOPK = 64, 64, 6
CAP = int(N * TOPK * 2.0 / NE)
NGRP = 2
CR = -(-CAP // 128) * 128 + 256 * NGRP
ZR = NE * CR
XW = D + 2
BIG = 1e30
HALF = (128, T - 128)


GSTEPS = ((0, 26), (26, GA))


def group_tiles(a, b):
    tiles = min(b * TG, T) - a * TG
    return -(-(tiles * TOPK + NE) // TG) * TG


GT = [group_tiles(a, b) for a, b in GSTEPS]
T0 = (0, GT[0])
NT = sum(GT)
YZ = [128 * t for t in GT]


def after(eng, sem, value):
    if not isinstance(value, int) or value > 0:
        eng.wait_ge(sem, value)


def stretch(eng, begin, end, lo, hi, period, do):
    a, b = max(begin, lo), min(end, hi)
    a, b = a + -a % period, b - b % period
    if b - a < 2 * period:
        a = b = end
    for s in range(begin, a):
        do(s // period, s % period)
    if b > a:
        with eng.Fori(a // period, b // period) as i:
            for u in range(period):
                do(i, u)
    for s in range(b, end):
        do(s // period, s % period)


def do_parts(parts, first, stop, slots, period, i, u):
    for lag, fn in parts:
        g = period * i + (u - lag)
        if not isinstance(g, int) or first <= g < stop:
            fn(g, (u - lag) % slots, (period // slots) * i + (u - lag) // slots)


def pipeline(eng, first, stop, parts, slots=2, begin=None, end=None):
    longest = max(lag for lag, _ in parts)
    begin = first if begin is None else begin
    end = stop + longest if end is None else end
    stretch(eng, begin, end, first + longest + slots, stop - 1, slots,
            lambda i, u: do_parts(parts, first, stop, slots, slots, i, u))


EVERY = 4


def weave(eng, begin, end, stop, parts, slots, start, sums, sums_stop):
    period = 2 * EVERY
    longest = max(lag for lag, _ in parts)

    def do(i, u):
        s = period * i + u
        if (u - start) % EVERY == 0:
            c = (u - start) // EVERY
            if not isinstance(s, int) or start <= s < start + EVERY * sums_stop:
                do_parts(sums, 0, GSTEPS[0][1], 2, 2, i, c)
        do_parts(parts, 0, stop, slots, period, i, u)

    stretch(eng, begin, end, start + EVERY * (max(lag for lag, _ in sums) + 2),
            min(stop - 1, start + EVERY * min(sums_stop, GSTEPS[0][1])), period, do)


def place_of(r, late):
    return late + 3 * (r // 2) + 2 * (r % 2)


def braid(eng, begin, end, late, parts, r_first, r_stop):
    nb, period = B // 2, 6

    def do(i, u):
        third, m = (u - late) % 3, (u - late) // 3
        c = 2 * m + (third == 2)
        for kind, lag, fn in parts:
            if kind == 'b':
                g = period * i + (u - lag)
                if not isinstance(g, int) or 0 <= g < nb + (lag == 0 and fn.__name__ == "roots"):
                    fn(g, (u - lag) % 2, 3 * i + (u - lag) // 2)
            elif third != 1:
                g = 4 * i + (c - lag)
                if not isinstance(g, int) or r_first <= g < r_stop:
                    fn(g, (c - lag) % 4, i + (c - lag) // 4)

    longest = max([lag for kind, lag, fn in parts if kind == 'r'])
    stretch(eng, begin, end, place_of(max(r_first + longest, 4 + longest), late), min(nb, place_of(r_stop, late)),
            period, do)


def halves(fn):
    return lambda g, slot, rnd: fn(g, slot % 2, 2 * rnd + slot // 2)


def tiles_of(g, total=T):
    return min(TG, total - TG * g) if isinstance(g, int) else TG


def build(nc, io):
    def dram(name, shape):
        return nc.dram_tensor(name, shape, F32, kind="Internal").ap()

    h1d = dram("h1d", (B, T, D))
    h3d = dram("h3d", (N, D))
    h4d = dram("h4d", (N, D))
    gbd = dram("gbd", (2, T * D))
    xed = dram("xed", (ZR + 128, XW))
    yed = [dram(f"yed{k}", (YZ[k] + 128, D)) for k in range(NGRP)]
    destd = dram("destd", (T, 128, NE))
    out = io["out"].rearrange("b t d -> (b t) d")

    with ExitStack() as ctx:
        def sb(name, shape, dt=F32, c=ctx):
            return c.enter_context(nc.sbuf_tensor(name, shape, dt))

        def sem(name):
            return ctx.enter_context(nc.semaphore(name))

        bank = [ctx.enter_context(nc.psum_tensor(f"bank{i}", [128, 512], F32)) for i in range(4)]
        wide = [ctx.enter_context(nc.psum_tensor(f"wide{i}", [128, 1024], F32)) for i in range(2)]

        ident = sb("ident", [128, 128])
        identb = sb("identb", [128, 128], BF16)
        ones = sb("ones", [128, 128])
        onesb = sb("onesb", [128, 128], BF16)
        before = sb("before", [128, 128])
        beforeb = sb("beforeb", [128, 128], BF16)
        eps_ln = sb("eps_ln", [128, 1])
        tenth = sb("tenth", [128, 1])
        wq = sb("wq", [128, 128], BF16)
        fscale = sb("fscale", [128, 4])

        front(nc, io, sb, bank, wide, dict(
            ident=ident, identb=identb, ones=ones, onesb=onesb, before=before, beforeb=beforeb,
            eps_ln=eps_ln, tenth=tenth, wq=wq, fscale=fscale), h1d, gbd)
        back(nc, io, sb, sem, bank, wide, dict(
            ident=ident, identb=identb, ones=ones, onesb=onesb, before=before, beforeb=beforeb,
            wq=wq, fscale=fscale, eps_ln=eps_ln), h1d, h3d, h4d, xed, yed, destd, out)


def front(nc, io, sb0, bank, wide, c, h1d, gbd):
    used = []

    def sem(name):
        used.append(nc.alloc_semaphore(name=name))
        return used[-1]

    with ExitStack() as ctx:
        def sb(name, shape, dt=F32):
            return sb0(name, shape, dt, ctx)

        ident, ones, onesb = c["ident"], c["ones"], c["onesb"]
        H = sb("H", [128, T * D])
        img = H[:, 0:CH * S * S].rearrange("p (c r w) -> p c r w", c=CH, r=S)
        tok = H[:, :].rearrange("p (t d) -> p t d", d=D)
        w5 = sb("w5", [128, NCTX, D])
        gam = sb("gam", [128, T, NCTX])
        bet = sb("bet", [128, T, NCTX])
        tokb = sb("tokb", [1, D])
        post = sb("post", [128, NN])
        possq = sb("possq", [128, NN])
        psqr = sb("psqr", [1, NN])
        psq_parts = sb("psq_parts", [1, 3, NN], BF16)
        psq3 = sb("psq3", [3, NN], BF16)
        valt = sb("valt", [128, NN])
        wot = sb("wot", [128, D])
        bout = sb("bout", [1, D])
        v2 = sb("v2", [128, 2, D])
        scb = sb("scb", [128, NN])
        wffn = sb("wffn", [128, D])
        part = sb("part", [128, 64])
        mstd = sb("mstd", [128, 2])
        rstd = sb("rstd", [128, 1])
        mstdT = sb("mstdT", [2, 128])
        eps_tok = sb("eps_tok", [128, 1])
        gbs = sb("gbs", [128, 4, D])

        xs = sb("xs", [128, 2, TG, NCTX, 128])
        weff = sb("weff", [128, 2, TG, NCTX, 128])
        gbx = sb("gbx", [2, 2, TG * D])
        bst = sb("bst", [128, TG, 6])
        mv = sb("mv", [128, 2, TG, 2])
        std = sb("std", [128, 2, TG])
        rs0 = sb("rs0", [128, 2, TG])
        vr = sb("vr", [128, TG])
        xsq = sb("xsq", [128, 2, TG])
        xh = sb("xh", [128, 2, TG, D])
        xT = sb("xT", [128, TG, D])
        d2 = sb("d2", [128, TG, NN])
        lnr = sb("lnr", [128, TG, NN])
        rr = sb("rr", [128, TG, NN])
        lg = sb("lg", [128, 2, TG, NN])
        mn = sb("mn", [128, 2, TG])
        zz = sb("zz", [128, 2, TG])
        rz = sb("rz", [128, TG])
        eT = sb("eT", [128, TG * 2, 128])
        bst1 = sb("bst1", [128, TG, 6])
        mvs = sb("mvs", [128, TG, 2])
        mv1 = sb("mv1", [128, T, 2])
        hmax = sb("hmax", [128, T])
        hmin = sb("hmin", [128, T])
        hstd = sb("hstd", [128, T])
        am = sb("am", [128, 8])
        am2 = sb("am2", [128, 2])
        qtmp = sb("qtmp", [128, D])
        qm = sb("qm", [128, D])

        s_img = [sem(f"s_img{i}") for i in range(4)]
        s_w = sem("s_w")
        s_const = sem("s_const")
        s_fix = sem("s_fix")
        s_vc = sem("s_vc")
        s_sq = sem("s_sq")
        s_var = sem("s_var")
        s_mstd = sem("s_mstd")
        s_mT = sem("s_mT")
        s_gb = sem("s_gb")
        s_gbs = sem("s_gbs")
        s_gbo = sem("s_gbo")
        s_psq = sem("s_psq")
        s_psp = sem("s_psp")
        s_ps3 = sem("s_ps3")
        s_v2 = sem("s_v2")

        with nc.Block() as block:
            @block.sync
            def _(sp):
                for i in range(4):
                    w = CH * S * S // 4
                    sp.dma_start(H[:, i * w:(i + 1) * w], io["ximg"][:, i * w:(i + 1) * w]).then_inc(s_img[i], 16)
                for dst, src in ((w5, "w5"), (gam, "gam"), (bet, "bet")):
                    sp.dma_start(dst[:, :, :], io[src]).then_inc(s_w, 16)
                for dst, src in ((tokb, "tokb"), (post, "post"), (valt, "valt"), (wot, "wot"),
                                 (bout, "bout"), (wffn, "wffn")):
                    sp.dma_start(dst[:, :], io[src]).then_inc(s_w, 16)
                sp.dma_start(scb[:, :], io["scales"].partition_broadcast(128)).then_inc(s_w, 16)
                sp.wait_ge(s_gbs, 1)
                for q in range(2):
                    sp.dma_start(gbd[q, 0:128 * D].rearrange("(p d) -> p d", d=D), gbs[:, q, :]).then_inc(s_gbo, 16)
                    sp.dma_start(gbd[q, 128 * D:T * D].rearrange("(p d) -> p d", d=D),
                                 gbs[0:T - 128, 2 + q, :]).then_inc(s_gbo, 16)
                sp.wait_ge(s_psp, 3)
                for k in range(3):
                    sp.dma_start(psq3[k:k + 1, :], psq_parts[:, k, :]).then_inc(s_ps3, 16)
                sp.wait_ge(s_gbo, 64)
                sp.wait_ge(s_ps3, 48)

            @block.gpsimd
            def _(g):
                g.memset(c["ident"][:, :], 0.0).then_inc(s_const, 1)
                g.memset(c["before"][:, :], 0.0).then_inc(s_const, 1)
                g.memset(c["ones"][:, :], 1.0).then_inc(s_const, 1)
                g.memset(c["onesb"][:, :], 1.0).then_inc(s_const, 1)
                g.memset(c["eps_ln"][:, :], LN_EPS).then_inc(s_const, 1)
                g.memset(c["tenth"][:, :], 0.1).then_inc(s_const, 1)
                g.memset(eps_tok[:, :], TOK_EPS).then_inc(s_const, 1)
                g.wait_ge(s_const, 7)
                g.affine_select(out=ident[:, :], in_=ident[:, :], compare_op=ALU.not_equal, fill=1.0, base=0,
                                pattern=[[-1, 128]], channel_multiplier=1).then_inc(s_fix, 1)
                g.affine_select(out=c["before"][:, :], in_=c["before"][:, :], compare_op=ALU.is_ge, fill=1.0,
                                base=0, pattern=[[-1, 128]], channel_multiplier=1).then_inc(s_fix, 1)
                g.wait_ge(s_fix, 2)
                g.tensor_copy(c["identb"][:, :], ident[:, :]).then_inc(s_fix, 1)
                g.tensor_copy(c["beforeb"][:, :], c["before"][:, :]).then_inc(s_fix, 1)
                g.wait_ge(s_fix, 4)

            def edges(v, sign, dst, link):
                at = dst
                for w0 in (0, S - HP):
                    link(v.tensor_reduce(part[:, at:at + 1], img[:, :, :, w0:w0 + HP], AX.XYZ, ALU.add))
                    at += 1
                for r0 in (0, S - HP):
                    link(v.tensor_reduce(part[:, at:at + 1], img[:, :, r0:r0 + HP, :], AX.XYZ, ALU.add))
                    at += 1
                for w0 in (0, S - HP):
                    for r0 in (0, S - HP):
                        link(v.tensor_reduce(part[:, at:at + 1], img[:, :, r0:r0 + HP, w0:w0 + HP], AX.XYZ, ALU.add))
                        at += 1

            def weigh(v, link, base, dst):
                link(v.tensor_reduce(part[:, 30:31], part[:, base:base + 4], AX.X, ALU.add))
                link(v.tensor_reduce(part[:, 31:32], part[:, base + 4:base + 8], AX.X, ALU.add))
                link(v.tensor_reduce(part[:, 32:33], part[:, base + 8:base + 12], AX.X, ALU.add))
                link(v.scalar_tensor_tensor(part[:, 33:34], part[:, 30:31], 5.0, part[:, 32:33], ALU.mult, ALU.add))
                link(v.scalar_tensor_tensor(dst, part[:, 31:32], -2.0, part[:, 33:34], ALU.mult, ALU.add))

            @block.vector
            def _(v):
                count = [0]

                def link(ins):
                    count[0] += 1
                    ins.then_inc(s_vc, 1)
                    v.wait_ge(s_vc, count[0])

                w = CH * S * S // 4
                for i in range(4):
                    v.wait_ge(s_img[i], 16)
                    link(v.tensor_reduce(part[:, i:i + 1], H[:, i * w:(i + 1) * w], AX.X, ALU.add))
                edges(v, 1, 4, link)
                weigh(v, link, 0, part[:, 40:41])
                v.tensor_scalar(mstd[:, 0:1], part[:, 40:41], -1.0 / NPIX, None, ALU.mult).then_inc(s_mstd, 1)
                v.wait_ge(s_sq, 4)
                edges(v, 1, 20, link)
                for i in range(4):
                    link(v.tensor_copy(part[:, 16 + i:17 + i], part[:, 50 + i:51 + i]))
                weigh(v, link, 16, part[:, 41:42])
                v.wait_ge(s_mstd, 1)
                link(v.tensor_tensor(part[:, 42:43], mstd[:, 0:1], mstd[:, 0:1], ALU.mult))
                link(v.scalar_tensor_tensor(part[:, 43:44], part[:, 42:43], NPAD, part[:, 41:42], ALU.mult, ALU.add))
                v.tensor_scalar(part[:, 44:45], part[:, 43:44], 1.0 / NPIX, None, ALU.mult).then_inc(s_var, 1)
                v.wait_ge(s_mstd, 2)
                v.reciprocal(rstd[:, :], mstd[:, 1:2]).then_inc(s_mstd, 1)
                v.wait_ge(s_mT, 1)
                v.tensor_copy(mstdT[:, :], bank[2][0:2, 0:128]).then_inc(s_mT, 1)
                v.wait_ge(s_w, 160)
                v.tensor_tensor(possq[:, :], post[:, :], post[:, :], ALU.mult).then_inc(s_psq, 1)
                v.wait_ge(s_psq, 1)
                v.tensor_scalar(post[:, :], post[:, :], -2.0, None, ALU.mult).then_inc(s_psq, 1)
                v.wait_ge(s_psq, 3)
                for k in range(3):
                    src = bank[3][0:1, 0:NN] if k == 0 else psqr[:, :]
                    v.tensor_copy(psq_parts[:, k, :], src).then_inc(s_psp, 1)
                    v.wait_ge(s_psp, k + 1)
                    if k < 2:
                        link(v.tensor_tensor(psqr[:, :], src, psq_parts[:, k, :], ALU.subtract))
                v.wait_ge(s_v2, 1)
                v.tensor_copy(v2[:, :, :].rearrange("p a d -> p (a d)"), bank[1][:, 0:2 * D]).then_inc(s_v2, 1)
                v.wait_ge(s_gb, 1)
                v.tensor_copy(gbs[:, 0:2, :].rearrange("p a d -> p (a d)"), bank[0][:, 0:2 * D]).then_inc(s_gb, 1)
                v.tensor_copy(gbs[0:T - 128, 2:4, :].rearrange("p a d -> p (a d)"),
                              bank[0][0:T - 128, 2 * D:4 * D]).then_inc(s_gbs, 1)
                v.wait_ge(s_gb, 2)

            @block.scalar
            def _(a):
                w = CH * S * S // 4
                a.wait_ge(s_mstd, 1)
                for i in range(4):
                    a.activation(H[:, i * w:(i + 1) * w], H[:, i * w:(i + 1) * w], ACT.Square, bias=mstd[:, 0:1],
                                 accum_out=part[:, 50 + i:51 + i]).then_inc(s_sq, 1)
                a.wait_ge(s_const, 7)
                a.wait_ge(s_var, 1)
                a.activation(mstd[:, 1:2], part[:, 44:45], ACT.Sqrt, bias=eps_tok[:, :]).then_inc(s_mstd, 1)

            @block.tensor
            def _(pe):
                pe.wait_ge(s_w, 160)
                pe.wait_ge(s_const, 7)
                pe.wait_ge(s_fix, 4)
                for half, (p0, n) in enumerate(((0, 128), (128, T - 128))):
                    for q, src in enumerate((gam, bet)):
                        dst = bank[0][0:n, (2 * half + q) * D:(2 * half + q + 1) * D]
                        for k in range(NCTX):
                            last = pe.matmul(dst, src[:, p0:p0 + n, k], w5[:, k, :], start=(k == 0),
                                             stop=(k == NCTX - 1 and q == 0))
                        if q == 1:
                            last = pe.matmul(dst, ones[0:1, 0:n], tokb[:, :], start=False, stop=True)
                last.then_inc(s_gb, 1)
                for a in range(2):
                    dst = bank[1][:, a * D:(a + 1) * D]
                    pe.matmul(dst, valt[:, a * 128:(a + 1) * 128], wot[:, :], start=True, stop=False)
                    last = pe.matmul(dst, ones[0:1, :], bout[:, :], start=False, stop=True)
                last.then_inc(s_v2, 1)
                pe.wait_ge(s_mstd, 2)
                pe.transpose(bank[2][0:2, 0:128], mstd[:, :], ident[:, :]).then_inc(s_mT, 1)
                pe.wait_ge(s_psq, 2)
                pe.matmul(bank[3][0:1, 0:NN], ones[:, 0:1], possq[:, :], start=True, stop=True).then_inc(s_psq, 1)

        xs_in = [sem(f"xs_in{i}") for i in range(2)]
        h1_out = [sem(f"h1_out{i}") for i in range(2)]
        weff_ready = sem("weff_ready")
        conv_done = sem("conv_done")
        h0_ready = sem("h0_ready")
        bn0 = sem("bn0")
        mv0 = sem("mv0")
        std0 = sem("std0")
        rs0_ready = sem("rs0_ready")
        vr_ready = sem("vr_ready")
        xsq_ready = sem("xsq_ready")
        xh_ready = sem("xh_ready")
        xt_done = sem("xt_done")
        xT_ready = sem("xT_ready")
        cross_done = sem("cross_done")
        d2_ready = sem("d2_ready")
        dist_ready = sem("dist_ready")
        ln_ready = sem("ln_ready")
        r_ready = sem("r_ready")
        t_ready = sem("t_ready")
        rs_ready = sem("rs_ready")
        lg_ready = sem("lg_ready")
        mn_ready = sem("mn_ready")
        ex_ready = sem("ex_ready")
        et_done = sem("et_done")
        eT_low = sem("eT_low")
        eT_high = sem("eT_high")
        out_done = sem("out_done")
        rz_ready = sem("rz_ready")
        h1_ready = sem("h1_ready")
        bn1 = sem("bn1")
        mvs_ready = sem("mvs_ready")
        mv1_ready = sem("mv1_ready")
        s_end = sem("s_end")
        s_std1 = sem("s_std1")
        s_am = sem("s_am")
        s_amall = sem("s_amall")

        psY = [bank[0], bank[1]]
        psT, psO = bank[2], bank[3]
        psD, psE = wide

        with nc.Block() as block:
            @block.sync
            def _(sp):
                def load(g, slot, rnd):
                    nj = tiles_of(g)
                    after(sp, conv_done, g - 1)
                    sp.dma_start(xs[:, slot, 0:nj, :, :], io["xcol"][:, bass.ds(TG * g, nj), :, :])\
                        .then_inc(xs_in[slot], 16)
                    sp.dma_start(gbx[:, slot, 0:nj * D], gbd[:, bass.ds(TG * D * g, nj * D)])\
                        .then_inc(xs_in[slot], 16)

                def store(g, slot, rnd):
                    nj = tiles_of(g)
                    sp.wait_ge(h1_ready, g + 1)
                    sp.dma_start(h1d[:, bass.ds(TG * g, nj), :], tok[:, bass.ds(TG * g, nj), :])\
                        .then_inc(h1_out[slot], 16)

                pipeline(sp, 0, GA, [(0, load), (5, store)])
                sp.wait_ge(h1_out[0], 16 * (-(-GA // 2)))
                sp.wait_ge(h1_out[1], 16 * (GA // 2))

            @block.gpsimd
            def _(p):
                def fold(g, slot, rnd):
                    nj = tiles_of(g)
                    after(p, conv_done, g - 1)
                    for j in range(nj):
                        ins = p.tensor_tensor(
                            weff[:, slot, j, :, :], w5[:, :, :],
                            gam[:, bass.ds(TG * g + j, 1), :].rearrange("p o c -> p (o c)").unsqueeze(2).to_broadcast([128, NCTX, 128]),
                            ALU.mult)
                    ins.then_inc(weff_ready, 1)

                def scale(g, slot, rnd):
                    nj = tiles_of(g)
                    p.wait_ge(r_ready, g + 1)
                    after(p, lg_ready, g)
                    p.tensor_tensor(lnr[:, 0:nj, :], rr[:, 0:nj, :],
                                    scb[:, :].unsqueeze(1).to_broadcast([128, nj, NN]), ALU.mult).then_inc(rs_ready, 1)

                pipeline(p, 0, GA, [(0, fold), (2, scale)])
                p.wait_ge(s_am, 1)
                p.partition_all_reduce(am[:, 0:2], am2[:, :], 128, RMAX).then_inc(s_amall, 1)

            @block.tensor
            def _(pe):
                def conv(g, slot, rnd):
                    pe.wait_ge(xs_in[slot], 32 * (rnd + 1))
                    pe.wait_ge(weff_ready, g + 1)
                    after(pe, h0_ready, g - 1)
                    for j in range(tiles_of(g)):
                        dst = psY[slot][:, j * D:(j + 1) * D]
                        for k in range(NCTX):
                            pe.matmul(dst, xs[:, slot, j, k, :], weff[:, slot, j, k, :], start=(k == 0), stop=False)
                        last = pe.matmul(dst, mstdT[:, :], gbx[:, slot, j * D:(j + 1) * D], start=False, stop=True)
                    last.then_inc(conv_done, 1)

                def turn(g, slot, rnd):
                    pe.wait_ge(xh_ready, g + 1)
                    after(pe, xT_ready, g)
                    for j in range(tiles_of(g)):
                        last = pe.transpose(psT[:, j * 128:(j + 1) * 128], xh[:, slot, j, :], ident[:, :])
                    last.then_inc(xt_done, 1)

                def cross(g, slot, rnd):
                    pe.wait_ge(xT_ready, g + 1)
                    after(pe, d2_ready, g)
                    for j in range(tiles_of(g)):
                        dst = psD[:, j * NN:(j + 1) * NN]
                        pe.matmul(dst, xT[:, j, :], post[:, :], start=True, stop=False)
                        last = pe.matmul(dst, onesb[0:3, :], psq3[:, :], start=False, stop=True)
                    last.then_inc(cross_done, 1)

                def turn_probs(g, slot, rnd):
                    pe.wait_ge(ex_ready, g + 1)
                    after(pe, eT_low, g)
                    after(pe, eT_high, g)
                    for j in range(tiles_of(g)):
                        for a in range(2):
                            last = pe.transpose(psE[:, (2 * j + a) * 128:(2 * j + a + 1) * 128],
                                                lg[:, slot, j, a * 128:(a + 1) * 128], ident[:, :])
                    last.then_inc(et_done, 1)

                def mix(g, slot, rnd):
                    pe.wait_ge(eT_low, g + 1)
                    pe.wait_ge(eT_high, g + 1)
                    after(pe, h1_ready, g)
                    for j in range(tiles_of(g)):
                        for a in range(2):
                            last = pe.matmul(psO[:, j * D:(j + 1) * D], eT[:, 2 * j + a, :], v2[:, a, :],
                                             start=(a == 0), stop=(a == 1))
                    last.then_inc(out_done, 1)

                pipeline(pe, 0, GA, [(2, turn), (4, turn_probs), (2, cross), (4, mix), (0, conv)])

            @block.scalar
            def _(a):
                def copy_h0(g, slot, rnd):
                    a.wait_ge(conv_done, g + 1)
                    nj = tiles_of(g)
                    a.activation(tok[:, bass.ds(TG * g, nj), :], psY[slot][:, 0:nj * D].rearrange("p (j d) -> p j d", d=D),
                                 ACT.Copy, scale=rstd[:, 0:1]).then_inc(h0_ready, 1)

                def sqrt_var(g, slot, rnd):
                    a.wait_ge(mv0, g + 1)
                    after(a, rs0_ready, g - 1)
                    nj = tiles_of(g)
                    a.activation(std[:, slot, 0:nj], mv[:, slot, 0:nj, 1], ACT.Sqrt, bias=c["eps_ln"][:, :])\
                        .then_inc(std0, 1)

                def copy_xT(g, slot, rnd):
                    a.wait_ge(xt_done, g + 1)
                    after(a, cross_done, g)
                    nj = tiles_of(g)
                    a.activation(xT[:, 0:nj, :].rearrange("p j d -> p (j d)"), psT[:, 0:nj * D], ACT.Copy).then_inc(xT_ready, 1)

                def distance(g, slot, rnd):
                    nj = tiles_of(g)
                    a.wait_ge(d2_ready, g + 1)
                    a.activation(d2[:, 0:nj, :], d2[:, 0:nj, :], ACT.Sqrt).then_inc(dist_ready, 1)

                def inverse(g, slot, rnd):
                    nj = tiles_of(g)
                    a.wait_ge(dist_ready, g + 1)
                    after(a, lg_ready, g)
                    a.activation(lnr[:, 0:nj, :], d2[:, 0:nj, :], ACT.Ln, bias=c["tenth"][:, :]).then_inc(ln_ready, 1)
                    a.wait_ge(ln_ready, g + 1)
                    a.activation(rr[:, 0:nj, :], lnr[:, 0:nj, :], ACT.Exp, scale=-1.0).then_inc(r_ready, 1)

                def probs(g, slot, rnd):
                    a.wait_ge(mn_ready, g + 1)
                    after(a, rz_ready, g - 1)
                    for j in range(tiles_of(g)):
                        last = a.activation(lg[:, slot, j, :], lg[:, slot, j, :], ACT.Exp, scale=-1.0,
                                            bias=mn[:, slot, j:j + 1], accum_out=zz[:, slot, j:j + 1])
                    last.then_inc(ex_ready, 1)

                def copy_eT(g, slot, rnd):
                    nj = tiles_of(g)
                    a.wait_ge(et_done, g + 1)
                    after(a, out_done, g)
                    n = min(nj, 2)
                    a.activation(eT[:, 0:2 * n, :].rearrange("p j d -> p (j d)"), psE[:, 0:n * 256], ACT.Copy)\
                        .then_inc(eT_low, 1)

                pipeline(a, 0, GA, [(2, copy_xT), (4, copy_eT), (3, probs), (1, sqrt_var), (2, distance), (2, inverse),
                                    (0, copy_h0)])
                a.wait_ge(mv1_ready, GA)
                a.activation(hstd[:, :], mv1[:, :, 1], ACT.Sqrt, bias=c["eps_ln"][:, :]).then_inc(s_std1, 1)

            @block.vector
            def _(v):
                def stats(src, dst6, dst2, nj, done6, done2, g):
                    for j in range(nj):
                        last = v.bn_stats(dst6[:, j, :], src(j))
                    last.then_inc(done6, 1)
                    v.wait_ge(done6, g + 1)
                    v.nop(nofuse=True)
                    for j in range(nj):
                        last = v.bn_aggr(dst2(j), dst6[:, j, :])
                    last.then_inc(done2, 1)

                def stats0(g, slot, rnd):
                    v.wait_ge(h0_ready, g + 1)
                    stats(lambda j: tok[:, bass.ds(TG * g + j, 1), :].rearrange("p o d -> p (o d)"), bst,
                          lambda j: mv[:, slot, j, :], tiles_of(g), bn0, mv0, g)

                def normalise0(g, slot, rnd):
                    nj = tiles_of(g)
                    v.wait_ge(std0, g + 1)
                    after(v, xt_done, g - 1)
                    v.reciprocal(rs0[:, slot, 0:nj], std[:, slot, 0:nj]).then_inc(rs0_ready, 1)
                    v.wait_ge(rs0_ready, g + 1)
                    for j in range(nj):
                        last = v.tensor_scalar(xh[:, slot, j, :], tok[:, bass.ds(TG * g + j, 1), :].rearrange("p o d -> p (o d)"),
                                               mv[:, slot, j, 0:1], rs0[:, slot, j:j + 1], ALU.subtract, ALU.mult)
                    last.then_inc(xh_ready, 1)
                    v.scalar_tensor_tensor(vr[:, 0:nj], mv[:, slot, 0:nj, 1], float(D), rs0[:, slot, 0:nj],
                                           ALU.mult, ALU.mult).then_inc(vr_ready, 1)
                    v.wait_ge(vr_ready, g + 1)
                    v.tensor_tensor(xsq[:, slot, 0:nj], vr[:, 0:nj], rs0[:, slot, 0:nj], ALU.mult).then_inc(xsq_ready, 1)

                def dist2(g, slot, rnd):
                    v.wait_ge(xsq_ready, g + 1)
                    v.wait_ge(cross_done, g + 1)
                    after(v, lg_ready, g)
                    for j in range(tiles_of(g)):
                        last = v.tensor_scalar(d2[:, j, :], psD[:, j * NN:(j + 1) * NN], xsq[:, slot, j:j + 1], 0.0,
                                               ALU.add, ALU.max)
                    last.then_inc(d2_ready, 1)

                def logits(g, slot, rnd):
                    nj = tiles_of(g)
                    v.wait_ge(r_ready, g + 1)
                    v.scalar_tensor_tensor(d2[:, 0:nj, :], d2[:, 0:nj, :], 0.1, rr[:, 0:nj, :], ALU.add, ALU.mult)\
                        .then_inc(t_ready, 1)
                    v.wait_ge(t_ready, g + 1)
                    v.wait_ge(rs_ready, g + 1)
                    after(v, et_done, g - 1)
                    v.scalar_tensor_tensor(lg[:, slot, 0:nj, :], d2[:, 0:nj, :], 2.0, lnr[:, 0:nj, :],
                                           ALU.subtract, ALU.mult).then_inc(lg_ready, 1)
                    v.wait_ge(lg_ready, g + 1)
                    v.tensor_reduce(mn[:, slot, 0:nj], lg[:, slot, 0:nj, :], AX.X, ALU.min).then_inc(mn_ready, 1)

                def copy_eT(g, slot, rnd):
                    v.wait_ge(et_done, g + 1)
                    after(v, out_done, g)
                    n = max(tiles_of(g) - 2, 0)
                    if n:
                        v.tensor_copy(eT[:, 4:4 + 2 * n, :].rearrange("p j d -> p (j d)"),
                                      psE[:, 512:512 + n * 256]).then_inc(eT_high, 1)
                    else:
                        v.nop(nofuse=True).then_inc(eT_high, 1)

                def residual(g, slot, rnd):
                    nj = tiles_of(g)
                    v.wait_ge(ex_ready, g + 1)
                    v.reciprocal(rz[:, 0:nj], zz[:, slot, 0:nj]).then_inc(rz_ready, 1)
                    v.wait_ge(rz_ready, g + 1)
                    v.wait_ge(out_done, g + 1)
                    for j in range(nj):
                        t = tok[:, bass.ds(TG * g + j, 1), :].rearrange("p o d -> p (o d)")
                        last = v.scalar_tensor_tensor(t, psO[:, j * D:(j + 1) * D], rz[:, j:j + 1], t, ALU.mult, ALU.add)
                    last.then_inc(h1_ready, 1)

                def stats1(g, slot, rnd):
                    nj = tiles_of(g)
                    v.wait_ge(h1_ready, g + 1)
                    here = tok[:, bass.ds(TG * g, nj), :]
                    v.tensor_reduce(hmax[:, bass.ds(TG * g, nj)], here, AX.X, ALU.max)
                    v.tensor_reduce(hmin[:, bass.ds(TG * g, nj)], here, AX.X, ALU.min)
                    stats(lambda j: tok[:, bass.ds(TG * g + j, 1), :].rearrange("p o d -> p (o d)"), bst1,
                          lambda j: mvs[:, j, :], nj, bn1, mvs_ready, g)
                    v.wait_ge(mvs_ready, g + 1)
                    v.tensor_copy(mv1[:, bass.ds(TG * g, nj), :], mvs[:, 0:nj, :]).then_inc(mv1_ready, 1)

                pipeline(v, 0, GA, [(3, logits), (4, copy_eT), (2, dist2), (1, stats0), (1, normalise0), (4, residual),
                                    (5, stats1)])
                count = [0]
                s_vf = s_end

                def link(ins):
                    count[0] += 1
                    ins.then_inc(s_vf, 1)
                    v.wait_ge(s_vf, count[0])

                v.wait_ge(mv1_ready, GA)
                link(v.tensor_tensor(hmax[:, :], hmax[:, :], mv1[:, :, 0], ALU.subtract))
                link(v.tensor_tensor(hmin[:, :], mv1[:, :, 0], hmin[:, :], ALU.subtract))
                link(v.tensor_tensor(hmax[:, :], hmax[:, :], hmin[:, :], ALU.max))
                v.wait_ge(s_std1, 1)
                link(v.reciprocal(hmin[:, :], hstd[:, :]))
                link(v.tensor_tensor(hmax[:, :], hmax[:, :], hmin[:, :], ALU.mult))
                link(v.tensor_reduce(am2[:, 0:1], hmax[:, :], AX.X, ALU.max))
                link(v.tensor_reduce(am[:, 2:3], wffn[:, :], AX.X, ALU.max))
                link(v.tensor_reduce(am[:, 3:4], wffn[:, :], AX.X, ALU.min))
                link(v.tensor_scalar(am[:, 3:4], am[:, 3:4], -1.0, None, ALU.mult))
                v.tensor_tensor(am2[:, 1:2], am[:, 2:3], am[:, 3:4], ALU.max).then_inc(s_am, 1)
                v.wait_ge(s_amall, 1)
                link(v.tensor_scalar(am[:, 0:2], am[:, 0:2], 1e-12, None, ALU.max))
                link(v.reciprocal(am[:, 4:6], am[:, 0:2]))
                link(v.tensor_scalar(am[:, 6:8], am[:, 4:6], FP8_MAX, None, ALU.mult))
                link(v.tensor_copy(c["fscale"][:, 0:1], am[:, 6:7]))
                link(v.tensor_tensor(am[:, 2:3], am[:, 0:1], am[:, 1:2], ALU.mult))
                link(v.tensor_scalar(c["fscale"][:, 1:2], am[:, 2:3], 1.0 / FP8_MAX / FP8_MAX, None, ALU.mult))
                quantise(v, link, wffn[:, :], am[:, 7:8], qtmp[:, :], qm[:, :], c["wq"][:, :])

    nc.clear_and_free_semaphores(used)
    nc.all_engine_barrier()

def quantise(v, link, src, scale, tmp, mag, dst):
    link(v.tensor_scalar(tmp, src, scale, FP8_MAX, ALU.mult, ALU.min))
    link(v.tensor_scalar(mag.bitcast(I32), tmp.bitcast(I32), 0x7F800000, None, ALU.bitwise_and))
    link(v.tensor_scalar(mag, mag, MINEXP, ROUND, ALU.max, ALU.mult))
    link(v.scalar_tensor_tensor(tmp, tmp, -FP8_MAX, mag, ALU.max, ALU.add))
    link(v.tensor_tensor(dst, tmp, mag, ALU.subtract))


def rsqrt(v, var, eps, out, xe, half, done, base):
    v.tensor_scalar(xe, var, eps, None, ALU.add).then_inc(done, 1)
    v.wait_ge(done, base + 1)
    v.tensor_scalar(half.bitcast(I32), xe.bitcast(I32), 1, None, ALU.logical_shift_right).then_inc(done, 1)
    v.wait_ge(done, base + 2)
    v.tensor_scalar(out.bitcast(I32), half.bitcast(I32), -1.0, float(0x5F3759DF), ALU.mult, ALU.add).then_inc(done, 1)
    for k in range(3):
        v.wait_ge(done, base + 3 + 3 * k)
        v.tensor_tensor(half, out, out, ALU.mult).then_inc(done, 1)
        v.wait_ge(done, base + 4 + 3 * k)
        v.scalar_tensor_tensor(half, half, -0.5, xe, ALU.mult, ALU.mult).then_inc(done, 1)
        v.wait_ge(done, base + 5 + 3 * k)
        v.scalar_tensor_tensor(out, half, 1.5, out, ALU.add, ALU.mult).then_inc(done, 1)
    v.wait_ge(done, base + RSQRT_STEPS)


RSQRT_STEPS = 12


def back(nc, io, sb, sem, bank, wide, c, h1d, h3d, h4d, xed, yed, destd, out):
    ident, identb, ones, onesb = c["ident"], c["identb"], c["ones"], c["onesb"]
    before, beforeb, wq, fscale = c["before"], c["beforeb"], c["wq"], c["fscale"]
    NB = B // 2
    GR = GA
    NQ = NT // TG
    ES = 4
    Q1, C1 = T0[1] // TG, GSTEPS[0][1]

    def entries(engine, table, first, count, top):
        return nc.values_load_multi_w_load_instructions(
            table[0:1, bass.ds(first, count)], engines=[engine], min_val=0, max_val=top,
            skip_runtime_bounds_check_because="the chip computes the table and keeps it within the bounds")[1]

    wgu = sb("wgu", [128, NE, 2 * F])
    wdt = sb("wdt", [F, NE, D])
    rwt = sb("rwt", [128, NE])
    rbias = sb("rbias", [1, NE])
    sgu = sb("sgu", [128, 4 * F])
    sdt = sb("sdt", [128, D])
    zrow = sb("zrow", [128, XW])

    h1s = sb("h1s", [128, 2, 4, D])
    bstb = sb("bstb", [128, 4, 6])
    mvb = sb("mvb", [128, 4, 2])
    xe = sb("xe", [128, 8])
    sd = sb("sd", [128, 8])
    root = sb("root", [128, 8])
    ra, rb = root[:, 4:8], root[:, 0:4]
    xq = sb("xq", [128, 4, D])
    qmag = sb("qmag", [128, 4, D])
    xqb = sb("xqb", [128, 4, D], BF16)
    xqT = sb("xqT", [128, 4, D], BF16)
    h2 = sb("h2", [128, 2, 4, D])
    bstc = sb("bstc", [128, 4, 6])
    mvc = sb("mvc", [128, 4, 2])
    xn = sb("xn", [128, 2, 4, D + 4])
    xnT = sb("xnT", [128, 2, T + 1])
    e0 = sb("e0", [128, 2, T + 1])
    e1 = sb("e1", [128, 2, T + 1])
    rzb = sb("rzb", [128, 4])
    h3 = sb("h3", [128, 2, 4, D])

    h3s = sb("h3s", [128, 4, TG, D])
    bstd = sb("bstd", [128, TG, 6])
    mvd = sb("mvd", [128, TG, 2])
    rc = sb("rc", [128, TG])
    xec = sb("xec", [128, TG])
    hfc = sb("hfc", [128, TG])
    xr = sb("xr", [128, 4, TG, XW])
    x4T = sb("x4T", [128, TG, D])
    lo = sb("lo", [128, TG, NE + 2])
    lr = sb("lr", [128, TG, NE + 2])
    t8 = sb("t8", [128, TG, 8])
    mask = sb("mask", [128, TG, NE], BF16)
    taken = sb("taken", [128, NE])
    first1 = sb("first1", [128, NE])
    slotm = sb("slotm", [128, TG, NE])
    valid = sb("valid", [128, TG, NE])
    dest = sb("dest", [128, 2, TG, NE])
    dk = sb("dk", [128, TG, 8])
    zk = sb("zk", [128, TG, TOPK])
    idxs = sb("idxs", [128, 4, TG, TOPK], I32)
    ex = sb("ex", [128, TG, NE])
    zz = sb("zz4", [128, TG])
    s6 = sb("s6", [128, TG])
    den = sb("den", [128, TG])
    th = sb("th", [128, TG, 2 * F])
    sa = sb("sa", [128, TG, 2 * F])
    hs = sb("hs", [128, TG, 2 * F])
    hsT = sb("hsT", [128, TG, D])
    h4 = sb("h4", [128, 2, TG, D])

    eiota = sb("eiota", [NE + 1, 2], I32)
    iiota = sb("iiota", [NE + 1, max(GT)], I32)
    it = sb("it", [NE + 1, max(GT)])
    itin = sb("itin", [NE + 1, max(GT)])
    oh = sb("oh", [NE + 1, max(GT)])
    col = sb("col", [NE + 1, 16])
    coli = sb("coli", [NE, 2], I32)
    bcol = sb("bcol", [NE, 1])
    diag = sb("diag", [NE, NE])
    tin = sb("tin", [1, NT], I32)
    texp = sb("texp", [1, NT], I32)
    tbias = sb("tbias", [1, NT])
    ttail = sb("ttail", [1, NGRP * NE], I32)

    xin = xr
    xeT = sb("xeT", [128, 2, TG, 128])
    gate = sb("gate", [128, ES, TG])
    the = sb("the", [128, TG, F])
    ae = sb("ae", [128, TG, F])
    hh = sb("hh", [128, 2, TG, F])
    hT = sb("hT", [F, 2, TG, 128])
    yo = sb("yo", [128, 2, TG, D])

    dests = sb("dests", [128, 2, TG, NE])
    shift = sb("shift", [128, NGRP, NE])
    drow = sb("drow", [128, TG, NE])
    dg = sb("dg", [128, TG, 8])
    zg = sb("zg", [128, TG, TOPK])
    idxg = sb("idxg", [128, 2, TG, TOPK], I32)
    yg = sb("yg", [128, 2, TG, TOPK, D])
    h4s, ot = h3s, h4

    n = {}
    for name in ("s_wt", "s_c", "s_c2", "s_z", "s_half",
                 "bnb", "mvb_r", "xea_r", "xq_r", "q_r", "xqb_r", "qt_done", "xqT_r", "ffn_done", "h2_r", "bnc",
                 "mvc_r", "xeb_r", "sd_r", "root_r", "xn_r", "xt_done2", "xnT_r", "s_done", "e_r", "pv_done", "rzb_r", "h3_r",
                 "bnd", "mvd_r", "rsc", "x4_r", "x4t_done", "x4T_r", "lo_done", "gate_done", "up_done", "lo_r", "top_r",
                 "rep_r", "mask_r", "nl_r", "cum_done", "slot_r", "valid_r", "dest0_r", "dest_r", "taken_r",
                 "dk_r", "zk_r", "idx_r", "shift_p", "shift_r", "ex_r", "em_r", "s6_r", "den_r", "row_r",
                 "th_r", "sa_r", "hs_r", "hst_done", "hsT_r", "sh_done", "h4_r",
                 "tab_v", "tab_p", "tab_ready", "tail_z", "tail_z2",
                 "xet_done", "xeT_r", "geu_done", "g1_r", "gx_r", "gate_r", "the_r", "ae_r", "hh_r", "ht_done",
                 "hT_r", "dn_done", "yo_r",
                 "idxg_r", "sh0_r", "sh1_r", "dg_r", "zg_r", "add1_r", "add2_r", "add3_r", "ot_r"):
        n[name] = sem(name)
    h1_in = [sem(f"h1_in{i}") for i in range(2)]
    h3_out = [sem(f"h3_out{i}") for i in range(2)]
    h3_in = [sem(f"h3_in{i}") for i in range(4)]
    h4_out = [sem(f"h4_out{i}") for i in range(2)]
    scat = [sem(f"scat{i}") for i in range(4)]
    xin_in = [sem(f"xin_in{i}") for i in range(ES)]
    yo_out = [sem(f"yo_out{i}") for i in range(2)]
    gath = [sem(f"gath{i}") for i in range(2)]
    h4_in = [sem(f"h4_in{i}") for i in range(2)]
    dest_out = [sem(f"dest_out{i}") for i in range(2)]
    dest_in = [sem(f"dest_in{i}") for i in range(2)]
    ot_out = [sem(f"ot_out{i}") for i in range(2)]

    pQT, pDen = bank[0][:, 0:256].bitcast(BF16), bank[0][:, 256:260]
    pF = pX = bank[1]
    pS0, pS1 = bank[2], bank[3]
    pP, rA = wide[0][:, 0:512], wide[0][:, 512:1024]
    rB, rC = wide[1][:, 0:512], wide[1][:, 512:1024]
    LATE = 7
    CUT = place_of(GSTEPS[0][1], LATE) + 1
    SPAN = [(0, CUT, LATE), (CUT, place_of(GA, LATE + 1) + 1, LATE + 1)]
    WEIGHTS = 16 * 8
    TABV, TABP = 7, 8
    eT_ = (bank[0], bank[2])
    eG = (bank[1], bank[3])
    eH = (wide[0][:, 0:512], wide[0][:, 512:1024])
    eO = (wide[1][:, 0:512], wide[1][:, 512:1024])
    SP, PE, POOL = mybir.EngineType.SP, mybir.EngineType.PE, mybir.EngineType.Pool

    with nc.Block() as block:
        @block.gpsimd
        def _(p):
            p.memset(zrow[:, :], 0.0).then_inc(n["s_c"], 1)
            p.memset(xe[:, :], 1.0).then_inc(n["s_half"], 1)
            p.memset(h1s[:, :, :, :], 0.0).then_inc(n["s_c"], 1)
            for slot in range(2):
                for j in range(4):
                    p.memset(xn[:, slot, j, D:D + 1], 1.0)
            p.memset(lo[:, :, :], BIG)
            p.memset(taken[:, :], 0.0)
            p.memset(col[:, :], 0.0)
            p.iota(eiota[:, :], [[0, 2]], base=0, channel_multiplier=1)
            p.iota(iiota[:, :], [[128, max(GT)]], base=0, channel_multiplier=0).then_inc(n["s_c"], 1)

            def scatter(g, slot, rnd):
                nj = tiles_of(g)
                p.wait_ge(n["row_r"], g + 1)
                p.wait_ge(n["idx_r"], g + 1)
                p.nop(nofuse=True)
                for j in range(nj):
                    for k in range(TOPK):
                        p.indirect_dma_start(
                            xed[:, :], bass.IndirectOffsetOnAxis(ap=idxs[:, slot, j, k:k + 1], axis=0),
                            xr[:, slot, j, :], None, bounds_check=ZR - 1, oob_is_err=False).then_inc(scat[slot], 16)

            def gather(group, g, slot, rnd):
                p.wait_ge(n["idxg_r"], g + 1)
                after(p, n["ot_r"], g - 1)
                p.nop(nofuse=True)
                for j in range(tiles_of(g)):
                    for k in range(TOPK):
                        p.indirect_dma_start(
                            yg[:, slot, j, k, :], None, yed[group][:, :],
                            bass.IndirectOffsetOnAxis(ap=idxg[:, slot, j, k:k + 1], axis=0)).then_inc(gath[slot], 16)

            pipeline(p, 0, GR, [(0, scatter)], 4)
            p.wait_ge(n["tab_ready"], 2)
            for e in range(0, NE, 4):
                for row in entries(POOL, ttail, NE + e, 4, ZR - 128):
                    p.dma_start(xed[bass.ds(row, 128), :], zrow[:, :]).then_inc(n["tail_z2"], 16)
            p.wait_ge(n["tail_z2"], 16 * NE)
            p.wait_ge(n["s_z"], 16 * NGRP)
            for group, ((a, b), q) in enumerate(zip(GSTEPS, (Q1, NQ))):
                p.wait_ge(yo_out[0], 16 * (-(-q // 2)))
                p.wait_ge(yo_out[1], 16 * (q // 2))
                pipeline(p, a, b, [(0, lambda g, slot, rnd, group=group: gather(group, g, slot, rnd))])

        @block.sync
        def _(sp):
            def load_h1(g, slot, rnd):
                after(sp, n["h2_r"], g - 1)
                src = h1d[bass.ds(2 * g, 2), :, :].rearrange("b t d -> t b d")
                sp.dma_start(h1s[:, slot, 0:4:2, :], src[0:HALF[0]]).then_inc(h1_in[slot], 16)
                sp.dma_start(h1s[0:HALF[1], slot, 1:4:2, :], src[HALF[0]:T]).then_inc(h1_in[slot], 16)

            def store_h3(g, slot, rnd):
                sp.wait_ge(n["h3_r"], g + 1)
                dst = h3d[bass.ds(2 * T * g, 2 * T), :].rearrange("(b t) d -> t b d", t=T)
                sp.dma_start(dst[0:HALF[0]], h3[:, slot, 0:4:2, :]).then_inc(h3_out[slot], 16)
                sp.dma_start(dst[HALF[0]:T], h3[0:HALF[1], slot, 1:4:2, :]).then_inc(h3_out[slot], 16)

            sp.wait_ge(n["s_c"], 3)
            for dst, src in ((wgu, "wgu"), (wdt, "wdt")):
                sp.dma_start(dst[:, :, :], io[src]).then_inc(n["s_wt"], 16)
            for dst, src in ((rwt, "rwt"), (rbias, "rbias"), (sgu, "sgu"), (sdt, "sdt")):
                sp.dma_start(dst[:, :], io[src]).then_inc(n["s_wt"], 16)
            sp.dma_start(bcol[:, :], io["rbias"].rearrange("o e -> e o")).then_inc(n["s_wt"], 16)
            sp.dma_start(xed[ZR:ZR + 128, :], zrow[:, :]).then_inc(n["s_wt"], 16)
            for k in range(NGRP):
                sp.dma_start(yed[k][YZ[k]:YZ[k] + 128, :], zrow[:, 0:D]).then_inc(n["s_z"], 16)

            def load_h3(g, slot, rnd):
                nj = tiles_of(g)
                last = 3 * (slot // 2) + 2 + slot % 2
                for p in range(2):
                    stored = 3 * rnd + (last - p) // 2 + 1
                    sp.wait_ge(h3_out[p], 32 * (min(stored, NB // 2) if isinstance(stored, int) else stored))
                after(sp, n["h4_r"], g - 3)
                sp.dma_start(h3s[:, slot, 0:nj, :],
                             h3d[bass.ds(TG * 128 * g, nj * 128), :].rearrange("(j p) d -> p j d", p=128))\
                    .then_inc(h3_in[slot], 16)

            def store_h4(g, slot, rnd):
                nj = tiles_of(g)
                sp.wait_ge(n["h4_r"], g + 1)
                sp.dma_start(h4d[bass.ds(TG * 128 * g, nj * 128), :].rearrange("(j p) d -> p j d", p=128),
                             h4[:, slot, 0:nj, :]).then_inc(h4_out[slot], 16)
                sp.wait_ge(n["dest_r"], g + 1)
                sp.dma_start(destd[bass.ds(TG * g, nj), :, :].rearrange("j p e -> p j e"),
                             dest[:, slot, 0:nj, :]).then_inc(dest_out[slot], 16)

            braid(sp, 0, place_of(GR + 2, LATE - 1) + 1, LATE - 1,
                  [('b', 0, load_h1), ('b', 3, store_h3), ('r', 3, halves(store_h4)), ('r', 0, load_h3)], 0, GR)

            def load_rows(q, slot, rnd):
                rows = entries(SP, tin, TG * q, TG, ZR)
                after(sp, n["gate_r"], q - ES + 1)
                for j, row in enumerate(rows):
                    sp.dma_start(xin[:, slot, j, :], xed[bass.ds(row, 128), :]).then_inc(xin_in[slot], 16)

            def store_rows(group, q, slot, rnd):
                if isinstance(q, int):
                    group = int(q >= Q1)
                row = 128 * (TG * q - T0[group])
                sp.wait_ge(n["yo_r"], q + 1)
                sp.dma_start(yed[group][bass.ds(row, TG * 128), :].rearrange("(j p) d -> p j d", p=128),
                             yo[:, slot % 2, :, :]).then_inc(yo_out[slot % 2], 16)

            sp.wait_ge(n["tab_ready"], 1)
            for e in range(0, NE, 4):
                for row in entries(SP, ttail, e, 4, ZR - 128):
                    sp.dma_start(xed[bass.ds(row, 128), :], zrow[:, :]).then_inc(n["tail_z"], 16)
            sp.wait_ge(n["tail_z"], 16 * NE)
            sp.wait_ge(n["tab_ready"], 2)
            for k in range(4):
                sp.wait_ge(scat[k], 16 * TOPK * sum(tiles_of(g) for g in range(k, GR, 4)))
            sp.wait_ge(h4_out[0], 16 * (-(-GR // 2)))
            sp.wait_ge(h4_out[1], 16 * (GR // 2))
            sp.wait_ge(dest_out[0], 16 * (-(-GR // 2)))
            sp.wait_ge(dest_out[1], 16 * (GR // 2))

            def load_dest(g, slot, rnd):
                nj = tiles_of(g)
                after(sp, n["sh1_r"], g - 1)
                sp.dma_start(dests[:, slot, 0:nj, :], destd[bass.ds(TG * g, nj), :, :].rearrange("j p e -> p j e"))\
                    .then_inc(dest_in[slot], 16)

            def load_h4(g, slot, rnd):
                nj = tiles_of(g)
                after(sp, n["ot_r"], g - 1)
                sp.dma_start(h4s[:, slot, 0:nj, :],
                             h4d[bass.ds(TG * 128 * g, nj * 128), :].rearrange("(j p) d -> p j d", p=128))\
                    .then_inc(h4_in[slot], 16)

            def store_out(g, slot, rnd):
                nj = tiles_of(g)
                sp.wait_ge(n["ot_r"], g + 1)
                sp.dma_start(out[bass.ds(TG * 128 * g, nj * 128), :].rearrange("(j p) d -> p j d", p=128),
                             ot[:, slot, 0:nj, :]).then_inc(ot_out[slot], 16)

            def move(group):
                return [(0, load_rows), (5, lambda q, slot, rnd: store_rows(group, q, slot, rnd))]

            move_sums = [(0, load_dest), (2, load_h4), (4, store_out)]
            pipeline(sp, 0, NQ, move(0), ES, end=Q1)
            sp.wait_ge(n["tail_z2"], 16 * NE)
            weave(sp, Q1, NQ + 5, NQ, move(1), ES, Q1, move_sums, C1)
            pipeline(sp, 0, GR, move_sums, begin=C1)
            sp.wait_ge(ot_out[0], 16 * (-(-GR // 2)))
            sp.wait_ge(ot_out[1], 16 * (GR // 2))

        @block.tensor
        def _(pe):
            pe.wait_ge(n["s_wt"], WEIGHTS)
            pe.wait_ge(n["s_c"], 3)
            def turn_q(g, slot, rnd):
                pe.wait_ge(n["xqb_r"], g + 1)
                after(pe, n["xqT_r"], g)
                for j in range(4):
                    last = pe.transpose(pQT[:, j * D:(j + 1) * D], xqb[:, j, :], identb[:, :])
                last.then_inc(n["qt_done"], 1)

            def ffn(g, slot, rnd):
                pe.wait_ge(n["xqT_r"], g + 1)
                after(pe, n["xnT_r"], g)
                for j in range(4):
                    last = pe.matmul(pF[:, j * D:(j + 1) * D], xqT[:, j, :], wq[:, :], start=True, stop=True)
                last.then_inc(n["ffn_done"], 1)

            def turn_x(g, slot, rnd):
                pe.wait_ge(n["xn_r"], g + 1)
                after(pe, n["xnT_r"], g)
                for i in range(2):
                    for h, m in enumerate(HALF):
                        last = pe.transpose(pX[:, 256 * i + 128 * h:256 * i + 128 * h + m],
                                            xn[0:m, slot, 2 * i + h, 0:D], ident[0:m, 0:m])
                last.then_inc(n["xt_done2"], 1)

            def scores(g, slot, rnd):
                pe.wait_ge(n["xnT_r"], g + 1)
                after(pe, n["e_r"], 2 * g)
                for i in range(2):
                    for h, m in enumerate(HALF):
                        dst = (pS0, pS1)[h][0:m, 256 * i:256 * i + T]
                        last = pe.matmul(dst, xnT[:, i, 128 * h:128 * h + m], xnT[:, i, 0:T], start=True, stop=True)
                last.then_inc(n["s_done"], 1)

            def mix(g, slot, rnd):
                pe.wait_ge(n["e_r"], 2 * g + 2)
                after(pe, n["h3_r"], g)
                for i in range(2):
                    for h, m in enumerate(HALF):
                        parts = list(zip((e0, e1), HALF, (0, 1)))
                        for e, m2, h2_ in parts:
                            pe.matmul(pP[0:m, 256 * i + D * h:256 * i + D * h + D], e[0:m2, i, 128 * h:128 * h + m],
                                      xn[0:m2, slot, 2 * i + h2_, 0:D], start=(h2_ == 0), stop=(h2_ == 1))
                        for e, m2, h2_ in parts:
                            last = pe.matmul(pDen[0:m, 2 * i + h:2 * i + h + 1], e[0:m2, i, 128 * h:128 * h + m],
                                             xn[0:m2, slot, 2 * i + h2_, D:D + 1], start=(h2_ == 0), stop=(h2_ == 1))
                last.then_inc(n["pv_done"], 1)

            def turn_r(g, slot, rnd):
                pe.wait_ge(n["x4_r"], g + 1)
                after(pe, n["h4_r"], g)
                for j in range(tiles_of(g)):
                    last = pe.transpose(rA[:, j * 128:(j + 1) * 128], xr[:, slot, j, 0:D], ident[:, :])
                last.then_inc(n["x4t_done"], 1)

            def route(g, slot, rnd):
                nj = tiles_of(g)
                pe.wait_ge(n["x4T_r"], g + 1)
                after(pe, n["taken_r"], g)
                after(pe, n["slot_r"], g)
                for j in range(nj):
                    dst = rB[:, j * NE:(j + 1) * NE]
                    pe.matmul(dst, x4T[:, j, :], rwt[:, :], start=True, stop=False)
                    last = pe.matmul(dst, ones[0:1, :], rbias[:, :], start=False, stop=True)
                last.then_inc(n["lo_done"], 1)
                after(pe, n["hs_r"], g)
                for j in range(nj):
                    last = pe.matmul(rC[:, j * 128:(j + 1) * 128], x4T[:, j, :], sgu[:, 0:2 * F], start=True, stop=True)
                last.then_inc(n["gate_done"], 1)

            def shared_up(g, slot, rnd):
                pe.wait_ge(n["sa_r"], g + 1)
                for j in range(tiles_of(g)):
                    last = pe.matmul(rC[:, j * 128:(j + 1) * 128], x4T[:, j, :], sgu[:, 2 * F:4 * F],
                                     start=True, stop=True)
                last.then_inc(n["up_done"], 1)

            def count(g, slot, rnd):
                nj = tiles_of(g)
                pe.wait_ge(n["mask_r"], g + 1)
                pe.wait_ge(n["lo_r"], g + 1)
                for j in range(nj):
                    dst = rB[:, 256 + j * NE:256 + (j + 1) * NE]
                    for i in range(j + 1):
                        pe.matmul(dst, beforeb[:, :] if i == j else onesb[:, :], mask[:, i, :],
                                  start=(i == 0), stop=(i == j))
                for i in range(nj):
                    last = pe.matmul(rB[:, 0:NE], onesb[:, :], mask[:, i, :], start=(i == 0), stop=(i == nj - 1))
                last.then_inc(n["cum_done"], 1)

            def turn_h(g, slot, rnd):
                pe.wait_ge(n["hs_r"], g + 1)
                for j in range(tiles_of(g)):
                    last = pe.transpose(rA[:, j * 128:(j + 1) * 128], hs[:, j, :], ident[:, :])
                last.then_inc(n["hst_done"], 1)

            def shared_down(g, slot, rnd):
                pe.wait_ge(n["hsT_r"], g + 1)
                for j in range(tiles_of(g)):
                    last = pe.matmul(rA[:, j * D:(j + 1) * D], hsT[:, j, :], sdt[:, :], start=True, stop=True)
                last.then_inc(n["sh_done"], 1)

            def turn_e(q, slot, rnd):
                pe.wait_ge(xin_in[slot], 64 * (rnd + 1))
                after(pe, n["g1_r"], q - 1)
                for j in range(TG):
                    last = pe.transpose(eT_[slot % 2][:, j * 128:(j + 1) * 128], xin[:, slot, j, 0:D], ident[:, :])
                last.then_inc(n["xet_done"], 1)

            def up(q, slot, rnd):
                experts = entries(PE, texp, TG * q, TG, NE - 1)
                pe.wait_ge(n["xeT_r"], q + 1)
                after(pe, n["hh_r"], q - 1)
                pe.nop(nofuse=True)
                lg = eT_[slot % 2]
                pe.matmul(lg[:, 0:TG], ones[0:1, :], tbias[:, bass.ds(TG * q, TG)], start=True, stop=False)
                for j, e in enumerate(experts):
                    pe.matmul(lg[:, j:j + 1], xeT[:, slot % 2, j, :], rwt[:, bass.ds(e, 1)], start=False,
                              stop=(j == TG - 1))
                    last = pe.matmul(eG[slot % 2][:, j * 128:(j + 1) * 128], xeT[:, slot % 2, j, :],
                                     wgu[:, bass.ds(e, 1), :].rearrange("p o f -> p (o f)"), start=True, stop=True)
                last.then_inc(n["geu_done"], 1)

            def turn_hh(q, slot, rnd):
                pe.wait_ge(n["hh_r"], q + 1)
                after(pe, n["hT_r"], q - 1)
                pe.nop(nofuse=True)
                for j in range(TG):
                    last = pe.transpose(eH[slot % 2][0:F, j * 128:(j + 1) * 128], hh[:, slot % 2, j, :], ident[:, :])
                last.then_inc(n["ht_done"], 1)

            def down(q, slot, rnd):
                experts = entries(PE, texp, TG * q, TG, NE - 1)
                pe.wait_ge(n["hT_r"], q + 1)
                after(pe, n["yo_r"], q - 1)
                pe.nop(nofuse=True)
                for j, e in enumerate(experts):
                    last = pe.matmul(eO[slot % 2][:, j * D:(j + 1) * D], hT[:, slot % 2, j, :],
                                     wdt[:, bass.ds(e, 1), :].rearrange("p o f -> p (o f)"), start=True, stop=True)
                last.then_inc(n["dn_done"], 1)

            def first_rows():
                pe.matmul(rB[:, 0:NE], ones[0:NE, :], diag[:, :], start=True, stop=True).then_inc(n["tab_p"], 1)

            pe.wait_ge(n["tab_v"], 1)
            first_rows()
            for k, (a, b) in enumerate(GSTEPS):
                braid(pe, *SPAN[k], [('r', 1, halves(count)), ('r', 1, halves(shared_up)), ('b', 1, turn_x),
                                     ('b', 1, scores), ('b', 0, turn_q), ('b', 0, ffn), ('r', 1, halves(turn_h)),
                                     ('r', 1, halves(shared_down)), ('b', 1, mix), ('r', 0, turn_r),
                                     ('r', 0, halves(route))], a, b)
                pe.wait_ge(n["tab_v"], TABV * k + 2)
                pe.transpose(rB[0:NE, 0:128], taken[:, :], ident[:, :]).then_inc(n["tab_p"], 1)
                pe.wait_ge(n["tab_v"], TABV * k + 3)
                pe.matmul(rB[0:NE + 1, 128:129], before[0:NE, 0:NE + 1], col[0:NE, 2:3], start=True, stop=True)\
                    .then_inc(n["tab_p"], 1)
                for step, src in ((4, oh), (5, itin), (6, it)):
                    pe.wait_ge(n["tab_v"], TABV * k + step)
                    for i, w in enumerate(range(0, GT[k], 512)):
                        m = min(512, GT[k] - w)
                        last = pe.matmul((rA, rC)[i][0:1, 0:m], ones[0:NE + 1, 0:1], src[:, w:w + m],
                                         start=True, stop=True)
                    last.then_inc(n["tab_p"], 1)
                pe.wait_ge(n["tab_v"], TABV * k + 7)
                pe.matmul(rB[0:1, 0:NE], col[0:NE, 11:12], ident[0:NE, 0:NE], start=True, stop=True)\
                    .then_inc(n["tab_p"], 1)
                pe.matmul(rB[:, 256:256 + NE], ones[0:NE, :], diag[:, :], start=True, stop=True).then_inc(n["tab_p"], 1)
                if k == 0:
                    pe.wait_ge(n["tab_v"], TABV + 1)
                    first_rows()
            pe.wait_ge(n["tab_ready"], NGRP)
            pipeline(pe, 0, NQ, [(0, turn_e), (1, up), (3, down), (2, turn_hh)], ES)

        @block.scalar
        def _(a):
            def copy_q(g, slot, rnd):
                a.wait_ge(n["qt_done"], g + 1)
                after(a, n["ffn_done"], g)
                a.activation(xqT[:, :, :].rearrange("p j d -> p (j d)"), pQT, ACT.Copy)\
                    .then_inc(n["xqT_r"], 1)

            def copy_x(g, slot, rnd):
                a.wait_ge(n["xt_done2"], g + 1)
                after(a, n["s_done"], g)
                a.activation(xnT[:, :, 0:T], pX[:, :].rearrange("p (i t) -> p i t", i=2)[:, :, 0:T], ACT.Copy)\
                    .then_inc(n["xnT_r"], 1)

            def expo(g, slot, rnd):
                a.wait_ge(n["s_done"], g + 1)
                after(a, n["pv_done"], g)
                for e, ps, m in ((e0, pS0, HALF[0]), (e1, pS1, HALF[1])):
                    a.activation(e[0:m, :, 0:T], ps[0:m, :].rearrange("p (i t) -> p i t", i=2)[:, :, 0:T], ACT.Exp,
                                 scale=SCALE).then_inc(n["e_r"], 1)

            def roots(s_, slot, rnd):
                if not isinstance(s_, int) or s_ < NB:
                    a.wait_ge(n["xea_r"], s_ + 1)
                after(a, n["xeb_r"], s_)
                after(a, n["root_r"], s_)
                a.activation(sd[:, :], xe[:, :], ACT.Sqrt, bias=c["eps_ln"][:, :]).then_inc(n["sd_r"], 1)

            a.wait_ge(n["s_half"], 3)

            def copy_x4(g, slot, rnd):
                nj = tiles_of(g)
                a.wait_ge(n["x4t_done"], g + 1)
                after(a, n["up_done"], g)
                a.activation(x4T[:, 0:nj, :].rearrange("p j d -> p (j d)"), rA[:, 0:nj * 128], ACT.Copy)\
                    .then_inc(n["x4T_r"], 1)

            def tanh(g, slot, rnd):
                nj = tiles_of(g)
                a.wait_ge(n["gate_done"], g + 1)
                after(a, n["sa_r"], g)
                a.activation(th[:, 0:nj, :], rC[:, 0:nj * 128].rearrange("p (j f) -> p j f", j=nj),
                             ACT.Tanh, scale=0.5).then_inc(n["th_r"], 1)

            def probs(g, slot, rnd):
                a.wait_ge(n["nl_r"], g + 1)
                after(a, n["den_r"], g)
                for j in range(tiles_of(g)):
                    last = a.activation(ex[:, j, :], lo[:, j, 0:NE], ACT.Exp, bias=xr[:, slot, j, D:D + 1],
                                        accum_out=zz[:, j:j + 1])
                last.then_inc(n["ex_r"], 1)

            def copy_h(g, slot, rnd):
                nj = tiles_of(g)
                a.wait_ge(n["hst_done"], g + 1)
                after(a, n["sh_done"], g)
                a.activation(hsT[:, 0:nj, :].rearrange("p j d -> p (j d)"), rA[:, 0:nj * 128], ACT.Copy)\
                    .then_inc(n["hsT_r"], 1)

            def copy_xe(q, slot, rnd):
                a.wait_ge(n["xet_done"], q + 1)
                after(a, n["geu_done"], q - 1)
                a.activation(xeT[:, slot % 2, :, :].rearrange("p j d -> p (j d)"), eT_[slot % 2][:, :], ACT.Copy)\
                    .then_inc(n["xeT_r"], 1)

            def tanh_e(q, slot, rnd):
                a.wait_ge(n["geu_done"], q + 1)
                after(a, n["ae_r"], q)
                a.activation(the[:, :, :], eG[slot % 2][:, :].rearrange("p (j f) -> p j f", j=TG)[:, :, 0:F],
                             ACT.Tanh, scale=0.5).then_inc(n["the_r"], 1)

            def gate_e(q, slot, rnd):
                a.wait_ge(n["g1_r"], q + 1)
                a.activation(gate[:, slot, :], gate[:, slot, :], ACT.Exp).then_inc(n["gx_r"], 1)

            def copy_y(q, slot, rnd):
                a.wait_ge(n["dn_done"], q + 1)
                a.wait_ge(n["gate_r"], q + 1)
                half = slot % 2
                if not isinstance(q, int) or q >= 2:
                    a.wait_ge(yo_out[half], 16 * (2 * rnd + slot // 2))
                for j in range(TG):
                    last = a.activation(yo[:, half, j, :], eO[half][:, j * D:(j + 1) * D], ACT.Copy,
                                        scale=gate[:, slot, j:j + 1])
                last.then_inc(n["yo_r"], 1)

            for span, (s0, s1) in zip(SPAN, GSTEPS):
                braid(a, *span, [('r', 1, halves(tanh)), ('b', 0, roots), ('r', 1, probs), ('b', 1, copy_x), ('b', 1, expo),
                                 ('b', 0, copy_q), ('r', 1, halves(copy_h)), ('r', 0, halves(copy_x4))], s0, s1)
            pipeline(a, 0, NQ, [(0, copy_xe), (1, tanh_e), (1, gate_e), (3, copy_y)], ES)

        @block.vector
        def _(v):
            v.wait_ge(n["s_wt"], WEIGHTS)
            v.tensor_scalar(wdt[:, :, :], wdt[:, :, :], 0.5, None, ALU.mult).then_inc(n["s_half"], 1)
            v.tensor_scalar(sdt[:, :], sdt[:, :], 0.25, None, ALU.mult).then_inc(n["s_half"], 1)
            v.wait_ge(n["s_c"], 3)

            def stats(src, dst6, dst2, nj, done6, done2, g):
                for j in range(nj):
                    last = v.bn_stats(dst6[:, j, :], src[:, j, :])
                last.then_inc(n[done6], 1)
                v.wait_ge(n[done6], g + 1)
                v.nop(nofuse=True)
                for j in range(nj):
                    last = v.bn_aggr(dst2[:, j, :], dst6[:, j, :])
                last.then_inc(n[done2], 1)
                v.wait_ge(n[done2], g + 1)

            def stats_q(g, slot, rnd):
                v.wait_ge(h1_in[slot], 32 * (rnd + 1))
                stats(h1s[:, slot, :, :], bstb, mvb, 4, "bnb", "mvb_r", g)
                v.tensor_scalar(xe[:, 4:8], mvb[:, :, 1], 0.0, None, ALU.add).then_inc(n["xea_r"], 1)

            def roots(s_, slot, rnd):
                v.wait_ge(n["sd_r"], s_ + 1)
                v.reciprocal(root[:, :], sd[:, :]).then_inc(n["root_r"], 1)
                v.wait_ge(n["root_r"], s_ + 1)

            def quant(g, slot, rnd):
                after(v, n["xqb_r"], g)
                for j in range(4):
                    last = v.tensor_scalar(xq[:, j, :], h1s[:, slot, j, :], mvb[:, j, 0:1], ra[:, j:j + 1],
                                           ALU.subtract, ALU.mult)
                last.then_inc(n["xq_r"], 1)
                v.wait_ge(n["xq_r"], g + 1)
                v.tensor_scalar(xq[:, :, :], xq[:, :, :], fscale[:, 0:1], FP8_MAX, ALU.mult, ALU.min).then_inc(n["q_r"], 1)
                v.wait_ge(n["q_r"], 4 * g + 1)
                v.tensor_scalar(qmag[:, :, :].bitcast(I32), xq[:, :, :].bitcast(I32), 0x7F800000, None,
                                ALU.bitwise_and).then_inc(n["q_r"], 1)
                v.wait_ge(n["q_r"], 4 * g + 2)
                v.tensor_scalar(qmag[:, :, :], qmag[:, :, :], MINEXP, ROUND, ALU.max, ALU.mult).then_inc(n["q_r"], 1)
                v.wait_ge(n["q_r"], 4 * g + 3)
                v.scalar_tensor_tensor(xq[:, :, :], xq[:, :, :], -FP8_MAX, qmag[:, :, :], ALU.max, ALU.add)\
                    .then_inc(n["q_r"], 1)
                v.wait_ge(n["q_r"], 4 * g + 4)
                after(v, n["qt_done"], g)
                v.tensor_tensor(xqb[:, :, :], xq[:, :, :], qmag[:, :, :], ALU.subtract).then_inc(n["xqb_r"], 1)

            def ffn_out(g, slot, rnd):
                v.wait_ge(n["ffn_done"], g + 1)
                after(v, n["h3_r"], g - 1)
                after(v, n["xn_r"], g)
                v.scalar_tensor_tensor(h2[:, slot, :, :], pF[:, :].rearrange("p (j d) -> p j d", j=4),
                                       fscale[:, 1:2], h1s[:, slot, :, :], ALU.mult, ALU.add).then_inc(n["h2_r"], 1)
                v.wait_ge(n["h2_r"], g + 1)
                stats(h2[:, slot, :, :], bstc, mvc, 4, "bnc", "mvc_r", g)
                v.tensor_scalar(xe[:, 0:4], mvc[:, :, 1], 0.0, None, ALU.add).then_inc(n["xeb_r"], 1)

            def norm_x(g, slot, rnd):
                after(v, n["pv_done"], g - 1)
                for j in range(4):
                    last = v.tensor_scalar(xn[:, slot, j, 0:D], h2[:, slot, j, :], mvc[:, j, 0:1], rb[:, j:j + 1],
                                           ALU.subtract, ALU.mult)
                last.then_inc(n["xn_r"], 1)

            def attn_out(g, slot, rnd):
                v.wait_ge(n["pv_done"], g + 1)
                if not isinstance(g, int) or g >= 2:
                    v.wait_ge(h3_out[slot], 32 * rnd)
                for h, m in enumerate(HALF):
                    den_ = pDen[0:m, h:4:2]
                    last = v.reciprocal(rzb[0:m, h:4:2], den_)
                last.then_inc(n["rzb_r"], 1)
                v.wait_ge(n["rzb_r"], g + 1)
                for i in range(2):
                    for h, m in enumerate(HALF):
                        j = 2 * i + h
                        last = v.scalar_tensor_tensor(h3[0:m, slot, j, :], pP[0:m, 256 * i + D * h:256 * i + D * h + D],
                                                      rzb[0:m, j:j + 1], h2[0:m, slot, j, :], ALU.mult, ALU.add)
                last.then_inc(n["h3_r"], 1)

            def norm(g, slot, rnd):
                nj = tiles_of(g)
                v.wait_ge(h3_in[slot], 16 * (rnd + 1))
                after(v, n["x4_r"], g)
                stats(h3s[:, slot, :, :], bstd, mvd, nj, "bnd", "mvd_r", g)
                rsqrt(v, mvd[:, 0:nj, 1], LN_EPS, rc[:, 0:nj], xec[:, 0:nj], hfc[:, 0:nj], n["rsc"], RSQRT_STEPS * g)
                scattered(g, slot, rnd)
                for j in range(nj):
                    last = v.tensor_scalar(xr[:, slot, j, 0:D], h3s[:, slot, j, :], mvd[:, j, 0:1], rc[:, j:j + 1],
                                           ALU.subtract, ALU.mult)
                last.then_inc(n["x4_r"], 1)

            def scattered(g, slot, rnd):
                if not isinstance(g, int) or g >= 4:
                    v.wait_ge(scat[slot], 16 * TOPK * TG * rnd)

            def choose(g, slot, rnd):
                nj = tiles_of(g)
                v.wait_ge(n["lo_done"], g + 1)
                after(v, n["ex_r"], g)
                v.tensor_copy(lo[:, 0:nj, 0:NE], rB[:, 0:nj * NE].rearrange("p (j e) -> p j e", j=nj))\
                    .then_inc(n["lo_r"], 1)
                v.wait_ge(n["lo_r"], g + 1)
                v.nop(nofuse=True)
                for j in range(nj):
                    last = v.max(t8[:, j, :], lo[:, j, :])
                last.then_inc(n["top_r"], 1)
                v.wait_ge(n["top_r"], g + 1)
                v.tensor_scalar(xr[:, slot, 0:nj, D], t8[:, 0:nj, 2], -1.0, None, ALU.mult).then_inc(n["nl_r"], 1)
                for j in range(nj):
                    last = v.match_replace(lr[:, j, :], t8[:, j, :], lo[:, j, :], -BIG)
                last.then_inc(n["rep_r"], 1)
                v.wait_ge(n["rep_r"], g + 1)
                v.tensor_scalar(mask[:, 0:nj, :], lr[:, 0:nj, 0:NE], -BIG / 2, None, ALU.is_le).then_inc(n["mask_r"], 1)

            def silu_gate(g, slot, rnd):
                nj = tiles_of(g)
                v.wait_ge(n["th_r"], g + 1)
                after(v, n["hs_r"], g)
                v.scalar_tensor_tensor(sa[:, 0:nj, :], th[:, 0:nj, :], 1.0,
                                       rC[:, 0:nj * 128].rearrange("p (j f) -> p j f", j=nj), ALU.add, ALU.mult)\
                    .then_inc(n["sa_r"], 1)

            def silu_up(g, slot, rnd):
                nj = tiles_of(g)
                v.wait_ge(n["up_done"], g + 1)
                after(v, n["hst_done"], g)
                v.tensor_tensor(hs[:, 0:nj, :], sa[:, 0:nj, :], rC[:, 0:nj * 128].rearrange("p (j f) -> p j f", j=nj),
                                ALU.mult).then_inc(n["hs_r"], 1)

            def place(g, slot, rnd):
                nj = tiles_of(g)
                half, pairs = slot % 2, 2 * rnd + slot // 2
                v.wait_ge(n["cum_done"], g + 1)
                after(v, n["taken_r"], g)
                v.tensor_tensor(slotm[:, 0:nj, :], rB[:, 256:256 + nj * NE].rearrange("p (j e) -> p j e", j=nj),
                                taken[:, :].unsqueeze(1).to_broadcast([128, nj, NE]), ALU.add).then_inc(n["slot_r"], 1)
                v.wait_ge(n["slot_r"], g + 1)
                v.tensor_tensor(taken[:, :], taken[:, :], rB[:, 0:NE], ALU.add).then_inc(n["taken_r"], 1)
                v.scalar_tensor_tensor(valid[:, 0:nj, :], slotm[:, 0:nj, :], float(CAP), mask[:, 0:nj, :],
                                       ALU.is_lt, ALU.mult).then_inc(n["valid_r"], 1)
                if not isinstance(g, int) or g >= 2:
                    v.wait_ge(dest_out[half], 16 * pairs)
                v.tensor_tensor(dest[:, half, 0:nj, :], slotm[:, 0:nj, :],
                                first1[:, :].unsqueeze(1).to_broadcast([128, nj, NE]), ALU.add).then_inc(n["dest0_r"], 1)
                v.wait_ge(n["dest0_r"], g + 1)
                v.wait_ge(n["valid_r"], g + 1)
                v.tensor_tensor(dest[:, half, 0:nj, :], dest[:, half, 0:nj, :], valid[:, 0:nj, :], ALU.mult).then_inc(n["dest_r"], 1)
                v.wait_ge(n["dest_r"], g + 1)
                v.nop(nofuse=True)
                for j in range(nj):
                    last = v.max(dk[:, j, :], dest[:, half, j, :])
                last.then_inc(n["dk_r"], 1)
                v.wait_ge(n["dk_r"], g + 1)
                v.tensor_scalar(zk[:, 0:nj, :], dk[:, 0:nj, 0:TOPK], 0.0, float(ZR + 1), ALU.is_equal, ALU.mult)\
                    .then_inc(n["zk_r"], 1)
                v.wait_ge(n["zk_r"], g + 1)
                v.scalar_tensor_tensor(idxs[:, slot, 0:nj, :], dk[:, 0:nj, 0:TOPK], -1.0, zk[:, 0:nj, :],
                                       ALU.add, ALU.add).then_inc(n["idx_r"], 1)

            def denominator(g, slot, rnd):
                nj = tiles_of(g)
                v.wait_ge(n["ex_r"], g + 1)
                v.tensor_tensor(lr[:, 0:nj, 0:NE], ex[:, 0:nj, :], mask[:, 0:nj, :], ALU.mult).then_inc(n["em_r"], 1)
                v.wait_ge(n["em_r"], g + 1)
                v.tensor_reduce(s6[:, 0:nj], lr[:, 0:nj, 0:NE], AX.X, ALU.add).then_inc(n["s6_r"], 1)
                v.wait_ge(n["s6_r"], g + 1)
                v.scalar_tensor_tensor(den[:, 0:nj], zz[:, 0:nj], 1e-9, s6[:, 0:nj], ALU.mult, ALU.add)\
                    .then_inc(n["den_r"], 1)
                v.wait_ge(n["den_r"], g + 1)
                v.reciprocal(xr[:, slot, 0:nj, D + 1], den[:, 0:nj]).then_inc(n["row_r"], 1)

            def shared_out(g, slot, rnd):
                nj = tiles_of(g)
                half, pairs = slot % 2, 2 * rnd + slot // 2
                v.wait_ge(n["sh_done"], g + 1)
                if not isinstance(g, int) or g >= 2:
                    v.wait_ge(h4_out[half], 16 * pairs)
                v.tensor_tensor(h4[:, half, 0:nj, :], rA[:, 0:nj * D].rearrange("p (j d) -> p j d", j=nj),
                                h3s[:, slot, 0:nj, :], ALU.add).then_inc(n["h4_r"], 1)

            def link_to(name):
                count = [0]

                def link(ins):
                    count[0] += 1
                    ins.then_inc(n[name], 1)
                    v.wait_ge(n[name], count[0])
                return link

            link = link_to("s_c2")
            C = NE
            link(v.tensor_copy(col[:, 12:13], eiota[:, 0:1]))
            link(v.tensor_scalar(col[0:C, 5:6], col[0:C, 12:13], float(CR), None, ALU.mult))
            link(v.memset(col[C:C + 1, 12:13], 0.0))
            link(v.tensor_copy(col[0:C, 14:15], bcol[:, :]))
            link(v.memset(col[C:C + 1, 2:3], 128.0 * 16384))

            def offsets(k):
                link(v.tensor_tensor(col[0:C, 10:11], col[0:C, 5:6], col[0:C, 6:7], ALU.subtract))
                link(v.tensor_scalar(col[0:C, 10:11], col[0:C, 10:11], 1.0, None, ALU.add))
                v.tensor_scalar(diag[:, :], ident[0:C, 0:C], col[0:C, 10:11], None, ALU.mult).then_inc(n["tab_v"], 1)
                v.wait_ge(n["tab_p"], TABP * k + 1)
                link(v.tensor_copy(first1[:, :], rB[:, 0:NE]))

            offsets(0)
            v.wait_ge(n["s_half"], 3)

            def tables(k):
                nt, pv, pp = GT[k], TABV * k, TABP * k
                link(v.tensor_copy(it[:, 0:nt], iiota[:, 0:nt]))
                v.wait_ge(n["taken_r"], GSTEPS[k][1])
                v.wait_ge(n["h4_r"], GSTEPS[k][1])
                v.nop(nofuse=True).then_inc(n["tab_v"], 1)
                v.wait_ge(n["tab_p"], pp + 2)
                link(v.tensor_scalar(col[0:C, 7:8], rB[0:C, 0:1], float(CAP), None, ALU.min))
                link(v.tensor_tensor(col[0:C, 1:2], col[0:C, 7:8], col[0:C, 6:7], ALU.subtract))
                link(v.tensor_scalar(coli[:, 0:1], col[0:C, 1:2], 127.0, None, ALU.add))
                link(v.tensor_scalar(coli[:, 1:2], coli[:, 0:1], 7, None, ALU.logical_shift_right))
                v.tensor_scalar(col[0:C, 2:3], coli[:, 1:2], 128.0, None, ALU.mult).then_inc(n["tab_v"], 1)
                v.wait_ge(n["tab_v"], pv + 3)
                v.wait_ge(n["tab_p"], pp + 3)
                link(v.tensor_copy(col[:, 4:5], rB[0:C + 1, 128:129]))
                link(v.tensor_tensor(col[:, 3:4], col[:, 4:5], col[:, 2:3], ALU.add))
                link(v.tensor_tensor(col[0:C, 8:9], col[0:C, 5:6], col[0:C, 4:5], ALU.subtract))
                link(v.tensor_scalar(col[0:C, 9:10], col[0:C, 8:9], -1.0, None, ALU.mult))
                link(v.tensor_scalar(diag[:, :], ident[0:C, 0:C], col[0:C, 9:10], None, ALU.mult))
                link(v.memset(col[C:C + 1, 8:9], float(ZR)))
                link(v.tensor_scalar(itin[:, 0:nt], it[:, 0:nt], col[:, 4:5], None, ALU.is_ge))
                link(v.scalar_tensor_tensor(oh[:, 0:nt], it[:, 0:nt], col[:, 3:4], itin[:, 0:nt], ALU.is_lt, ALU.mult))
                link(v.memset(it[C:C + 1, 0:nt], 0.0))
                link(v.scalar_tensor_tensor(itin[:, 0:nt], it[:, 0:nt], col[:, 8:9], oh[:, 0:nt], ALU.add, ALU.mult))
                link(v.tensor_scalar(it[:, 0:nt], oh[:, 0:nt], col[:, 14:15], None, ALU.mult))
                v.tensor_scalar(oh[:, 0:nt], oh[:, 0:nt], col[:, 12:13], None, ALU.mult).then_inc(n["tab_v"], 1)
                for step, dst in enumerate((texp, tin, tbias)):
                    v.wait_ge(n["tab_p"], pp + 4 + step)
                    for i, w in enumerate(range(0, nt, 512)):
                        m = min(512, nt - w)
                        link(v.tensor_copy(dst[:, T0[k] + w:T0[k] + w + m], (rA, rC)[i][0:1, 0:m]))
                    if step < 2:
                        v.nop(nofuse=True).then_inc(n["tab_v"], 1)
                link(v.tensor_tensor(col[0:C, 11:12], col[0:C, 5:6], col[0:C, 1:2], ALU.add))
                v.nop(nofuse=True).then_inc(n["tab_v"], 1)
                v.wait_ge(n["tab_p"], pp + TABP)
                link(v.tensor_copy(ttail[:, NE * k:NE * (k + 1)], rB[0:1, 0:NE]))
                link(v.tensor_copy(shift[:, k, :], rB[:, 256:256 + NE]))
                v.wait_ge(n["s_half"], 3)
                v.nop(nofuse=True).then_inc(n["tab_ready"], 1)
                if k + 1 < NGRP:
                    link(v.scalar_tensor_tensor(col[0:C, 5:6], col[0:C, 2:3], 128.0, col[0:C, 5:6], ALU.add, ALU.add))
                    link(v.tensor_copy(col[0:C, 6:7], col[0:C, 7:8]))
                    offsets(k + 1)

            def gate_sum(q, slot, rnd):
                v.wait_ge(n["geu_done"], q + 1)
                after(v, n["yo_r"], q - ES + 1)
                v.tensor_tensor(gate[:, slot, :], eT_[slot % 2][:, 0:TG], xin[:, slot, :, D], ALU.add)\
                    .then_inc(n["g1_r"], 1)

            def act_e(q, slot, rnd):
                gu = eG[slot % 2][:, :].rearrange("p (j f) -> p j f", j=TG)
                v.wait_ge(n["the_r"], q + 1)
                after(v, n["hh_r"], q)
                v.scalar_tensor_tensor(ae[:, :, :], the[:, :, :], 1.0, gu[:, :, 0:F], ALU.add, ALU.mult)\
                    .then_inc(n["ae_r"], 1)
                v.wait_ge(n["ae_r"], q + 1)
                after(v, n["ht_done"], q - 1)
                v.tensor_tensor(hh[:, slot % 2, :, :], ae[:, :, :], gu[:, :, F:2 * F], ALU.mult).then_inc(n["hh_r"], 1)
                v.wait_ge(n["gx_r"], q + 1)
                v.tensor_tensor(gate[:, slot, :], gate[:, slot, :], xin[:, slot, :, D + 1], ALU.mult)\
                    .then_inc(n["gate_r"], 1)

            def copy_hT(q, slot, rnd):
                v.wait_ge(n["ht_done"], q + 1)
                after(v, n["dn_done"], q - 1)
                v.tensor_copy(hT[:, slot % 2, :, :].rearrange("p j d -> p (j d)"), eH[slot % 2][0:F, :])\
                    .then_inc(n["hT_r"], 1)

            for k, (a, b) in enumerate(GSTEPS):
                braid(v, *SPAN[k], [('b', 1, ffn_out), ('b', 0, stats_q), ('r', 1, choose), ('r', 1, halves(silu_gate)),
                                    ('b', 2, attn_out), ('r', 1, place), ('b', 0, roots), ('b', 1, norm_x),
                                    ('b', 0, quant), ('r', 1, halves(silu_up)), ('r', 1, denominator), ('r', 0, norm),
                                    ('r', 1, shared_out)], a, b)
                tables(k)

            def indices(group, g, slot, rnd):
                nj = tiles_of(g)
                v.wait_ge(dest_in[slot], 16 * (rnd + 1))
                v.tensor_tensor(drow[:, 0:nj, :], dests[:, slot, 0:nj, :],
                                shift[:, group, :].unsqueeze(1).to_broadcast([128, nj, NE]), ALU.add).then_inc(n["sh0_r"], 1)
                v.wait_ge(n["sh0_r"], g + 1)
                v.scalar_tensor_tensor(drow[:, 0:nj, :], dests[:, slot, 0:nj, :], 0.0, drow[:, 0:nj, :],
                                       ALU.is_gt, ALU.mult).then_inc(n["sh1_r"], 1)
                v.wait_ge(n["sh1_r"], g + 1)
                v.nop(nofuse=True)
                for j in range(nj):
                    last = v.max(dg[:, j, :], drow[:, j, :])
                last.then_inc(n["dg_r"], 1)
                v.wait_ge(n["dg_r"], g + 1)
                v.tensor_scalar(zg[:, 0:nj, :], dg[:, 0:nj, 0:TOPK], 0.0, float(YZ[group] + 1), ALU.is_equal, ALU.mult)\
                    .then_inc(n["zg_r"], 1)
                v.wait_ge(n["zg_r"], g + 1)
                if not isinstance(g, int) or g >= 2:
                    v.wait_ge(gath[slot], 16 * TOPK * TG * rnd)
                v.scalar_tensor_tensor(idxg[:, slot, 0:nj, :], dg[:, 0:nj, 0:TOPK], -1.0, zg[:, 0:nj, :],
                                       ALU.add, ALU.add).then_inc(n["idxg_r"], 1)

            def add_up(g, slot, rnd):
                nj = tiles_of(g)
                y = yg[:, slot, 0:nj, :, :]
                v.wait_ge(gath[slot], 16 * TOPK * (TG * rnd + nj))
                v.tensor_tensor(y[:, :, 0:3, :], y[:, :, 0:3, :], y[:, :, 3:6, :], ALU.add).then_inc(n["add1_r"], 1)
                v.wait_ge(n["add1_r"], g + 1)
                v.tensor_tensor(y[:, :, 0, :], y[:, :, 0, :], y[:, :, 1, :], ALU.add).then_inc(n["add2_r"], 1)
                v.wait_ge(h4_in[slot], 16 * (rnd + 1))
                v.tensor_tensor(y[:, :, 2, :], y[:, :, 2, :], h4s[:, slot, 0:nj, :], ALU.add).then_inc(n["add3_r"], 1)
                v.wait_ge(n["add2_r"], g + 1)
                v.wait_ge(n["add3_r"], g + 1)
                if not isinstance(g, int) or g >= 2:
                    v.wait_ge(ot_out[slot], 16 * rnd)
                v.tensor_tensor(ot[:, slot, 0:nj, :], y[:, :, 0, :], y[:, :, 2, :], ALU.add).then_inc(n["ot_r"], 1)

            def sums(group):
                return [(0, lambda g, slot, rnd: indices(group, g, slot, rnd)), (2, add_up)]

            hidden = [(1, gate_sum), (1, act_e), (2, copy_hT)]
            pipeline(v, 0, NQ, hidden, ES, end=Q1)
            weave(v, Q1, NQ + 2, NQ, hidden, ES, Q1 + EVERY, sums(0), C1)
            pipeline(v, 0, GR, sums(1), begin=C1)


def lay_out(a):
    import numpy as np
    x = np.ascontiguousarray(a["x"])
    padded = np.zeros((B, CH, S + 2 * HP, S + 2 * HP), x.dtype)
    padded[:, :, HP:HP + S, HP:HP + S] = x
    own = x.reshape(B, CH, NI, PATCH, NI, PATCH).transpose(2, 4, 1, 3, 5, 0).reshape(NI, NI, K, B)
    off = padded.reshape(B, CH, NI + 1, PATCH, NI + 1, PATCH).transpose(2, 4, 1, 3, 5, 0).reshape(NI + 1, NI + 1, K, B)
    col = np.stack([own, off[1:, :NI], off[1:, 1:], off[:NI, :NI], off[:NI, 1:]], axis=2)
    col = col.reshape(T, NCTX, K, B).transpose(2, 0, 1, 3)

    def by_position(m):
        m = np.asarray(m).reshape(NCTX, CH, NI, PATCH, NI, PATCH)
        return m.transpose(1, 3, 5, 2, 4, 0).reshape(K, T, NCTX)

    wg, wu = np.asarray(a["L1_ffn_w_gate"]), np.asarray(a["L1_ffn_w_up"])
    sg, su = np.asarray(a["L1_ffn_shared_w_gate"]), np.asarray(a["L1_ffn_shared_w_up"])
    sd = np.asarray(a["L1_ffn_shared_w_down"])
    return {
        "ximg": x.reshape(B, CH * S * S),
        "xcol": col,
        "w5": np.asarray(a["L0_tok_W"]).reshape(D, NCTX, K).transpose(2, 1, 0),
        "gam": by_position(a["L0_tok_gamma"]),
        "bet": by_position(a["L0_tok_beta"]),
        "tokb": np.asarray(a["L0_tok_b"]).reshape(1, D),
        "post": np.asarray(a["L0_attn_positions"]).T,
        "scales": np.asarray(a["L0_attn_scales"]),
        "valt": np.asarray(a["L0_attn_values"]).T,
        "wot": np.asarray(a["L0_attn_W_out"]).T,
        "bout": np.asarray(a["L0_attn_b_out"]).reshape(1, D),
        "wffn": np.asarray(a["L0_ffn_weight"]),
        "rwt": np.asarray(a["L1_ffn_router_w"]).T,
        "rbias": np.asarray(a["L1_ffn_bias"]).reshape(1, NE),
        "sgu": np.concatenate([sg.reshape(2 * F, D), su.reshape(2 * F, D)]).T,
        "sdt": sd.transpose(0, 2, 1).reshape(2 * F, D),
        "wgu": np.concatenate([wg, wu], axis=1).transpose(2, 0, 1),
        "wdt": np.asarray(a["L1_ffn_w_down"]).transpose(2, 0, 1),
    }


def kernel(**inputs):
    import numpy as _np
    import concourse.bacc as _bacc
    from concourse.bass_utils import run_bass_kernel_spmd as _run

    nc = _bacc.Bacc("TRN2", target_bir_lowering=False, num_devices=1)
    arrays, io = {}, {}
    for name, a in lay_out(inputs).items():
        arrays[f"in_{name}"] = _np.ascontiguousarray(a)
        io[name] = nc.dram_tensor(f"in_{name}", arrays[f"in_{name}"].shape, F32, kind="ExternalInput").ap()
    io["out"] = nc.dram_tensor("out_tokens", (B, T, D), F32, kind="ExternalOutput").ap()
    build(nc, io)
    r = _run(nc, [arrays], core_ids=[0])
    return r.results[0]["out_tokens"]
```
